# Optimizing a Trainium2 kernel written in Bass

```python
import numpy as np
import jax
import jax.numpy as jnp

def _softmax(x, axis=-1):
    return jax.nn.softmax(x, axis=axis)

def _gelu(x):
    return jax.nn.gelu(x, approximate=True)

def _silu(x):
    return jax.nn.silu(x)

def _sigmoid(x):
    return jax.nn.sigmoid(x)

def _layernorm(x, axis=-1, eps=1e-05):
    m = jnp.mean(x, axis=axis, keepdims=True)
    v = jnp.var(x, axis=axis, keepdims=True)
    return (x - m) / jnp.sqrt(v + eps)

def _scatter_add(tgt, idx, src, axis=0):
    return tgt.at[idx].add(src)

def _segment_sum(src, seg, n):
    return jax.ops.segment_sum(src, seg, n)
kernel_name = 'mk_macaron_d1_jaxref_r8_01b902'

def setup_inputs(seed: int=0):
    np.random.seed(seed)
    _w = jnp.asarray

    def _L0_attn_setup():
        import jax, jax.numpy as jnp
        import numpy as np
        EPS = 1e-12

        def _ln(x, g, b):
            m = x.mean(-1, keepdims=True)
            v = x.var(-1, keepdims=True)
            return (x - m) / jnp.sqrt(v + EPS) * g + b

        def _shift(x):
            return jnp.pad(x[:, :-1], ((0, 0), (1, 0), (0, 0)))
        key = jax.random.key(seed)
        ks = jax.random.split(key, 20)
        B, T, H = (4, 256, 256)
        I = 4 * H
        f32 = jnp.float32

        def gamma(k):
            return 1.0 + 0.1 * jax.random.normal(k, (H,), f32)

        def beta(k):
            return 0.1 * jax.random.normal(k, (H,), f32)

        def w(k, i, o):
            return 0.02 * jax.random.normal(k, (i, o), f32)
        return {'x': jax.random.normal(ks[0], (B, T, H), f32), 'ln1_g': gamma(ks[1]), 'ln1_b': beta(ks[2]), 'ln2_g': gamma(ks[3]), 'ln2_b': beta(ks[4]), 'tm_g': gamma(ks[5]), 'tm_b': beta(ks[6]), 'time_decay': -(0.2 + jax.random.uniform(ks[7], (H,), f32)), 'time_first': jax.random.uniform(ks[8], (H,), f32), 'Wk': w(ks[9], H, H), 'Wv': w(ks[10], H, H), 'Wr': w(ks[11], H, H), 'Wo': w(ks[12], H, H), 'bo': jnp.zeros((H,), f32), 'cm_g': gamma(ks[13]), 'cm_b': beta(ks[14]), 'Wck': w(ks[15], H, I), 'Wcv': w(ks[16], I, H), 'Wcr': w(ks[17], H, H)}
    _L0_attn_in = _L0_attn_setup()

    def _L0_ffn_setup():
        import jax, jax.numpy as jnp
        import numpy as np
        B, S, D = (2, 256, 256)
        H, KV, HD = (16, 4, 128)
        E, F, TOPK = (8, 512, 2)
        THETA = 1000000.0
        EPS = 1e-05

        def rmsnorm(x, w):
            var = jnp.mean(jnp.square(x), axis=-1, keepdims=True)
            return x * jax.lax.rsqrt(var + EPS) * w

        def rope_cos_sin(seq_len):
            inv_freq = 1.0 / THETA ** (jnp.arange(0, HD, 2, dtype=jnp.float32) / HD)
            ang = jnp.arange(seq_len, dtype=jnp.float32)[:, None] * inv_freq[None, :]
            return (jnp.cos(ang)[None, :, None, :], jnp.sin(ang)[None, :, None, :])

        def apply_rope(x, cos, sin):
            x1, x2 = jnp.split(x, 2, axis=-1)
            return jnp.concatenate([x1 * cos - x2 * sin, x2 * cos + x1 * sin], axis=-1)

        def attention(x, wq, wk, wv, wo):
            b, s, _ = x.shape
            q = (x @ wq).reshape(b, s, H, HD)
            k = (x @ wk).reshape(b, s, KV, HD)
            v = (x @ wv).reshape(b, s, KV, HD)
            cos, sin = rope_cos_sin(s)
            q = apply_rope(q, cos, sin)
            k = apply_rope(k, cos, sin)
            rep = H // KV
            k = jnp.repeat(k, rep, axis=2)
            v = jnp.repeat(v, rep, axis=2)
            scores = jnp.einsum('bqhd,bkhd->bhqk', q, k) / np.sqrt(HD)
            causal = jnp.tril(jnp.ones((s, s), dtype=bool))
            scores = jnp.where(causal[None, None], scores, jnp.finfo(scores.dtype).min)
            probs = jax.nn.softmax(scores, axis=-1)
            out = jnp.einsum('bhqk,bkhd->bqhd', probs, v).reshape(b, s, H * HD)
            return out @ wo

        def moe(x, gate_w, w1, w3, w2):
            b, s, d = x.shape
            xt = x.reshape(b * s, d)
            logits = xt @ gate_w
            topv, topi = jax.lax.top_k(logits, TOPK)
            probs = jax.nn.softmax(topv, axis=-1)
            w = jnp.zeros_like(logits)
            for kk in range(TOPK):
                w = w + jax.nn.one_hot(topi[:, kk], E, dtype=logits.dtype) * probs[:, kk:kk + 1]
            out = jnp.zeros_like(xt)
            for e in range(E):
                h = jax.nn.silu(xt @ w1[e]) * (xt @ w3[e])
                out = out + w[:, e:e + 1] * (h @ w2[e])
            return out.reshape(b, s, d)
        key = jax.random.key(seed)
        ks = jax.random.split(key, 10)
        init = lambda k, shape: jax.random.normal(k, shape, jnp.float32) * 0.02
        return {'hidden_states': jax.random.normal(ks[0], (B, S, D), jnp.float32), 'norm1_w': jnp.ones((D,), jnp.float32), 'norm2_w': jnp.ones((D,), jnp.float32), 'wq': init(ks[1], (D, H * HD)), 'wk': init(ks[2], (D, KV * HD)), 'wv': init(ks[3], (D, KV * HD)), 'wo': init(ks[4], (H * HD, D)), 'gate_w': init(ks[5], (D, E)), 'w1': init(ks[6], (E, D, F)), 'w3': init(ks[7], (E, D, F)), 'w2': init(ks[8], (E, F, D))}
    _L0_ffn_in = _L0_ffn_setup()
    _d = {'L0_attn_x': _L0_attn_in['x'], 'L0_attn_ln1_g': _L0_attn_in['ln1_g'], 'L0_attn_ln1_b': _L0_attn_in['ln1_b'], 'L0_attn_ln2_g': _L0_attn_in['ln2_g'], 'L0_attn_ln2_b': _L0_attn_in['ln2_b'], 'L0_attn_tm_g': _L0_attn_in['tm_g'], 'L0_attn_tm_b': _L0_attn_in['tm_b'], 'L0_attn_time_decay': _L0_attn_in['time_decay'], 'L0_attn_time_first': _L0_attn_in['time_first'], 'L0_attn_Wk': _L0_attn_in['Wk'], 'L0_attn_Wv': _L0_attn_in['Wv'], 'L0_attn_Wr': _L0_attn_in['Wr'], 'L0_attn_Wo': _L0_attn_in['Wo'], 'L0_attn_bo': _L0_attn_in['bo'], 'L0_attn_cm_g': _L0_attn_in['cm_g'], 'L0_attn_cm_b': _L0_attn_in['cm_b'], 'L0_attn_Wck': _L0_attn_in['Wck'], 'L0_attn_Wcv': _L0_attn_in['Wcv'], 'L0_attn_Wcr': _L0_attn_in['Wcr'], 'L0_ffn_norm1_w': _L0_ffn_in['norm1_w'], 'L0_ffn_norm2_w': _L0_ffn_in['norm2_w'], 'L0_ffn_wq': _L0_ffn_in['wq'], 'L0_ffn_wk': _L0_ffn_in['wk'], 'L0_ffn_wv': _L0_ffn_in['wv'], 'L0_ffn_wo': _L0_ffn_in['wo'], 'L0_ffn_gate_w': _L0_ffn_in['gate_w'], 'L0_ffn_w1': _L0_ffn_in['w1'], 'L0_ffn_w3': _L0_ffn_in['w3'], 'L0_ffn_w2': _L0_ffn_in['w2']}
    _x0 = _d['L0_attn_x']
    _d['L0_attn_x'] = jax.random.normal(jax.random.fold_in(jax.random.key(seed), 1), (1, 1024, 256), dtype=_x0.dtype)
    del _x0
    return _d

def reference(L0_attn_x, L0_attn_ln1_g, L0_attn_ln1_b, L0_attn_ln2_g, L0_attn_ln2_b, L0_attn_tm_g, L0_attn_tm_b, L0_attn_time_decay, L0_attn_time_first, L0_attn_Wk, L0_attn_Wv, L0_attn_Wr, L0_attn_Wo, L0_attn_bo, L0_attn_cm_g, L0_attn_cm_b, L0_attn_Wck, L0_attn_Wcv, L0_attn_Wcr, L0_ffn_norm1_w, L0_ffn_norm2_w, L0_ffn_wq, L0_ffn_wk, L0_ffn_wv, L0_ffn_wo, L0_ffn_gate_w, L0_ffn_w1, L0_ffn_w3, L0_ffn_w2):

    def _L0_attn_ref(x, ln1_g, ln1_b, ln2_g, ln2_b, tm_g, tm_b, time_decay, time_first, Wk, Wv, Wr, Wo, bo, cm_g, cm_b, Wck, Wcv, Wcr):
        import jax, jax.numpy as jnp
        import numpy as np
        EPS = 1e-12

        def _ln(x, g, b):
            m = x.mean(-1, keepdims=True)
            v = x.var(-1, keepdims=True)
            return (x - m) / jnp.sqrt(v + EPS) * g + b

        def _shift(x):
            return jnp.pad(x[:, :-1], ((0, 0), (1, 0), (0, 0)))
        B, T, H = x.shape
        x1 = _ln(x, ln1_g, ln1_b)
        xln = _ln(x1, tm_g, tm_b)
        xs = _shift(xln)
        mix = xln * time_first + xs * (1.0 - time_first)
        v = xln @ Wv
        r = jax.nn.sigmoid(mix @ Wr)
        dec = jnp.exp(time_decay[None, :] * (T - 1 - jnp.arange(T))[:, None])
        vmix = jnp.einsum('bth,th->bh', v, dec)[:, None, :]
        time_out = r * (vmix @ Wo + bo)
        x2 = x + time_out
        xc = _ln(_ln(x2, ln2_g, ln2_b), cm_g, cm_b)
        xcs = _shift(xc)
        kc = jnp.square(jax.nn.relu(xcs @ Wck))
        vc = kc @ Wcv
        rc = jax.nn.sigmoid(xc @ Wcr)
        return x2 + rc * vc

    def _L0_ffn_ref(hidden_states, norm1_w, norm2_w, wq, wk, wv, wo, gate_w, w1, w3, w2):
        import jax, jax.numpy as jnp
        import numpy as np
        B, S, D = (2, 256, 256)
        H, KV, HD = (16, 4, 128)
        E, F, TOPK = (8, 512, 2)
        THETA = 1000000.0
        EPS = 1e-05

        def rmsnorm(x, w):
            var = jnp.mean(jnp.square(x), axis=-1, keepdims=True)
            return x * jax.lax.rsqrt(var + EPS) * w

        def rope_cos_sin(seq_len):
            inv_freq = 1.0 / THETA ** (jnp.arange(0, HD, 2, dtype=jnp.float32) / HD)
            ang = jnp.arange(seq_len, dtype=jnp.float32)[:, None] * inv_freq[None, :]
            return (jnp.cos(ang)[None, :, None, :], jnp.sin(ang)[None, :, None, :])

        def apply_rope(x, cos, sin):
            x1, x2 = jnp.split(x, 2, axis=-1)
            return jnp.concatenate([x1 * cos - x2 * sin, x2 * cos + x1 * sin], axis=-1)

        def attention(x, wq, wk, wv, wo):
            b, s, _ = x.shape
            q = (x @ wq).reshape(b, s, H, HD)
            k = (x @ wk).reshape(b, s, KV, HD)
            v = (x @ wv).reshape(b, s, KV, HD)
            cos, sin = rope_cos_sin(s)
            q = apply_rope(q, cos, sin)
            k = apply_rope(k, cos, sin)
            rep = H // KV
            k = jnp.repeat(k, rep, axis=2)
            v = jnp.repeat(v, rep, axis=2)
            scores = jnp.einsum('bqhd,bkhd->bhqk', q, k) / np.sqrt(HD)
            causal = jnp.tril(jnp.ones((s, s), dtype=bool))
            scores = jnp.where(causal[None, None], scores, jnp.finfo(scores.dtype).min)
            probs = jax.nn.softmax(scores, axis=-1)
            out = jnp.einsum('bhqk,bkhd->bqhd', probs, v).reshape(b, s, H * HD)
            return out @ wo

        def moe(x, gate_w, w1, w3, w2):
            b, s, d = x.shape
            xt = x.reshape(b * s, d)
            logits = xt @ gate_w
            topv, topi = jax.lax.top_k(logits, TOPK)
            probs = jax.nn.softmax(topv, axis=-1)
            w = jnp.zeros_like(logits)
            for kk in range(TOPK):
                w = w + jax.nn.one_hot(topi[:, kk], E, dtype=logits.dtype) * probs[:, kk:kk + 1]
            out = jnp.zeros_like(xt)
            for e in range(E):
                h = jax.nn.silu(xt @ w1[e]) * (xt @ w3[e])
                out = out + w[:, e:e + 1] * (h @ w2[e])
            return out.reshape(b, s, d)
        attn_out = attention(rmsnorm(hidden_states, norm1_w), wq, wk, wv, wo)
        h = hidden_states + attn_out
        out = h + moe(rmsnorm(h, norm2_w), gate_w, w1, w3, w2)
        return out
    x = L0_attn_x
    x = x + 0.5 * _L0_ffn_ref(_layernorm(x, axis=-1), L0_ffn_norm1_w, L0_ffn_norm2_w, L0_ffn_wq, L0_ffn_wk, L0_ffn_wv, L0_ffn_wo, L0_ffn_gate_w, L0_ffn_w1, L0_ffn_w3, L0_ffn_w2)
    x = x + _L0_attn_ref(_layernorm(x, axis=-1), L0_attn_ln1_g, L0_attn_ln1_b, L0_attn_ln2_g, L0_attn_ln2_b, L0_attn_tm_g, L0_attn_tm_b, L0_attn_time_decay, L0_attn_time_first, L0_attn_Wk, L0_attn_Wv, L0_attn_Wr, L0_attn_Wo, L0_attn_bo, L0_attn_cm_g, L0_attn_cm_b, L0_attn_Wck, L0_attn_Wcv, L0_attn_Wcr)
    x = x + 0.5 * _L0_ffn_ref(_layernorm(x, axis=-1), L0_ffn_norm1_w, L0_ffn_norm2_w, L0_ffn_wq, L0_ffn_wk, L0_ffn_wv, L0_ffn_wo, L0_ffn_gate_w, L0_ffn_w1, L0_ffn_w3, L0_ffn_w2)
    return x

_drawn_inputs = setup_inputs


def setup_inputs(seed=0):
    import zlib

    import numpy as np

    out = dict(_drawn_inputs(seed))
    spreads = {'L0_attn_bo': (0.0, 0.408), 'L0_ffn_norm1_w': (1.0, 0.6), 'L0_ffn_norm2_w': (1.0, 0.6)}
    factors = {'L0_attn_ln1_g': 8.0,
     'L0_attn_ln1_b': 8.0,
     'L0_attn_ln2_g': 8.0,
     'L0_attn_ln2_b': 8.0,
     'L0_attn_tm_g': 8.0,
     'L0_attn_tm_b': 8.0,
     'L0_attn_time_decay': 7.235,
     'L0_attn_time_first': 8.0,
     'L0_attn_Wr': 8.0,
     'L0_attn_cm_g': 8.0,
     'L0_attn_cm_b': 8.0,
     'L0_attn_Wck': 3.724,
     'L0_attn_Wcv': 3.359,
     'L0_attn_Wcr': 8.0,
     'L0_ffn_wq': 8.0,
     'L0_ffn_wk': 8.0,
     'L0_ffn_wv': 4.41,
     'L0_ffn_wo': 4.472,
     'L0_ffn_gate_w': 6.514,
     'L0_ffn_w1': 5.836,
     'L0_ffn_w3': 5.73,
     'L0_ffn_w2': 5.739}
    for name, (base, spread) in spreads.items():
        noise = np.random.default_rng([zlib.crc32(name.encode()), seed]).standard_normal(out[name].shape)
        drawn = base * np.exp(spread * noise) if base else spread * noise
        out[name] = jnp.asarray(drawn.astype(out[name].dtype))
    for name, factor in factors.items():
        out[name] = (out[name] * factor).astype(out[name].dtype)
    return out
```

```python
from contextlib import ExitStack

import numpy as np

import concourse.bass as bass
from concourse import mybir

F32 = mybir.dt.float32
BF16 = mybir.dt.bfloat16
I32 = mybir.dt.int32
U32 = mybir.dt.uint32
ALU = mybir.AluOpType
ACT = mybir.ActivationFunctionType
AX = mybir.AxisListType

P = 128
T, D = 1024, 256
NT, DC = T // P, D // P
HEADS, KVH, HD = 16, 4, 128
REP = HEADS // KVH
E, F = 8, 512
FC = F // P
TOPK = 2
NS = (TOPK * T + E * (P - 1)) // P
RI = 1024
IC = RI // P
HALF = 512
SCALE = float(1.0 / np.sqrt(HD))
EPS, EPS_RWKV = 1e-5, 1e-12
BIG = 1e30
THETA = 1000000.0

TURNS = NT * (NT + 1) // 2
SOFT = NT * REP


def turns_before(i):
    return i * (i + 1) // 2


def attention_order():
    order = [("scores", 0, h) for h in range(REP)]
    for i in range(NT):
        inner = []
        for j in range(i + 1):
            inner.append(("turn", i, j))
            if j:
                inner.append(("values", i, j - 1))
        inner.append(("values", i, i))
        extra = [("scores", i + 1, h) for h in range(REP)] if i + 1 < NT else []
        if i:
            extra.insert(1, ("out", i - 1, 0))
        n = len(inner)
        done = 0
        for k, step in enumerate(inner):
            while done < len(extra) and done * n < (k + 1) * len(extra):
                order.append(extra[done])
                done += 1
            order.append(step)
        order += extra[done:]
    order.append(("out", NT - 1, 0))
    return order


C_KEY, C_THR, C_BEFORE, C_SLOT = 0, 8, 72, 136
C_ALL = C_SLOT + NS * E


def constants():
    inv = (1.0 / THETA ** (np.arange(0, HD, 2, dtype=np.float32) / np.float32(HD))).astype(np.float32)
    ang = np.arange(T, dtype=np.float32)[None, :] * inv[:, None]
    cos, sin = np.cos(ang).astype(np.float32), np.sin(ang).astype(np.float32)
    rope = np.concatenate([np.concatenate([cos, cos]), np.concatenate([-sin, sin])], axis=1)
    ident = np.eye(P, dtype=np.float32)
    r = np.arange(P)
    mask = np.where(r[None, :] <= r[:, None], 0.0, -BIG).astype(np.float32)
    before = (r[:, None] < r[None, :]).astype(np.float32)
    small = np.zeros((P, C_ALL), np.float32)
    e = np.arange(E)
    small[:, C_KEY:C_KEY + E] = E - e
    small[:, C_THR:C_THR + E * E] = np.tile(P * e, E)
    small[:, C_BEFORE:C_BEFORE + E * E] = (e[None, :] < e[:, None]).ravel()
    small[:, C_SLOT:] = np.repeat(np.arange(NS), E)
    left = np.tile((T - 1 - np.arange(T, dtype=np.float32))[None, :], (P, 1))
    return {
        "c_rope": np.ascontiguousarray(rope, np.float32),
        "c_square": np.ascontiguousarray(np.concatenate([ident, mask, before], axis=1)),
        "c_small": small,
        "c_left": np.ascontiguousarray(left, np.float32),
    }


def macaron(nc, a, out, scratch):
    ORDER = attention_order()
    xs_dram, ys_dram, xsave_dram = scratch

    with ExitStack() as ctx:
        def sb(name, shape, dt=F32, c=ctx):
            return c.enter_context(nc.sbuf_tensor(name, shape, dt))

        def sem(name):
            return ctx.enter_context(nc.semaphore(name))

        ps = ctx.enter_context(nc.psum_tensor("ps", [P, 8, 512], F32))

        w1 = sb("w1", [P, E, DC, F])
        w3 = sb("w3", [P, E, DC, F])
        w2 = sb("w2", [P, E, FC, D])
        h = sb("h", [P, NT, D])
        xT = sb("xT", [P, DC, 1 + T])
        rope = sb("rope", [P, 2, T])
        probs = sb("probs", [P, 2, REP, T])
        flat = probs[:].rearrange("p a b t -> p (a b t)")
        x = flat[:, 0:NT * D].rearrange("p (t d) -> p t d", t=NT)
        y = flat[:, NT * D:2 * NT * D].rearrange("p (t d) -> p t d", t=NT)
        back = flat[:, 2 * NT * D:].rearrange("p (k t d) -> p k t d", k=2, t=NT)
        kT = flat[:, 2 * NT * D:].rearrange("p (i t) -> p i t", i=IC)
        zeros = flat[:, 2 * NT * D:].rearrange("p (n d) -> p n d", d=D)
        square = sb("square", [P, 3, P])
        ident, upper = square[:, 0, :], square[:, 2, :]
        square16 = sb("square16", [P, 2, P], BF16)
        ones = sb("ones", [P, P])
        small = sb("small", [P, C_ALL])
        cols = sb("cols", [P, 2, 8])
        gate = sb("gate", [P, DC, E])
        stats = sb("stats", [P, NT, 6])
        meanvar = sb("meanvar", [P, NT, 2])
        mean = sb("mean", [P, NT])
        var = sb("var", [P, 2, NT])
        std = sb("std", [P, 2, NT])
        rstd = sb("rstd", [P, 2, NT])
        negmax = sb("negmax", [P, 8])
        rowsum = sb("rowsum", [P, 3 * REP])
        rowinv = sb("rowinv", [P, 3 * REP])

        with ExitStack() as phase:
            w_qkv = sb("w_qkv", [P, DC, REP * HD + 2 * HD], c=phase)
            w_o = sb("w_o", [P, REP, D], c=phase)
            keysT = sb("keysT", [P, T], c=phase)
            values = sb("values", [P, NT, HD], c=phase)
            queriesT = sb("queriesT", [P, REP, T], c=phase)
            crossed = sb("crossed", [P, 2, HALF], c=phase)
            probsT = sb("probsT", [P, 3, REP * P], c=phase)
            attnT = sb("attnT", [P, 2, REP * P], c=phase)

        with ExitStack() as phase:
            xs = sb("xs", [P, 2, D], c=phase)
            xsT = sb("xsT", [P, 2, DC, P], c=phase)
            gated = sb("gated", [P, 2, F], c=phase)
            hid = sb("hid", [P, 2, F], c=phase)
            hidT = sb("hidT", [P, 2, FC, P], c=phase)
            ys = sb("ys", [P, 2, D], c=phase)
            logits = sb("logits", [P, NT, E], c=phase)
            work = sb("work", [P, NT, E], c=phase)
            pick = sb("pick", [P, 2, NT, E], c=phase)
            both = sb("both", [P, NT, E], c=phase)
            top = sb("top", [P, 2, NT], c=phase)
            key = sb("key", [P, NT], c=phase)
            wts = sb("wts", [P, 2, NT], c=phase)
            count = sb("count", [P, E], c=phase)
            cube = sb("cube", [P, NS, E], c=phase)
            tiles = sb("tiles", [P, E], c=phase)
            first = sb("first", [P, E], c=phase)
            slotf = sb("slotf", [P, 2, NT], c=phase)
            slot = sb("slot", [P, 2, NT], U32, c=phase)
            ownerf = sb("ownerf", [P, NS], c=phase)
            owner = sb("owner", [P, NS], I32, c=phase)
            Wv = sb("Wv", [P, DC, D], c=phase)
            Wr = sb("Wr", [P, DC, D], c=phase)
            Wo = sb("Wo", [P, DC, D], c=phase)
            Wck = sb("Wck", [P, DC, RI], c=phase)
            Wcv = sb("Wcv", [P, IC, D], c=phase)
            Wcr = sb("Wcr", [P, DC, D], c=phase)
            rows = sb("rows", [P, 5, D], c=phase)
        with ExitStack() as phase:
            mixT = sb("mixT", [P, DC, T], c=phase)
            decay = sb("decay", [P, HALF], c=phase)
            vsum = sb("vsum", [P, 4], c=phase)
            vmix = sb("vmix", [P, 2], c=phase)
            vwide = sb("vwide", [P, DC, P], c=phase)
            u = sb("u", [P, D], c=phase)
            rg = sb("rg", [P, 2, HALF], c=phase)
        left = y
        leftv = flat[:, NT * D:NT * D + T]

        N1, N2, TMG, TMB, CMG, CMB, TF, TD = range(8)

        S = {}
        for name in (
            "consts_in experts_in x_in cols_in zeros_set zeros_out qkv_in wo_in rwkv_in left_in saved x_back stored "
            "owner_ready dve_step consts_ready var_ready std_ready y_ready turned xT_ready "
            "rope_ps rope_read rope_part rope_done v_ps v_ready scores_ready max_ready exp_done "
            "turn_done probsT_ready pv_done attnT_ready out_ps out_added "
            "logits_ps routing_ps routed rowinv_ready pick_ready scattered gap_ready gap_exp "
            "xs_turned xsT_ready up_done silu_done hid_ready hid_turned hidT_ready down_done ys_ready "
            "mix_ready v_done decay_done decay_used vw_ready u_done u_ready r_done r_ready r_used ck_done ck_relu ck_sq "
            "cv_done cv_sig cv_used x_final"
        ).split():
            S[name] = sem(name)
        xs_in = [sem("xs_in_even"), sem("xs_in_odd")]
        ys_out = [sem("ys_out_even"), sem("ys_out_odd")]
        gathered = [sem(f"gathered_{t}") for t in range(NT)]
        PAR = [(NS + 1) // 2, NS // 2]

        x_dram = a["L0_attn_x"].rearrange("a (t p) d -> p (a t) d", p=P)
        out_dram = out.rearrange("a (t p) d -> p (a t) d", p=P)
        xsave = xsave_dram.rearrange("(t p) d -> p t d", p=P)
        xs_tiles = xs_dram.rearrange("(n p) d -> p n d", p=P)
        ys_tiles = ys_dram.rearrange("(n p) d -> p n d", p=P)
        wq_d = a["L0_ffn_wq"].rearrange("(c p) (g n) -> p c g n", p=P, g=KVH)
        wk_d = a["L0_ffn_wk"].rearrange("(c p) (g n) -> p c g n", p=P, g=KVH)
        wv_d = a["L0_ffn_wv"].rearrange("(c p) (g n) -> p c g n", p=P, g=KVH)
        wo_d = a["L0_ffn_wo"].rearrange("(g r p) d -> p g r d", p=P, g=KVH)

        def chunks(name):
            return a[name].rearrange("(c p) n -> p c n", p=P)

        def column(name):
            return a[name].rearrange("(c p) -> p c", p=P)

        def softmax_n(gg, i, hd):
            return gg * SOFT + i * REP + hd

        block = ctx.enter_context(nc.Block())

        @block.sync
        def _(sp):
            sp.dma_start(x, x_dram).then_inc(S["x_in"], 16)
            sp.dma_start(square[:], a["c_square"].rearrange("p (k n) -> p k n", k=3)).then_inc(S["consts_in"], 16)
            for n, name in enumerate(("L0_ffn_norm1_w", "L0_ffn_norm2_w", "L0_attn_tm_g", "L0_attn_tm_b",
                                      "L0_attn_cm_g", "L0_attn_cm_b", "L0_attn_time_first", "L0_attn_time_decay")):
                with nc.allow_non_contiguous_dma(reason="256 single features"):
                    sp.dma_start(cols[:, :, n], column(name)).then_inc(S["cols_in"], 16)
            sp.dma_start(rope[:], a["c_rope"].rearrange("p (k t) -> p k t", k=2)).then_inc(S["consts_in"], 16)
            sp.dma_start(small[:], a["c_small"]).then_inc(S["consts_in"], 16)
            sp.dma_start(gate[:], chunks("L0_ffn_gate_w")).then_inc(S["consts_in"], 16)

            def attention_weights(f):
                with sp.Fori(0, KVH) as g:
                    gg = f * KVH + g
                    sp.wait_ge(S["rope_ps"], 1 + 10 * gg)
                    sp.wait_ge(S["v_ps"], 1 + 2 * gg)
                    sp.dma_start(w_qkv[:, :, 0:REP * HD], wq_d[:, :, bass.ds(g, 1), :]).then_inc(S["qkv_in"], 16)
                    sp.dma_start(w_qkv[:, :, REP * HD:REP * HD + HD], wk_d[:, :, bass.ds(g, 1), :]).then_inc(S["qkv_in"], 16)
                    sp.dma_start(w_qkv[:, :, REP * HD + HD:], wv_d[:, :, bass.ds(g, 1), :]).then_inc(S["qkv_in"], 16)
                    sp.wait_ge(S["out_ps"], 1 + 2 * NT * gg)
                    sp.dma_start(w_o[:], wo_d[:, bass.ds(g, 1), :, :]).then_inc(S["wo_in"], 16)

            def load_xs(f, k, par, n):
                sp.dma_start(xs[:, par, :], xs_tiles[:, bass.ds(2 * k + par, 1), :]).then_inc(xs_in[par], 16)

            def store_ys(f, k, par):
                sp.wait_ge(S["ys_ready"], NS * f + 2 * k + par + 1)
                sp.dma_start(ys_tiles[:, bass.ds(2 * k + par, 1), :], ys[:, par, :]).then_inc(ys_out[par], 16)

            def moe(f):
                sp.wait_ge(S["out_ps"], 1 + 2 * NT * KVH * (f + 1))
                sp.dma_start(x, x_dram if f == 0 else xsave).then_inc(S["x_back"], 16)
                if f == 0:
                    for tile, src in ((Wv, "L0_attn_Wv"), (Wr, "L0_attn_Wr"), (Wo, "L0_attn_Wo"),
                                      (Wck, "L0_attn_Wck"), (Wcv, "L0_attn_Wcv"), (Wcr, "L0_attn_Wcr")):
                        sp.dma_start(tile[:], chunks(src)).then_inc(S["rwkv_in"], 16)
                    for n, name in enumerate(("ln1_g", "ln1_b", "ln2_g", "ln2_b", "bo")):
                        sp.dma_start(rows[:, n, :], a["L0_attn_" + name].rearrange("(a d) -> a d", a=1)
                                     .broadcast_to([P, D])).then_inc(S["rwkv_in"], 16)
                sp.wait_ge(S["scattered"], 16 * 16 * (f + 1))
                for par in range(2):
                    load_xs(f, 0, par, 0)
                with sp.Fori(0, (NS - 3) // 2) as k:
                    for par in range(2):
                        sp.wait_ge(S["xs_turned"], NS * f + 2 * k + par + 1)
                        load_xs(f, k + 1, par, 0)
                        store_ys(f, k, par)
                k = (NS - 3) // 2
                sp.wait_ge(S["xs_turned"], NS * f + 2 * k + 1)
                load_xs(f, k + 1, 0, 0)
                store_ys(f, k, 0)
                store_ys(f, k, 1)
                store_ys(f, k + 1, 0)

            attention_weights(0)
            moe(0)
            sp.wait_ge(S["turned"], 3 * NT)
            sp.dma_start(leftv, a["c_left"]).then_inc(S["left_in"], 16)
            sp.wait_ge(S["x_final"], 1)
            sp.dma_start(xsave, x).then_inc(S["saved"], 16)
            attention_weights(1)
            sp.wait_ge(S["saved"], 16)
            moe(1)
            sp.wait_ge(S["x_final"], 2)
            sp.dma_start(out_dram, x).then_inc(S["stored"], 16)
            sp.wait_ge(S["stored"], 16)
            for par in range(2):
                sp.wait_ge(ys_out[par], 16 * 2 * PAR[par])

        @block.gpsimd
        def _(pool):
            pool.memset(back, 0.0).then_inc(S["zeros_set"], 1)
            pool.wait_ge(S["zeros_set"], 1)
            pool.dma_start(xs_tiles[:, 0:16, :], zeros).then_inc(S["zeros_out"], 16)
            pool.dma_start(xs_tiles[:, 16:NS, :], zeros[:, 0:NS - 16, :]).then_inc(S["zeros_out"], 16)
            for e in range(E):
                pool.dma_start(w1[:, e], a["L0_ffn_w1"][e].rearrange("(c p) n -> p c n", p=P)).then_inc(S["experts_in"], 16)
                pool.dma_start(w3[:, e], a["L0_ffn_w3"][e].rearrange("(c p) n -> p c n", p=P)).then_inc(S["experts_in"], 16)
                pool.dma_start(w2[:, e], a["L0_ffn_w2"][e].rearrange("(c p) n -> p c n", p=P)).then_inc(S["experts_in"], 16)

            def attention(f):
                with pool.Fori(0, KVH) as g:
                    gg = f * KVH + g
                    for b in range(10):
                        dst = keysT[:, b * HALF:(b + 1) * HALF] if b < 2 else \
                            queriesT[:, (b - 2) // 2, (b % 2) * HALF:(b % 2 + 1) * HALF]
                        pool.wait_ge(S["rope_part"], 10 * gg + b + 1)
                        pool.tensor_tensor(dst, dst, crossed[:, b % 2, :], ALU.add).then_inc(S["rope_done"], 1)

            def moe(f):
                pool.wait_ge(S["routed"], f + 1)
                if f == 0:
                    pool.wait_ge(S["zeros_out"], 32)
                for t in range(NT):
                    for k in range(TOPK):
                        pool.indirect_dma_start(
                            out=xs_dram, out_offset=bass.IndirectOffsetOnAxis(ap=slot[:, k, t:t + 1], axis=0),
                            in_=y[:, t, :], in_offset=None).then_inc(S["scattered"], 16)
                for par in range(2):
                    pool.wait_ge(ys_out[par], 16 * (f + 1) * PAR[par])
                for t in range(NT):
                    for k in range(TOPK):
                        pool.indirect_dma_start(
                            out=back[:, k, t, :], out_offset=None, in_=ys_dram,
                            in_offset=bass.IndirectOffsetOnAxis(ap=slot[:, k, t:t + 1], axis=0)
                        ).then_inc(gathered[t], 16)

            attention(0)
            moe(0)
            attention(1)
            moe(1)

        @block.scalar
        def _(act):
            n_std = [0]

            def sqrt(k=1):
                n_std[0] += 1
                act.wait_ge(S["var_ready"], n_std[0])
                act.activation(std[:, 0:k, :], var[:, 0:k, :], ACT.Sqrt).then_inc(S["std_ready"], 1)

            act.sem_inc(S["exp_done"], 1)
            act.sem_inc(S["probsT_ready"], 1)
            act.sem_inc(S["attnT_ready"], 1)

            def attention(f):
                if f == 0:
                    act.wait_ge(S["zeros_out"], 32)
                with act.Fori(0, KVH) as g:
                    gg = f * KVH + g
                    for b in range(2):
                        act.wait_ge(S["v_ps"], 1 + 2 * gg + b + 1)
                        act.activation(values[:, 4 * b:4 * b + 4, :],
                                       ps[:, 2 + b, :].rearrange("p (t n) -> p t n", t=4), ACT.Copy).then_inc(S["v_ready"], 1)
                    for what, i, k in ORDER:
                        if what == "scores":
                            n = softmax_n(gg, i, k)
                            s = 2 * (k % 2)
                            w = (i + 1) * P
                            m, r = (i % 2) * REP + k, (i % 3) * REP + k
                            act.wait_ge(S["max_ready"], n + 1)
                            act.activation(probs[:, i % 2, k, 0:w],
                                           ps[:, s:s + 2, :].rearrange("p b n -> p (b n)")[:, 0:w], ACT.Exp,
                                           bias=negmax[:, m:m + 1], accum_out=rowsum[:, r:r + 1]).then_inc(S["exp_done"], 1)
                        if what == "turn":
                            m = turns_before(i) + k
                            act.wait_ge(S["turn_done"], TURNS * gg + m + 1)
                            act.activation(probsT[:, m % 3, :], ps[:, 4 + m % 2, :], ACT.Copy).then_inc(S["probsT_ready"], 1)
                        if what == "values" and k == i:
                            act.wait_ge(S["pv_done"], NT * gg + i + 1)
                            act.activation(attnT[:, i % 2, :], ps[:, 6, :], ACT.Copy).then_inc(S["attnT_ready"], 1)

            def expert_tile(f, tau, par, turn, silu):
                n = NS * f + tau
                if turn:
                    act.wait_ge(S["hid_turned"], n)
                    act.activation(hidT[:, 1 - par].rearrange("p c n -> p (c n)"), ps[:, 6, :], ACT.Copy
                                   ).then_inc(S["hidT_ready"], 1)
                if silu:
                    act.wait_ge(S["up_done"], n + 1)
                    act.activation(gated[:, par, :], ps[:, 2 * par, :], ACT.Silu).then_inc(S["silu_done"], 1)

            def moe(f):
                sqrt()
                act.wait_ge(S["gap_ready"], f + 1)
                act.activation(key[:], key[:], ACT.Exp).then_inc(S["gap_exp"], 1)
                expert_tile(f, 0, 0, False, True)
                with act.Fori(0, (NS - 3) // 2) as k:
                    expert_tile(f, 2 * k + 1, 1, True, True)
                    expert_tile(f, 2 * k + 2, 0, True, True)
                expert_tile(f, NS - 2, 1, True, True)
                expert_tile(f, NS - 1, 0, True, True)
                expert_tile(f, NS, 1, True, False)

            def rwkv():
                sqrt(2)
                sqrt()
                act.wait_ge(S["left_in"], 16)
                for n in range(4):
                    hc, th = divmod(n, 2)
                    if n:
                        act.wait_ge(S["decay_used"], n)
                    act.activation(decay[:], leftv[:, th * HALF:(th + 1) * HALF], ACT.Exp,
                                   scale=cols[:, hc, TD:TD + 1]).then_inc(S["decay_done"], 1)
                for n in range(NT // 2):
                    act.wait_ge(S["r_done"], n + 1)
                    if n >= 2:
                        act.wait_ge(S["r_used"], n - 1)
                    act.activation(rg[:, n % 2, :], ps[:, 4 + n % 2, :], ACT.Sigmoid).then_inc(S["r_ready"], 1)
                sqrt()
                sqrt()
                for th in range(2):
                    for ic in range(IC):
                        n = th * IC + ic
                        act.wait_ge(S["ck_done"], n + 1)
                        act.activation(kT[:, ic, :], ps[:, n % 4, :], ACT.Relu).then_inc(S["ck_relu"], 1)
                    for t in range(4):
                        n = th * 4 + t
                        act.wait_ge(S["cv_done"], n + 1)
                        if n >= 2:
                            act.wait_ge(S["cv_used"], n - 1)
                        act.activation(rg[:, n % 2, 0:D], ps[:, 4 + n % 2, D:2 * D], ACT.Sigmoid).then_inc(S["cv_sig"], 1)

            sqrt(2)
            attention(0)
            moe(0)
            rwkv()
            sqrt(2)
            attention(1)
            moe(1)

        @block.vector
        def _(dve):
            steps = [0]

            def link(ins):
                steps[0] += 1
                ins.then_inc(S["dve_step"], 1)
                dve.wait_ge(S["dve_step"], steps[0])

            n_std = [0]
            n_turn = [0]

            def rstds(k=1):
                n_std[0] += 1
                dve.wait_ge(S["std_ready"], n_std[0])
                link(dve.reciprocal(rstd[:, 0:k, :], std[:, 0:k, :]))

            def moments(src):
                for t in range(NT):
                    last = dve.bn_stats(stats[:, t, :], src[:, t, :])
                link(last)
                for t in range(NT):
                    last = dve.bn_aggr(meanvar[:, t, :], stats[:, t, :])
                link(last)

            def normalise(dst, src, row=0, signal=False):
                for t in range(NT):
                    last = dve.tensor_scalar(dst[:, t, :], src[:, t, :], meanvar[:, t, 0:1], rstd[:, row, t:t + 1],
                                             ALU.subtract, ALU.mult)
                    if signal:
                        last.then_inc(S["y_ready"], 1)
                if not signal:
                    link(last)

            def scale_rows(dst, src, row, signal):
                for t in range(NT):
                    last = dve.tensor_scalar(dst[:, t, :], src[:, t, :], rstd[:, row, t:t + 1], None, ALU.mult)
                    if signal:
                        last.then_inc(S["y_ready"], 1)
                if not signal:
                    link(last)

            def two_norms(eps1, eps2):
                link(dve.tensor_scalar(var[:, 0, :], meanvar[:, :, 1], eps1, None, ALU.add))
                link(dve.reciprocal(std[:, 0, :], var[:, 0, :]))
                link(dve.tensor_tensor(var[:, 1, :], meanvar[:, :, 1], std[:, 0, :], ALU.mult))
                dve.tensor_scalar(var[:, 1, :], var[:, 1, :], eps2, None, ALU.add).then_inc(S["var_ready"], 1)
                rstds(2)

            def one_norm(eps):
                dve.tensor_scalar(var[:, 0, :], meanvar[:, :, 1], eps, None, ALU.add).then_inc(S["var_ready"], 1)
                rstds()

            def take_turned(gain, bias=None):
                u0 = NT * n_turn[0]
                n_turn[0] += 1
                for t in range(NT):
                    dve.wait_ge(S["turned"], u0 + t + 1)
                    src = ps[:, 4 + t % 2, 0:D].rearrange("p (c n) -> p c n", c=DC)
                    for c in range(DC):
                        dst = xT[:, c, 1 + t * P:1 + (t + 1) * P]
                        g = cols[:, c, gain:gain + 1]
                        if bias is None:
                            last = dve.tensor_scalar(dst, src[:, c, :], g, None, ALU.mult)
                        else:
                            last = dve.tensor_scalar(dst, src[:, c, :], g, cols[:, c, bias:bias + 1], ALU.mult, ALU.add)
                    last.then_inc(S["xT_ready"], 1)

            dve.sem_inc(S["rope_read"], 1)
            dve.sem_inc(S["out_added"], 1)
            dve.memset(ones[:], 1.0)
            dve.memset(xT[:, :, 0:1], 0.0)
            dve.wait_ge(S["consts_in"], 16 * 4)
            dve.tensor_copy(square16[:], square[:, 0:2, :]).then_inc(S["consts_ready"], 1)
            dve.wait_ge(S["cols_in"], 16 * 8)
            dve.wait_ge(S["x_in"], 16)

            def attention(f):
                moments(x)
                two_norms(EPS, EPS)
                normalise(h, x)
                scale_rows(y, h, 1, True)
                take_turned(N1)
                with dve.Fori(0, KVH) as g:
                    gg = f * KVH + g
                    bank = [0, 1, 4, 5, 6, 7, 0, 1, 2, 3]
                    for b in range(10):
                        half = slice((b % 2) * HALF, (b % 2 + 1) * HALF)
                        dst = keysT[:, half] if b < 2 else queriesT[:, (b - 2) // 2, half]
                        src = ps[:, bank[b], :]
                        dve.wait_ge(S["rope_ps"], 1 + 10 * gg + b + 1)
                        k = SCALE if b < 2 else 1.0
                        dve.scalar_tensor_tensor(out=dst, in0=src, scalar=k, in1=rope[:, 0, half], op0=ALU.mult, op1=ALU.mult)
                        if b >= 2:
                            dve.wait_ge(S["rope_done"], 10 * gg + b - 1)
                        dve.scalar_tensor_tensor(out=crossed[0:64, b % 2, :], in0=src[64:128], scalar=k,
                                                 in1=rope[0:64, 1, half], op0=ALU.mult, op1=ALU.mult)
                        dve.scalar_tensor_tensor(out=crossed[64:128, b % 2, :], in0=src[0:64], scalar=k,
                                                 in1=rope[64:128, 1, half], op0=ALU.mult, op1=ALU.mult
                                                 ).then_inc(S["rope_part"], 1)
                    for what, i, k in ORDER:
                        if what == "scores":
                            n = softmax_n(gg, i, k)
                            s = 2 * (k % 2)
                            w = (i + 1) * P
                            m = (i % 2) * REP + k
                            dve.wait_ge(S["scores_ready"], n + 1)
                            dve.tensor_reduce(negmax[:, m:m + 1], ps[:, s:s + 2, :].rearrange("p b n -> p (b n)")[:, 0:w],
                                              AX.X, ALU.max, negate=True).then_inc(S["max_ready"], 1)
                        if what == "out":
                            m = (i % 3) * REP
                            dve.wait_ge(S["exp_done"], 1 + softmax_n(gg, i, REP))
                            dve.reciprocal(rowinv[:, m:m + REP], rowsum[:, m:m + REP]).then_inc(S["rowinv_ready"], 1)
                            dve.wait_ge(S["rowinv_ready"], NT * gg + i + 1)
                            for hd in range(REP):
                                if hd % 2 == 0:
                                    dve.wait_ge(S["out_ps"], 1 + 2 * (NT * gg + i) + hd // 2 + 1)
                                else:
                                    dve.wait_ge(S["out_added"], 1 + REP * (NT * gg + i) + hd)
                                if hd == 2:
                                    dve.wait_ge(S["out_added"], 1 + REP * (NT * gg + i) + hd)
                                dve.scalar_tensor_tensor(out=h[:, i, :], in0=ps[:, 7, (hd % 2) * D:(hd % 2 + 1) * D],
                                                         scalar=rowinv[:, m + hd:m + hd + 1], in1=h[:, i, :],
                                                         op0=ALU.mult, op1=ALU.add).then_inc(S["out_added"], 1)
                dve.wait_ge(S["out_added"], 1 + REP * NT * KVH * (f + 1))

            def route(f):
                bc = lambda ap: ap.rearrange("p (t o) -> p t o", o=1).broadcast_to([P, NT, E])
                keys = small[:, C_KEY:C_KEY + E].rearrange("p (o e) -> p o e", o=1).broadcast_to([P, NT, E])
                dve.wait_ge(S["logits_ps"], f + 1)
                link(dve.tensor_copy(logits[:], ps[:, 0, 0:NT * E].rearrange("p (t e) -> p t e", t=NT)))
                for k in range(TOPK):
                    src = logits if k == 0 else work
                    if k == 1:
                        link(dve.scalar_tensor_tensor(out=work[:], in0=pick[:, 0], scalar=-BIG, in1=logits[:],
                                                      op0=ALU.mult, op1=ALU.add))
                    link(dve.tensor_reduce(top[:, k, :], src[:], AX.X, ALU.max))
                    link(dve.tensor_tensor(pick[:, k], src[:], bc(top[:, k, :]), ALU.is_equal))
                    link(dve.tensor_tensor(pick[:, k], pick[:, k], keys, ALU.mult))
                    link(dve.tensor_reduce(key[:], pick[:, k], AX.X, ALU.max))
                    link(dve.tensor_tensor(pick[:, k], pick[:, k], bc(key[:]), ALU.is_equal))
                dve.tensor_tensor(both[:], pick[:, 0], pick[:, 1], ALU.add).then_inc(S["pick_ready"], 1)
                dve.tensor_tensor(key[:], top[:, 1, :], top[:, 0, :], ALU.subtract).then_inc(S["gap_ready"], 1)
                dve.wait_ge(S["gap_exp"], f + 1)
                link(dve.tensor_scalar(wts[:, 1, :], key[:], 1.0, None, ALU.add))
                link(dve.reciprocal(wts[:, 0, :], wts[:, 1, :]))
                link(dve.tensor_tensor(wts[:, 1, :], key[:], wts[:, 0, :], ALU.mult))
                dve.wait_ge(S["routing_ps"], f + 1)
                link(dve.tensor_copy(count[:], ps[:, 1, 128:128 + E]))
                sq = cube[:, 0:E, :]
                link(dve.tensor_tensor(sq, count[:].rearrange("p (e o) -> p e o", o=1).broadcast_to([P, E, E]),
                                       small[:, C_THR:C_THR + E * E].rearrange("p (e k) -> p e k", e=E), ALU.is_gt))
                link(dve.tensor_reduce(tiles[:], sq, AX.X, ALU.add))
                link(dve.tensor_tensor(sq, tiles[:].rearrange("p (o e) -> p o e", o=1).broadcast_to([P, E, E]),
                                       small[:, C_BEFORE:C_BEFORE + E * E].rearrange("p (e k) -> p e k", e=E), ALU.mult))
                link(dve.tensor_reduce(first[:], sq, AX.X, ALU.add))
                link(dve.tensor_scalar(count[:], first[:], float(P), None, ALU.mult))
                link(dve.tensor_tensor(work[:], ps[:, 1, 0:NT * E].rearrange("p (t e) -> p t e", t=NT),
                                       count[:].rearrange("p (o e) -> p o e", o=1).broadcast_to([P, NT, E]), ALU.add))
                for k in range(TOPK):
                    link(dve.tensor_tensor(pick[:, k], pick[:, k], work[:], ALU.mult))
                    link(dve.tensor_reduce(slotf[:, k, :], pick[:, k], AX.X, ALU.add))
                dve.tensor_copy(slot[:], slotf[:]).then_inc(S["routed"], 1)
                link(dve.tensor_tensor(tiles[:], tiles[:], first[:], ALU.add))
                link(dve.tensor_tensor(cube[:], small[:, C_SLOT:].rearrange("p (n e) -> p n e", n=NS),
                                       tiles[:].rearrange("p (o e) -> p o e", o=1).broadcast_to([P, NS, E]), ALU.is_ge))
                link(dve.tensor_reduce(ownerf[:], cube[:], AX.X, ALU.add))
                dve.tensor_scalar(owner[:], ownerf[:], float(E - 1), None, ALU.min).then_inc(S["owner_ready"], 1)

            def take_xs(f, tau, par):
                n = NS * f + tau
                dve.wait_ge(S["xs_turned"], n + 1)
                for c in range(DC):
                    last = dve.tensor_scalar(xsT[:, par, c, :], ps[:, 4 + par, c * P:(c + 1) * P],
                                             cols[:, c, N2:N2 + 1], None, ALU.mult)
                last.then_inc(S["xsT_ready"], 1)

            def take_hid(f, tau, par):
                dve.wait_ge(S["silu_done"], NS * f + tau + 1)
                dve.tensor_tensor(hid[:, par, :], gated[:, par, :], ps[:, 2 * par + 1, :], ALU.mult).then_inc(S["hid_ready"], 1)

            def take_ys(f, tau, par, k):
                dve.wait_ge(S["down_done"], NS * f + tau + 1)
                if not (isinstance(k, int) and PAR[par] * f + k == 0):
                    dve.wait_ge(ys_out[par], 16 * (PAR[par] * f + k))
                dve.tensor_copy(ys[:, par, :], ps[:, 7, 0:D]).then_inc(S["ys_ready"], 1)

            def moe(f):
                for t in range(NT):
                    last = dve.scalar_tensor_tensor(out=y[:, t, :], in0=h[:, t, :], scalar=1.0 / D, in1=h[:, t, :],
                                                    op0=ALU.mult, op1=ALU.mult, accum_out=var[:, 1, t:t + 1])
                link(last)
                dve.tensor_scalar(var[:, 0, :], var[:, 1, :], EPS, None, ALU.add).then_inc(S["var_ready"], 1)
                rstds()
                scale_rows(y, h, 0, True)
                take_turned(N2)
                route(f)
                take_xs(f, 0, 0)
                take_hid(f, 0, 0)
                take_xs(f, 1, 1)
                take_hid(f, 1, 1)
                take_xs(f, 2, 0)
                take_ys(f, 0, 0, 0)
                take_hid(f, 2, 0)
                take_xs(f, 3, 1)
                take_ys(f, 1, 1, 0)
                with dve.Fori(1, (NS - 3) // 2) as k:
                    take_hid(f, 2 * k + 1, 1)
                    take_xs(f, 2 * k + 2, 0)
                    take_ys(f, 2 * k, 0, k)
                    take_hid(f, 2 * k + 2, 0)
                    take_xs(f, 2 * k + 3, 1)
                    take_ys(f, 2 * k + 1, 1, k)
                k = (NS - 3) // 2
                take_hid(f, 2 * k + 1, 1)
                take_xs(f, 2 * k + 2, 0)
                take_ys(f, 2 * k, 0, k)
                take_hid(f, 2 * k + 2, 0)
                take_ys(f, 2 * k + 1, 1, k)
                take_ys(f, 2 * k + 2, 0, k + 1)
                dve.wait_ge(S["x_back"], 16 * (f + 1))
                for t in range(NT):
                    dve.wait_ge(gathered[t], 32 * (f + 1))
                    for k in range(TOPK):
                        link(dve.scalar_tensor_tensor(out=h[:, t, :], in0=back[:, k, t, :], scalar=wts[:, k, t:t + 1],
                                                      in1=h[:, t, :], op0=ALU.mult, op1=ALU.add))
                    last = dve.scalar_tensor_tensor(out=x[:, t, :], in0=h[:, t, :], scalar=0.5, in1=x[:, t, :],
                                                    op0=ALU.mult, op1=ALU.add)
                if f == 0:
                    link(last)
                else:
                    last.then_inc(S["x_final"], 1)

            def gain_rows(dst, k):
                for j, op in ((0, ALU.mult), (1, ALU.add)):
                    row = rows[:, k + j, :].rearrange("p (o d) -> p o d", o=1).broadcast_to([P, NT, D])
                    link(dve.tensor_tensor(dst, dst, row, op))

            def rwkv():
                dve.wait_ge(S["rwkv_in"], 16 * 11)
                moments(x)
                two_norms(EPS, EPS_RWKV)
                normalise(h, x)
                scale_rows(y, h, 1, False)
                gain_rows(y, 0)
                moments(y)
                one_norm(EPS_RWKV)
                normalise(y, y, signal=True)
                take_turned(TMG, TMB)
                link(dve.tensor_scalar(vmix[:], cols[:, :, TF], -1.0, 1.0, ALU.mult, ALU.add))
                for c in range(DC):
                    link(dve.tensor_scalar(mixT[:, c, :], xT[:, c, 0:T], vmix[:, c:c + 1], None, ALU.mult))
                    dve.scalar_tensor_tensor(out=mixT[:, c, :], in0=xT[:, c, 1:1 + T], scalar=cols[:, c, TF:TF + 1],
                                             in1=mixT[:, c, :], op0=ALU.mult, op1=ALU.add).then_inc(S["mix_ready"], 1)
                for n in range(4):
                    dve.wait_ge(S["v_done"], n + 1)
                    dve.wait_ge(S["decay_done"], n + 1)
                    dve.tensor_tensor_reduce(out=decay[:], in0=ps[:, n, :], in1=decay[:], scale=1.0, scalar=0.0,
                                             op0=ALU.mult, op1=ALU.add, accum_out=vsum[:, n:n + 1]).then_inc(S["decay_used"], 1)
                dve.wait_ge(S["decay_used"], 4)
                dve.wait_ge(S["mix_ready"], 2)
                link(dve.tensor_reduce(vmix[:], vsum[:].rearrange("p (c k) -> p c k", c=2), AX.X, ALU.add))
                for c in range(DC):
                    dve.tensor_scalar(vwide[:, c, :], ones[:], vmix[:, c:c + 1], None, ALU.mult).then_inc(S["vw_ready"], 1)
                dve.wait_ge(S["u_done"], 1)
                link(dve.tensor_tensor(u[:], ps[:, 0, 0:D], rows[:, 4, :], ALU.add))
                wide = u[:].rearrange("p (o d) -> p o d", o=1).broadcast_to([P, 2, D])
                for n in range(NT // 2):
                    dve.wait_ge(S["r_ready"], n + 1)
                    r2 = rg[:, n % 2, :].rearrange("p (k d) -> p k d", k=2)
                    link(dve.tensor_tensor(r2, r2, wide, ALU.mult))
                    last = dve.tensor_tensor(h[:, 2 * n:2 * n + 2, :], h[:, 2 * n:2 * n + 2, :], r2, ALU.add)
                    last.then_inc(S["r_used"], 1)
                dve.wait_ge(S["r_used"], NT // 2)
                moments(h)
                one_norm(EPS_RWKV)
                normalise(y, h)
                gain_rows(y, 2)
                moments(y)
                one_norm(EPS_RWKV)
                normalise(y, y, signal=True)
                take_turned(CMG, CMB)
                for th in range(2):
                    for ic in range(IC):
                        n = th * IC + ic
                        dve.wait_ge(S["ck_relu"], n + 1)
                        dve.tensor_tensor(kT[:, ic, :], kT[:, ic, :], kT[:, ic, :], ALU.mult).then_inc(S["ck_sq"], 1)
                    for t in range(4):
                        n = th * 4 + t
                        dve.wait_ge(S["cv_sig"], n + 1)
                        link(dve.tensor_tensor(rg[:, n % 2, D:2 * D], rg[:, n % 2, 0:D], ps[:, 4 + n % 2, 0:D], ALU.mult))
                        link(dve.tensor_tensor(h[:, n, :], h[:, n, :], rg[:, n % 2, D:2 * D], ALU.add))
                        dve.tensor_tensor(x[:, n, :], x[:, n, :], h[:, n, :], ALU.add).then_inc(S["cv_used"], 1)
                dve.wait_ge(S["cv_used"], NT)
                dve.sem_inc(S["x_final"], 1)

            attention(0)
            moe(0)
            rwkv()
            attention(1)
            moe(1)

        @block.tensor
        def _(pe):
            n_turn = [0]

            pe.sem_inc(S["rope_ps"], 1)
            pe.sem_inc(S["v_ps"], 1)
            pe.sem_inc(S["out_ps"], 1)
            pe.wait_ge(S["consts_ready"], 1)

            def turn_tokens():
                u0 = NT * n_turn[0]
                n_turn[0] += 1
                for t in range(NT):
                    pe.wait_ge(S["y_ready"], u0 + t + 1)
                    if t >= 2:
                        pe.wait_ge(S["xT_ready"], u0 + t - 1)
                    for c in range(DC):
                        last = pe.transpose(ps[:, 4 + t % 2, c * P:(c + 1) * P], y[:, t, c * P:(c + 1) * P], ident)
                    last.then_inc(S["turned"], 1)

            def tokens(c, t):
                return xT[:, c, 1 + t * P:1 + (t + 1) * P]

            def attention(f):
                turn_tokens()
                pe.wait_ge(S["xT_ready"], NT * n_turn[0])
                with pe.Fori(0, KVH) as g:
                    gg = f * KVH + g
                    pe.wait_ge(S["qkv_in"], 48 * (gg + 1))
                    pe.wait_ge(S["exp_done"], 1 + SOFT * gg)

                    def project(b, bank, col):
                        half = 1 + (b % 2) * HALF
                        for c in range(DC):
                            last = pe.matmul(ps[:, bank, :], w_qkv[:, c, col:col + HD], xT[:, c, half:half + HALF],
                                             start=(c == 0), stop=(c == DC - 1))
                        last.then_inc(S["rope_ps"], 1)

                    for b in range(2):
                        project(b, b, REP * HD)
                    for t in range(NT):
                        for c in range(DC):
                            last = pe.matmul(ps[:, 2 + t // 4, (t % 4) * HD:(t % 4 + 1) * HD], tokens(c, t),
                                             w_qkv[:, c, REP * HD + HD:], start=(c == 0), stop=(c == DC - 1))
                        if t % 4 == 3:
                            last.then_inc(S["v_ps"], 1)
                    bank = [4, 5, 6, 7, 0, 1, 2, 3]
                    for b in range(8):
                        if b == 0:
                            pe.wait_ge(S["probsT_ready"], 1 + TURNS * gg)
                        if b == 2:
                            pe.wait_ge(S["attnT_ready"], 1 + NT * gg)
                        if b == 3:
                            pe.wait_ge(S["out_added"], 1 + REP * NT * gg)
                        if b in (4, 5):
                            pe.wait_ge(S["rope_part"], 10 * gg + b - 3)
                        if b in (6, 7):
                            pe.wait_ge(S["v_ready"], 2 * gg + b - 5)
                        project(b, bank[b], (b // 2) * HD)
                    pe.wait_ge(S["rope_done"], 10 * gg + 10)
                    pe.wait_ge(S["wo_in"], 16 * (gg + 1))
                    for what, i, k in ORDER:
                        if what == "scores":
                            s = 2 * (k % 2)
                            n = softmax_n(gg, i, k)
                            if i or k >= 2:
                                pe.wait_ge(S["exp_done"], 1 + n - 1)
                            q = queriesT[:, k, i * P:(i + 1) * P]
                            w = (i + 1) * P
                            for b in range((w + 511) // 512):
                                n1 = min(512, w - 512 * b)
                                diag = b == i // 4
                                last = pe.matmul(ps[:, s + b, 0:n1], q, keysT[:, 512 * b:512 * b + n1], start=True, stop=not diag)
                            last = pe.matmul(ps[:, s + i // 4, (i % 4) * P:(i % 4 + 1) * P], square16[:, 0, :], square16[:, 1, :],
                                             start=False, stop=True)
                            last.then_inc(S["scores_ready"], 1)
                        if what == "turn":
                            m = turns_before(i) + k
                            if k == 0:
                                pe.wait_ge(S["exp_done"], 1 + softmax_n(gg, i, REP))
                            if m >= 2:
                                pe.wait_ge(S["probsT_ready"], 1 + TURNS * gg + m - 1)
                            for hd in range(REP):
                                last = pe.transpose(ps[:, 4 + m % 2, hd * P:(hd + 1) * P],
                                                    probs[:, i % 2, hd, k * P:(k + 1) * P], ident)
                            last.then_inc(S["turn_done"], 1)
                        if what == "values":
                            m = turns_before(i) + k
                            pe.wait_ge(S["probsT_ready"], 1 + TURNS * gg + m + 1)
                            if k == 0 and i:
                                pe.wait_ge(S["attnT_ready"], 1 + NT * gg + i)
                            last = pe.matmul(ps[:, 6, :], values[:, k, :], probsT[:, m % 3, :], start=(k == 0), stop=(k == i))
                            if k == i:
                                last.then_inc(S["pv_done"], 1)
                        if what == "out":
                            pe.wait_ge(S["attnT_ready"], 1 + NT * gg + i + 1)
                            for hd in range(REP):
                                if hd % 2 == 0 and (i or hd):
                                    pe.wait_ge(S["out_added"], 1 + REP * (NT * gg + i) + hd)
                                last = pe.matmul(ps[:, 7, (hd % 2) * D:(hd % 2 + 1) * D], attnT[:, i % 2, hd * P:(hd + 1) * P],
                                                 w_o[:, hd, :], start=True, stop=True)
                                if hd % 2 == 1:
                                    last.then_inc(S["out_ps"], 1)

            def expert(tau):
                return pe.value_load(owner[0:1, bass.ds(tau, 1)], min_val=0, max_val=E - 1)

            def turn_xs(f, tau, par, k):
                pe.wait_ge(xs_in[par], 16 * (PAR[par] * f + k + 1))
                for c in range(DC):
                    last = pe.transpose(ps[:, 4 + par, c * P:(c + 1) * P], xs[:, par, c * P:(c + 1) * P], ident)
                last.then_inc(S["xs_turned"], 1)

            def up(f, tau, par):
                e = expert(tau)
                pe.wait_ge(S["xsT_ready"], NS * f + tau + 1)
                for w, b in ((w1, 2 * par), (w3, 2 * par + 1)):
                    for c in range(DC):
                        last = pe.matmul(ps[:, b, :], xsT[:, par, c, :], w[:, bass.ds(e, 1), c, :],
                                         start=(c == 0), stop=(c == DC - 1))
                last.then_inc(S["up_done"], 1)

            def turn_hid(f, tau, par):
                pe.wait_ge(S["hid_ready"], NS * f + tau + 1)
                for c in range(FC):
                    last = pe.transpose(ps[:, 6, c * P:(c + 1) * P], hid[:, par, c * P:(c + 1) * P], ident)
                last.then_inc(S["hid_turned"], 1)

            def down(f, tau, par):
                e = expert(tau)
                pe.wait_ge(S["hidT_ready"], NS * f + tau + 1)
                if not (isinstance(tau, int) and NS * f + tau == 0):
                    pe.wait_ge(S["ys_ready"], NS * f + tau)
                for c in range(FC):
                    last = pe.matmul(ps[:, 7, 0:D], hidT[:, par, c, :], w2[:, bass.ds(e, 1), c, :],
                                     start=(c == 0), stop=(c == FC - 1))
                last.then_inc(S["down_done"], 1)

            def moe(f):
                turn_tokens()
                pe.wait_ge(S["xT_ready"], NT * n_turn[0])
                for t in range(NT):
                    for c in range(DC):
                        last = pe.matmul(ps[:, 0, t * E:(t + 1) * E], tokens(c, t), gate[:, c, :],
                                         start=(c == 0), stop=(c == DC - 1))
                last.then_inc(S["logits_ps"], 1)
                pe.wait_ge(S["pick_ready"], f + 1)
                pe.matmul(ps[:, 1, 0:NT * E], upper, both[:].rearrange("p t e -> p (t e)"), start=True, stop=False)
                for s in range(1, NT):
                    pe.matmul(ps[:, 1, s * E:NT * E], ones[:], both[:, 0:NT - s, :].rearrange("p t e -> p (t e)"),
                              start=False, stop=(s == NT - 1))
                for t in range(NT):
                    last = pe.matmul(ps[:, 1, 128:128 + E], ones[:], both[:, t, :], start=(t == 0), stop=(t == NT - 1))
                last.then_inc(S["routing_ps"], 1)
                pe.wait_ge(S["owner_ready"], f + 1)
                if f == 0:
                    pe.wait_ge(S["experts_in"], 16 * 3 * E)
                turn_xs(f, 0, 0, 0)
                up(f, 0, 0)
                turn_xs(f, 1, 1, 0)

                def step(tau, par, k, more=True):
                    turn_hid(f, tau - 1, 1 - par)
                    up(f, tau, par)
                    if more:
                        turn_xs(f, tau + 1, 1 - par, k)
                    down(f, tau - 1, 1 - par)

                with pe.Fori(0, (NS - 3) // 2) as k:
                    step(2 * k + 1, 1, k + 1)
                    step(2 * k + 2, 0, k + 1)
                k = (NS - 3) // 2
                step(NS - 2, 1, k + 1)
                step(NS - 1, 0, k + 1, more=False)
                turn_hid(f, NS - 1, 0)
                down(f, NS - 1, 0)

            def rwkv():
                turn_tokens()
                pe.wait_ge(S["xT_ready"], NT * n_turn[0])
                for n in range(4):
                    hc, th = divmod(n, 2)
                    for c in range(DC):
                        last = pe.matmul(ps[:, n, :], Wv[:, c, hc * P:(hc + 1) * P], xT[:, c, 1 + th * HALF:1 + (th + 1) * HALF],
                                         start=(c == 0), stop=(c == DC - 1))
                    last.then_inc(S["v_done"], 1)
                pe.wait_ge(S["mix_ready"], 2)
                for n in range(NT // 2):
                    if n >= 2:
                        pe.wait_ge(S["r_ready"], n - 1)
                    for k in range(2):
                        t = 2 * n + k
                        for c in range(DC):
                            last = pe.matmul(ps[:, 4 + n % 2, k * D:(k + 1) * D], mixT[:, c, t * P:(t + 1) * P], Wr[:, c, :],
                                             start=(c == 0), stop=(c == DC - 1))
                    last.then_inc(S["r_done"], 1)
                    if n == 1:
                        pe.wait_ge(S["vw_ready"], 2)
                        for c in range(DC):
                            last = pe.matmul(ps[:, 0, 0:D], vwide[:, c, :], Wo[:, c, :], start=(c == 0), stop=(c == DC - 1))
                        last.then_inc(S["u_done"], 1)
                turn_tokens()
                pe.wait_ge(S["xT_ready"], NT * n_turn[0])
                for th in range(2):
                    for ic in range(IC):
                        n = th * IC + ic
                        if n >= 4:
                            pe.wait_ge(S["ck_relu"], n - 3)
                        for c in range(DC):
                            last = pe.matmul(ps[:, n % 4, :], Wck[:, c, ic * P:(ic + 1) * P], xT[:, c, th * HALF:(th + 1) * HALF],
                                             start=(c == 0), stop=(c == DC - 1))
                        last.then_inc(S["ck_done"], 1)
                    pe.wait_ge(S["ck_sq"], IC * (th + 1))
                    for t in range(4):
                        n = th * 4 + t
                        if n >= 2:
                            pe.wait_ge(S["cv_used"], n - 1)
                        for c in range(DC):
                            pe.matmul(ps[:, 4 + n % 2, D:2 * D], tokens(c, n), Wcr[:, c, :], start=(c == 0), stop=(c == DC - 1))
                        for ic in range(IC):
                            last = pe.matmul(ps[:, 4 + n % 2, 0:D], kT[:, ic, t * P:(t + 1) * P], Wcv[:, ic, :],
                                             start=(ic == 0), stop=(ic == IC - 1))
                        last.then_inc(S["cv_done"], 1)

            attention(0)
            moe(0)
            rwkv()
            attention(1)
            moe(1)


_INS = ["L0_attn_x", "L0_attn_ln1_g", "L0_attn_ln1_b", "L0_attn_ln2_g", "L0_attn_ln2_b", "L0_attn_tm_g",
        "L0_attn_tm_b", "L0_attn_time_decay", "L0_attn_time_first", "L0_attn_Wv", "L0_attn_Wr", "L0_attn_Wo",
        "L0_attn_bo", "L0_attn_cm_g", "L0_attn_cm_b", "L0_attn_Wck", "L0_attn_Wcv", "L0_attn_Wcr",
        "L0_ffn_norm1_w", "L0_ffn_norm2_w", "L0_ffn_wq", "L0_ffn_wk", "L0_ffn_wv", "L0_ffn_wo",
        "L0_ffn_gate_w", "L0_ffn_w1", "L0_ffn_w3", "L0_ffn_w2"]


def kernel(**inputs):
    import concourse.bacc as _bacc
    from concourse.bass_utils import run_bass_kernel_spmd as _run

    nc = _bacc.Bacc("TRN2", target_bir_lowering=False, num_devices=1)
    arrays, args = {}, {}
    given = {name: inputs[name] for name in _INS}
    given.update(constants())
    for name, value in given.items():
        v = np.ascontiguousarray(value)
        arrays[f"in_{name}_dram"] = v
        args[name] = nc.dram_tensor(f"in_{name}_dram", v.shape, mybir.dt.from_np(v.dtype), kind="ExternalInput").ap()
    out = nc.dram_tensor("out_dram", (1, T, D), F32, kind="ExternalOutput").ap()
    scratch = (nc.dram_tensor("xs_dram", (NS * P, D), F32, kind="Internal").ap(),
               nc.dram_tensor("ys_dram", (NS * P, D), F32, kind="Internal").ap(),
               nc.dram_tensor("xsave_dram", (T, D), F32, kind="Internal").ap())
    macaron(nc, args, out, scratch)
    r = _run(nc, [arrays], core_ids=[0])
    return r.results[0]["out_dram"]
```

```python
from contextlib import ExitStack

import numpy as np

import concourse.bass as bass
from concourse import mybir

F32 = mybir.dt.float32
F32R = mybir.dt.float32r
BF16 = mybir.dt.bfloat16
I32 = mybir.dt.int32
U32 = mybir.dt.uint32
ALU = mybir.AluOpType
ACT = mybir.ActivationFunctionType
AX = mybir.AxisListType

P = 128
T, D = 1024, 256
NT, DC = T // P, D // P
HEADS, KVH, HD = 16, 4, 128
REP = HEADS // KVH
E, F = 8, 512
FC = F // P
TOPK = 2
NS = (TOPK * T + E * (P - 1)) // P
RI = 1024
IC = RI // P
HALF = 512
SCALE = float(1.0 / np.sqrt(HD))
EPS, EPS_RWKV = 1e-5, 1e-12
BIG = 1e30
THETA = 1000000.0

RES = 2
TURNS = NT * (NT + 1) // 2
SOFT = NT * REP


def turns_before(i):
    return i * (i + 1) // 2


def group_order(more):
    steps = {}

    def add(engine, step, us, place, *before):
        steps[step] = (engine, us, place, [x for x in before if x in steps])

    blocks = [("q1", k, 0.3 + 0.7 * k) for k in range(REP)]
    if more:
        blocks += [("q0", k, 4.6 + 0.5 * k) for k in range(REP)] + [("k", 0, 6.9), ("k", 1, 7.1)]
    for i in range(NT):
        for hd in range(REP):
            w = (i + 1) * P
            add("PE", ("scores", i, hd), 0.06 + 3 * w / 2400, i - 0.8 + 0.2 * hd, ("scores", i, hd - 1), ("scores", i - 1, REP - 1),
                ("turn", i - 2, i - 2), ("exp", i - 2, hd))
            add("DVE", ("max", i, hd), 0.17 + w / 960, i - 0.8 + 0.2 * hd, ("scores", i, hd), ("max", i, hd - 1),
                ("max", i - 1, REP - 1), ("attn_low", i - 3, 0))
            add("ACT", ("exp", i, hd), 0.38 + w / 1200, i - 0.8 + 0.2 * hd, ("max", i, hd), ("exp", i, hd - 1),
                ("exp", i - 1, REP - 1))
        for j in range(i + 1):
            at = i + j / (i + 1)
            m = turns_before(i) + j
            m_of = {turns_before(a) + b: (a, b) for a in range(NT) for b in range(a + 1)}
            bank, ring = m_of.get(m - 2, (-1, -1)), m_of.get(m - 3, (-1, -1))
            last = m_of.get(m - 1, (-1, -1))
            add("PE", ("turn", i, j), 0.43, at, ("exp", i, REP - 1), ("low", *bank), ("values", *ring), ("turn", *last))
            add("ACT", ("high", i, j), 0.52, at, ("turn", i, j), ("high", *last))
            add("DVE", ("low", i, j), 0.62, at, ("high", i, j), ("low", *last))
            add("PE", ("values", i, j), 0.64, at + 1.0 / (i + 1), ("low", i, j), ("values", *last), ("added", i - 2, 1))
        add("ACT", ("attn_high", i, 0), 0.52, i + 1.2, ("values", i, i), ("attn_high", i - 1, 0), ("out", i - 2, 1))
        add("DVE", ("attn_low", i, 0), 0.75, i + 1.2, ("attn_high", i, 0), ("attn_low", i - 1, 0))
        for k in range(2):
            add("PE", ("out", i, k), 0.64, i + 1.3 + 0.2 * k, ("attn_low", i, 0), ("added", i, k - 1), ("out", i - 1, 1))
            add("DVE", ("added", i, k), 0.95, i + 1.3 + 0.2 * k, ("out", i, k), ("added", i, k - 1), ("added", i - 1, 1))
    for n, (w, k, at) in enumerate(blocks):
        before = [(what, *blocks[n - 1][:2]) for what in ("project", "crossed", "straight", "rotated")] if n else [None] * 4
        two = [(what, *blocks[n - 2][:2]) for what in ("rotated",)] if n > 1 else [None]
        free = {"q1": None, "q0": ("scores", 3, REP - 1), "k": ("scores", NT - 1, REP - 1)}[w]
        add("PE", ("project", w, k), 1.28, at, before[0], free, ("w_split", 0, 0) if w != "q1" else None)
        add("ACT", ("crossed", w, k), 1.1, at, ("project", w, k), before[1], two[0])
        add("DVE", ("straight", w, k), 0.66, at, ("crossed", w, k), before[2])
        add("Pool", ("rotated", w, k), 4.6, at, ("crossed", w, k), ("straight", w, k), before[3])
        if (w, k) == ("q1", REP - 1) and more:
            add("Pool", ("w_split", 0, 0), 7.0, at + 0.1, ("project", w, k), ("rotated", w, k))
    if more:
        for k in range(2):
            add("PE", ("project", "v", k), 1.28, 7.8, ("project", "k", 1), ("project", "v", k - 1))
            add("ACT", ("v_high", k, 0), 0.52, 8, ("values", NT - 1, NT - 1), ("project", "v", k), ("v_high", k - 1, 0))
            add("DVE", ("v_low", k, 0), 0.66, 8, ("v_high", k, 0), ("v_low", k - 1, 0))
    for q, (_, _, at, _) in list(steps.items()):
        if q[0] == "scores" and q[1] == 4:
            steps[q][3].append(("rotated", "q1", q[2]))
        if q[0] == "scores" and q[1] >= 6 and more:
            pass

    leaves = {"scores": ["exp"], "project": ["straight"]}
    free_at = dict.fromkeys(("PE", "ACT", "DVE", "Pool"), 0.0)
    done, orders, slots = {}, {e: [] for e in free_at}, []
    while len(done) < len(steps):
        best = None
        for step, (engine, us, at, before) in steps.items():
            if step in done or any(x not in done for x in before):
                continue
            start = max([free_at[engine]] + [done[x] + (0.12 if steps[x][0] != engine else 0.07 * (engine != "PE")) for x in before])
            if step[0] in ("scores", "project") and len(slots) >= 2:
                user = slots[-2]
                left = [("v_low", user[2], 0)] if user[1] == "v" else [(what, *user[1:]) for what in leaves[user[0]]]
                if any(x not in done for x in left):
                    continue
                start = max([start] + [done[x] + 0.12 for x in left])
            rank = (max(start, free_at[engine] + SLACK[engine]), at, start)
            if best is None or rank < best[0]:
                best = (rank, start, step)
        _, start, step = best
        engine, us, _, _ = steps[step]
        done[step] = free_at[engine] = start + us
        orders[engine].append(step)
        if step[0] in ("scores", "project"):
            slots.append(step)
    return orders, max(done.values())


SLACK = {"PE": 0.1, "ACT": 0.1, "DVE": 0.1, "Pool": 0.1}


def slot_users(order):
    found, n, last = {}, 0, [None, None]
    for step in order["PE"]:
        if step[0] in ("scores", "project"):
            found[step] = (n % 2, n // 2, last[n % 2])
            last[n % 2] = step
            n += 1
    return found, n // 2


_first = [("k", 0), ("q0", 0), ("q0", 1), ("q0", 2), ("q0", 3), ("k", 1)]
FIRST = {
    "PE": [("project", *b) for b in _first] + [("project", "v", 0), ("project", "v", 1)],
    "ACT": [("crossed", *b) for b in _first] + [("v_high", 0, 0), ("v_high", 1, 0)],
    "DVE": [("straight", *b) for b in _first] + [("v_low", 0, 0), ("v_low", 1, 0)],
    "Pool": [("rotated", *b) for b in _first],
}


C_KEY, C_THR, C_BEFORE, C_SLOT = 0, 8, 72, 136
C_ALL = C_SLOT + NS * E


def constants():
    inv = (1.0 / THETA ** (np.arange(0, HD, 2, dtype=np.float32) / np.float32(HD))).astype(np.float32)
    ang = np.arange(T, dtype=np.float32)[None, :] * inv[:, None]
    cos, sin = np.cos(ang).astype(np.float32), np.sin(ang).astype(np.float32)
    rope = np.concatenate([np.concatenate([cos, cos]), np.concatenate([-sin, sin])], axis=1)
    ident = np.eye(P, dtype=np.float32)
    r = np.arange(P)
    mask = np.where(r[None, :] <= r[:, None], 0.0, -BIG).astype(np.float32)
    before = (r[:, None] < r[None, :]).astype(np.float32)
    small = np.zeros((P, C_ALL), np.float32)
    e = np.arange(E)
    small[:, C_KEY:C_KEY + E] = E - e
    small[:, C_THR:C_THR + E * E] = np.tile(P * e, E)
    small[:, C_BEFORE:C_BEFORE + E * E] = (e[None, :] < e[:, None]).ravel()
    small[:, C_SLOT:] = np.repeat(np.arange(NS), E)
    left = np.tile((T - 1 - np.arange(T, dtype=np.float32))[None, :], (P, 1))
    return {
        "c_rope": np.ascontiguousarray(rope, np.float32),
        "c_square": np.ascontiguousarray(np.concatenate([ident, mask, before], axis=1)),
        "c_small": small,
        "c_left": np.ascontiguousarray(left, np.float32),
    }


def macaron(nc, a, out, scratch):
    xs_dram, ys_dram, xsave_dram = scratch

    with ExitStack() as ctx:
        def sb(name, shape, dt=F32, c=ctx):
            return c.enter_context(nc.sbuf_tensor(name, shape, dt))

        def sem(name):
            return ctx.enter_context(nc.semaphore(name))

        ps = ctx.enter_context(nc.psum_tensor("ps", [P, 8, 512], F32))

        h = sb("h", [P, NT, D])
        rope = sb("rope", [P, 2, T])
        probs = sb("probs", [P, 2, REP, T])
        flat = probs[:].rearrange("p a b t -> p (a b t)")
        x = flat[:, 0:NT * D].rearrange("p (t d) -> p t d", t=NT)
        y = flat[:, NT * D:2 * NT * D].rearrange("p (t d) -> p t d", t=NT)
        back = flat[:, 2 * NT * D:].rearrange("p (k t d) -> p k t d", k=2, t=NT)
        kT = flat[:, 2 * NT * D:].rearrange("p (i t) -> p i t", i=IC)
        zeros = flat[:, 2 * NT * D:].rearrange("p (n d) -> p n d", d=D)
        square = sb("square", [P, 3, P])
        ident, upper = square[:, 0, :], square[:, 2, :]
        square16 = sb("square16", [P, 2, P], BF16)
        ones = sb("ones", [P, P])
        small = sb("small", [P, C_ALL])
        cols = sb("cols", [P, 2, 8])
        gate = sb("gate", [P, DC, E])
        stats = sb("stats", [P, NT, 6])
        meanvar = sb("meanvar", [P, NT, 2])
        mean = sb("mean", [P, NT])
        var = sb("var", [P, 2, NT])
        std = sb("std", [P, 2, NT])
        rstd = sb("rstd", [P, 2, NT])
        negmax = sb("negmax", [P, 8])
        rowsum = sb("rowsum", [P, 3 * REP])
        rowinv = sb("rowinv", [P, 3 * REP])

        with ExitStack() as phase:
            sb("resident", [P, RES, 3 * DC * F], c=phase)
            w_in = sb("w_in", [P, DC, REP * HD + 2 * HD], c=phase)
            w_qkv = sb("w_qkv", [P, 2, DC, REP * HD + 2 * HD], F32R, c=phase)
            wo_in = sb("wo_in", [P, REP, D], c=phase)
            w_o = sb("w_o", [P, 2, REP, D], F32R, c=phase)
            tokT = sb("tokT", [P, 2, DC, T], F32R, c=phase)
            keysT = sb("keysT", [P, 2, T], F32R, c=phase)
            values = sb("values", [P, 2, NT, HD], F32R, c=phase)
            queriesT = sb("queriesT", [P, 2, REP, T], F32R, c=phase)
            straight = sb("straight", [P, 2, HALF], c=phase)
            crossed = sb("crossed", [P, 2, HALF], c=phase)
            probsT = sb("probsT", [P, 3, 2, REP * P], F32R, c=phase)
            attnT = sb("attnT", [P, 2, 2, REP * P], F32R, c=phase)

        with ExitStack() as phase:
            experts = sb("experts", [P, E, 3 * DC * F], c=phase)
            w1 = experts[:, :, 0:DC * F].rearrange("p e (c n) -> p e c n", c=DC)
            w3 = experts[:, :, DC * F:2 * DC * F].rearrange("p e (c n) -> p e c n", c=DC)
            w2 = experts[:, :, 2 * DC * F:].rearrange("p e (c n) -> p e c n", c=FC)
            xT = sb("xT", [P, DC, 1 + T], c=phase)
            xs = sb("xs", [P, 2, D], c=phase)
            xsT = sb("xsT", [P, 2, DC, P], c=phase)
            gated = sb("gated", [P, 2, F], c=phase)
            hid = sb("hid", [P, 2, F], c=phase)
            hidT = sb("hidT", [P, 2, FC, P], c=phase)
            ys = sb("ys", [P, 2, D], c=phase)
            logits = sb("logits", [P, NT, E], c=phase)
            work = sb("work", [P, NT, E], c=phase)
            pick = sb("pick", [P, 2, NT, E], c=phase)
            both = sb("both", [P, NT, E], c=phase)
            top = sb("top", [P, 2, NT], c=phase)
            key = sb("key", [P, NT], c=phase)
            wts = sb("wts", [P, 2, NT], c=phase)
            count = sb("count", [P, E], c=phase)
            cube = sb("cube", [P, NS, E], c=phase)
            tiles = sb("tiles", [P, E], c=phase)
            first = sb("first", [P, E], c=phase)
            slotf = sb("slotf", [P, 2, NT], c=phase)
            slot = sb("slot", [P, 2, NT], U32, c=phase)
            ownerf = sb("ownerf", [P, NS], c=phase)
            owner = sb("owner", [P, NS], I32, c=phase)
            Wv = sb("Wv", [P, DC, D], c=phase)
            Wr = sb("Wr", [P, DC, D], c=phase)
            Wo = sb("Wo", [P, DC, D], c=phase)
            Wck = sb("Wck", [P, DC, RI], c=phase)
            Wcv = sb("Wcv", [P, IC, D], c=phase)
            Wcr = sb("Wcr", [P, DC, D], c=phase)
            rows = sb("rows", [P, 5, D], c=phase)
        with ExitStack() as phase:
            sb("resident_too", [P, RES, 3 * DC * F], c=phase)
            mixT = sb("mixT", [P, DC, T], c=phase)
            decay = sb("decay", [P, HALF], c=phase)
            vsum = sb("vsum", [P, 4], c=phase)
            vmix = sb("vmix", [P, 2], c=phase)
            vwide = sb("vwide", [P, DC, P], c=phase)
            u = sb("u", [P, D], c=phase)
            rg = sb("rg", [P, 2, HALF], c=phase)
        left = y
        leftv = flat[:, NT * D:NT * D + T]

        N1, N2, TMG, TMB, CMG, CMB, TF, TD = range(8)

        S = {}
        for name in (
            "consts_in experts_in x_in cols_in zeros_set zeros_out qkv_in wo_in rwkv_in left_in saved x_back stored "
            "owner_ready dve_step consts_ready var_ready std_ready y_ready turned xT_ready "
            "w_split wo_split projected_qk projected_v cross_ready straight_ready rotated qk_ready v_high v_low "
            "tokT_high tokT_low scores_ready max_ready exp_done rowinv_ready pool_step "
            "turn_done probsT_high probsT_low pv_done attnT_high attnT_low out_ps out_added xT_clear "
            "logits_ps routing_ps routed pick_ready scattered gap_ready gap_exp "
            "xs_turned xsT_ready up_done silu_done hid_ready hid_turned hidT_ready down_done ys_ready "
            "mix_ready v_done decay_done decay_used vw_ready u_done u_ready r_done r_ready r_used ck_done ck_relu ck_sq "
            "cv_done cv_sig cv_used x_final"
        ).split():
            S[name] = sem(name)
        xs_in = [sem("xs_in_even"), sem("xs_in_odd")]
        ys_out = [sem("ys_out_even"), sem("ys_out_odd")]
        gathered = [sem(f"gathered_{t}") for t in range(NT)]
        PAR = [(NS + 1) // 2, NS // 2]

        x_dram = a["L0_attn_x"].rearrange("a (t p) d -> p (a t) d", p=P)
        out_dram = out.rearrange("a (t p) d -> p (a t) d", p=P)
        xsave = xsave_dram.rearrange("(t p) d -> p t d", p=P)
        xs_tiles = xs_dram.rearrange("(n p) d -> p n d", p=P)
        ys_tiles = ys_dram.rearrange("(n p) d -> p n d", p=P)
        wq_d = a["L0_ffn_wq"].rearrange("(c p) (g n) -> p c g n", p=P, g=KVH)
        wk_d = a["L0_ffn_wk"].rearrange("(c p) (g n) -> p c g n", p=P, g=KVH)
        wv_d = a["L0_ffn_wv"].rearrange("(c p) (g n) -> p c g n", p=P, g=KVH)
        wo_d = a["L0_ffn_wo"].rearrange("(g r p) d -> p g r d", p=P, g=KVH)

        def chunks(name):
            return a[name].rearrange("(c p) n -> p c n", p=P)

        def column(name):
            return a[name].rearrange("(c p) -> p c", p=P)

        def softmax_n(gg, i, hd):
            return gg * SOFT + i * REP + hd

        ORDERS = {more: group_order(more)[0] for more in (True, False)}

        TURN_OF = [0, 4]

        class Group:

            def __init__(self, f, g, order):
                self.gg = f * KVH + g
                self.users, _ = slot_users(order)
                first = order is FIRST
                self.qk0 = 10 * KVH * f + (0 if first else 6 + 10 * g)
                self.qk = {}
                for step in order["PE"]:
                    if step[0] == "project" and step[1] != "v":
                        self.qk[step[1:]] = len(self.qk)
                self.v0 = 2 * (KVH * f + (0 if first else g + 1))

            def slot(self, step):
                return self.users[step][0]

            def qk_n(self, block):
                return self.qk0 + self.qk[block]

        def qk_place(what, k):
            if what == "k":
                return REP * HD, k, keysT[:, :, k * HALF:(k + 1) * HALF]
            half = int(what[1])
            return k * HD, half, queriesT[:, :, k, half * HALF:(half + 1) * HALF]

        block = ctx.enter_context(nc.Block())

        @block.sync
        def _(sp):
            sp.dma_start(x, x_dram).then_inc(S["x_in"], 16)
            sp.dma_start(square[:], a["c_square"].rearrange("p (k n) -> p k n", k=3)).then_inc(S["consts_in"], 16)
            for n, name in enumerate(("L0_ffn_norm1_w", "L0_ffn_norm2_w", "L0_attn_tm_g", "L0_attn_tm_b",
                                      "L0_attn_cm_g", "L0_attn_cm_b", "L0_attn_time_first", "L0_attn_time_decay")):
                with nc.allow_non_contiguous_dma(reason="256 single features"):
                    sp.dma_start(cols[:, :, n], column(name)).then_inc(S["cols_in"], 16)
            sp.dma_start(rope[:], a["c_rope"].rearrange("p (k t) -> p k t", k=2)).then_inc(S["consts_in"], 16)
            sp.dma_start(small[:], a["c_small"]).then_inc(S["consts_in"], 16)
            sp.dma_start(gate[:], chunks("L0_ffn_gate_w")).then_inc(S["consts_in"], 16)

            def attention_weights(f):
                def load(g):
                    gg = f * KVH + g
                    sp.dma_start(w_in[:, :, 0:REP * HD], wq_d[:, :, bass.ds(g, 1), :]).then_inc(S["qkv_in"], 16)
                    sp.dma_start(w_in[:, :, REP * HD:REP * HD + HD], wk_d[:, :, bass.ds(g, 1), :]).then_inc(S["qkv_in"], 16)
                    sp.dma_start(w_in[:, :, REP * HD + HD:], wv_d[:, :, bass.ds(g, 1), :]).then_inc(S["qkv_in"], 16)
                    sp.dma_start(wo_in[:], wo_d[:, bass.ds(g, 1), :, :]).then_inc(S["wo_in"], 16)
                load(0)
                with sp.Fori(1, KVH) as g:
                    sp.wait_ge(S["w_split"], 2 * (f * KVH + g))
                    sp.wait_ge(S["wo_split"], 2 * (f * KVH + g))
                    load(g)

            def load_expert(e):
                sp.dma_start(w1[:, e], a["L0_ffn_w1"][e].rearrange("(c p) n -> p c n", p=P)).then_inc(S["experts_in"], 16)
                sp.dma_start(w3[:, e], a["L0_ffn_w3"][e].rearrange("(c p) n -> p c n", p=P)).then_inc(S["experts_in"], 16)
                sp.dma_start(w2[:, e], a["L0_ffn_w2"][e].rearrange("(c p) n -> p c n", p=P)).then_inc(S["experts_in"], 16)

            def load_xs(f, k, par, n):
                sp.dma_start(xs[:, par, :], xs_tiles[:, bass.ds(2 * k + par, 1), :]).then_inc(xs_in[par], 16)

            def store_ys(f, k, par):
                sp.wait_ge(S["ys_ready"], NS * f + 2 * k + par + 1)
                sp.dma_start(ys_tiles[:, bass.ds(2 * k + par, 1), :], ys[:, par, :]).then_inc(ys_out[par], 16)

            def moe(f):
                sp.wait_ge(S["out_ps"], 2 * NT * KVH * (f + 1))
                for e in range(RES, E):
                    load_expert(e)
                sp.dma_start(x, x_dram if f == 0 else xsave).then_inc(S["x_back"], 16)
                if f == 0:
                    for tile, src in ((Wv, "L0_attn_Wv"), (Wr, "L0_attn_Wr"), (Wo, "L0_attn_Wo"),
                                      (Wck, "L0_attn_Wck"), (Wcv, "L0_attn_Wcv"), (Wcr, "L0_attn_Wcr")):
                        sp.dma_start(tile[:], chunks(src)).then_inc(S["rwkv_in"], 16)
                    for n, name in enumerate(("ln1_g", "ln1_b", "ln2_g", "ln2_b", "bo")):
                        sp.dma_start(rows[:, n, :], a["L0_attn_" + name].rearrange("(a d) -> a d", a=1)
                                     .broadcast_to([P, D])).then_inc(S["rwkv_in"], 16)
                sp.wait_ge(S["scattered"], 16 * 16 * (f + 1))
                for par in range(2):
                    load_xs(f, 0, par, 0)
                with sp.Fori(0, (NS - 3) // 2) as k:
                    for par in range(2):
                        sp.wait_ge(S["xs_turned"], NS * f + 2 * k + par + 1)
                        load_xs(f, k + 1, par, 0)
                        store_ys(f, k, par)
                k = (NS - 3) // 2
                sp.wait_ge(S["xs_turned"], NS * f + 2 * k + 1)
                load_xs(f, k + 1, 0, 0)
                store_ys(f, k, 0)
                store_ys(f, k, 1)
                store_ys(f, k + 1, 0)

            for e in range(RES):
                load_expert(e)
            attention_weights(0)
            moe(0)
            sp.wait_ge(S["turned"], 3 * NT)
            sp.dma_start(leftv, a["c_left"]).then_inc(S["left_in"], 16)
            sp.wait_ge(S["x_final"], 1)
            sp.dma_start(xsave, x).then_inc(S["saved"], 16)
            attention_weights(1)
            sp.wait_ge(S["saved"], 16)
            moe(1)
            sp.wait_ge(S["x_final"], 2)
            sp.dma_start(out_dram, x).then_inc(S["stored"], 16)
            sp.wait_ge(S["stored"], 16)
            for par in range(2):
                sp.wait_ge(ys_out[par], 16 * 2 * PAR[par])

        @block.gpsimd
        def _(pool):
            pool.memset(back, 0.0).then_inc(S["zeros_set"], 1)
            pool.wait_ge(S["zeros_set"], 1)
            pool.dma_start(xs_tiles[:, 0:16, :], zeros).then_inc(S["zeros_out"], 16)
            pool.dma_start(xs_tiles[:, 16:NS, :], zeros[:, 0:NS - 16, :]).then_inc(S["zeros_out"], 16)
            pool.wait_ge(S["consts_ready"], 1)

            def split(g_n, dst, src, arrived, need, signal):
                pool.wait_ge(S[arrived], need * (g_n + 1))
                one = ones[:, 0:1].rearrange("p (a b) -> p a b", a=1).broadcast_to([P, src.shape[1], src.shape[2]])
                pool.tensor_tensor(dst[:, 0], src, one, ALU.mult).then_inc(S[signal], 1)
                pool.wait_ge(S[signal], 2 * g_n + 1)
                pool.tensor_tensor(dst[:, 1], src, dst[:, 0].bitcast(F32), ALU.subtract).then_inc(S[signal], 1)

            def group(f, g, order):
                grp = Group(f, g, order)
                for what, i, k in order["Pool"]:
                    if what == "w_split":
                        pool.wait_ge(S["projected_qk"], grp.qk_n(("q1", REP - 1)) + 1)
                        split(grp.gg + 1, w_qkv, w_in[:], "qkv_in", 48, "w_split")
                        continue
                    _, half, dst = qk_place(i, k)
                    n, b = grp.qk_n((i, k)), grp.qk[i, k] % 2
                    pool.wait_ge(S["cross_ready"], n + 1)
                    pool.tensor_tensor(crossed[:, b], crossed[:, b], rope[:, 1, half * HALF:(half + 1) * HALF], ALU.mult
                                       ).then_inc(S["rotated"], 1)
                    pool.wait_ge(S["rotated"], 3 * n + 1)
                    pool.wait_ge(S["straight_ready"], n + 1)
                    pool.tensor_tensor(dst[:, 0], straight[:, b], crossed[:, b], ALU.add).then_inc(S["rotated"], 1)
                    pool.wait_ge(S["rotated"], 3 * n + 2)
                    pool.tensor_tensor(straight[:, b], straight[:, b], crossed[:, b], ALU.add).then_inc(S["rotated"], 1)
                    pool.wait_ge(S["rotated"], 3 * n + 3)
                    pool.tensor_tensor(dst[:, 1], straight[:, b], dst[:, 0].bitcast(F32), ALU.subtract).then_inc(S["qk_ready"], 1)
                if order is ORDERS[True]:
                    pool.wait_ge(S["out_ps"], 2 * NT * (grp.gg + 1))
                    split(grp.gg + 1, w_o, wo_in[:], "wo_in", 16, "wo_split")

            def attention(f):
                split(f * KVH, w_qkv, w_in[:], "qkv_in", 48, "w_split")
                split(f * KVH, w_o, wo_in[:], "wo_in", 16, "wo_split")
                group(f, 0, FIRST)
                with pool.Fori(0, KVH - 1) as g:
                    group(f, g, ORDERS[True])
                group(f, KVH - 1, ORDERS[False])

            def moe(f):
                pool.wait_ge(S["routed"], f + 1)
                if f == 0:
                    pool.wait_ge(S["zeros_out"], 32)
                for t in range(NT):
                    for k in range(TOPK):
                        pool.indirect_dma_start(
                            out=xs_dram, out_offset=bass.IndirectOffsetOnAxis(ap=slot[:, k, t:t + 1], axis=0),
                            in_=y[:, t, :], in_offset=None).then_inc(S["scattered"], 16)
                for par in range(2):
                    pool.wait_ge(ys_out[par], 16 * (f + 1) * PAR[par])
                for t in range(NT):
                    for k in range(TOPK):
                        pool.indirect_dma_start(
                            out=back[:, k, t, :], out_offset=None, in_=ys_dram,
                            in_offset=bass.IndirectOffsetOnAxis(ap=slot[:, k, t:t + 1], axis=0)
                        ).then_inc(gathered[t], 16)

            attention(0)
            moe(0)
            attention(1)
            moe(1)

        @block.scalar
        def _(act):
            n_std = [0]

            def sqrt(k=1):
                n_std[0] += 1
                act.wait_ge(S["var_ready"], n_std[0])
                act.activation(std[:, 0:k, :], var[:, 0:k, :], ACT.Sqrt).then_inc(S["std_ready"], 1)

            def group(f, g, order):
                grp = Group(f, g, order)
                gg = grp.gg
                for what, i, k in order["ACT"]:
                    if what == "crossed":
                        n, b, s = grp.qk_n((i, k)), grp.qk[i, k] % 2, grp.slot(("project", i, k))
                        scale = SCALE if i == "k" else 1.0
                        act.wait_ge(S["projected_qk"], n + 1)
                        if order is not FIRST or grp.qk[i, k] >= 2 or f:
                            act.wait_ge(S["qk_ready"], n - 1)
                        act.activation(crossed[0:64, b, :], ps[64:128, 2 * s, :], ACT.Copy, scale=scale)
                        act.activation(crossed[64:128, b, :], ps[0:64, 2 * s, :], ACT.Copy, scale=scale
                                       ).then_inc(S["cross_ready"], 1)
                    if what == "v_high":
                        s = grp.slot(("project", "v", i))
                        act.wait_ge(S["projected_v"], grp.v0 + i + 1)
                        if order is not FIRST:
                            act.wait_ge(S["pv_done"], NT * (gg + 1))
                        act.activation(values[:, 0, 4 * i:4 * i + 4, :], ps[:, 2 * s, :].rearrange("p (t n) -> p t n", t=4),
                                       ACT.Copy).then_inc(S["v_high"], 1)
                    if what == "exp":
                        n, w, slot_n = softmax_n(gg, i, k), (i + 1) * P, grp.slot(("scores", i, k))
                        m, r = (i % 2) * REP + k, (i % 3) * REP + k
                        act.wait_ge(S["max_ready"], n + 1)
                        act.activation(probs[:, i % 2, k, 0:w],
                                       ps[:, 2 * slot_n:2 * slot_n + 2, :].rearrange("p b n -> p (b n)")[:, 0:w], ACT.Exp,
                                       bias=negmax[:, m:m + 1], accum_out=rowsum[:, r:r + 1]).then_inc(S["exp_done"], 1)
                    if what == "high":
                        m = turns_before(i) + k
                        act.wait_ge(S["turn_done"], TURNS * gg + m + 1)
                        act.activation(probsT[:, m % 3, 0, :], ps[:, 4 + m % 2, :], ACT.Copy).then_inc(S["probsT_high"], 1)
                    if what == "attn_high":
                        act.wait_ge(S["pv_done"], NT * gg + i + 1)
                        act.activation(attnT[:, i % 2, 0, :], ps[:, 6 + i % 2, :], ACT.Copy).then_inc(S["attnT_high"], 1)

            def attention(f):
                for t in range(NT):
                    act.wait_ge(S["turned"], NT * TURN_OF[f] + t + 1)
                    for c in range(DC):
                        last = act.activation(tokT[:, 0, c, t * P:(t + 1) * P], ps[:, 4 + t % 2, c * P:(c + 1) * P],
                                              ACT.Copy, scale=cols[:, c, N1:N1 + 1])
                    last.then_inc(S["tokT_high"], 1)
                if f == 0:
                    act.wait_ge(S["zeros_out"], 32)
                group(f, 0, FIRST)
                with act.Fori(0, KVH - 1) as g:
                    group(f, g, ORDERS[True])
                group(f, KVH - 1, ORDERS[False])

            def expert_tile(f, tau, par, turn, silu):
                n = NS * f + tau
                if turn:
                    act.wait_ge(S["hid_turned"], n)
                    act.activation(hidT[:, 1 - par].rearrange("p c n -> p (c n)"), ps[:, 6, :], ACT.Copy
                                   ).then_inc(S["hidT_ready"], 1)
                if silu:
                    act.wait_ge(S["up_done"], n + 1)
                    act.activation(gated[:, par, :], ps[:, 2 * par, :], ACT.Silu).then_inc(S["silu_done"], 1)

            def moe(f):
                sqrt()
                act.wait_ge(S["gap_ready"], f + 1)
                act.activation(key[:], key[:], ACT.Exp).then_inc(S["gap_exp"], 1)
                expert_tile(f, 0, 0, False, True)
                with act.Fori(0, (NS - 3) // 2) as k:
                    expert_tile(f, 2 * k + 1, 1, True, True)
                    expert_tile(f, 2 * k + 2, 0, True, True)
                expert_tile(f, NS - 2, 1, True, True)
                expert_tile(f, NS - 1, 0, True, True)
                expert_tile(f, NS, 1, True, False)

            def rwkv():
                sqrt(2)
                sqrt()
                act.wait_ge(S["left_in"], 16)
                for n in range(4):
                    hc, th = divmod(n, 2)
                    if n:
                        act.wait_ge(S["decay_used"], n)
                    act.activation(decay[:], leftv[:, th * HALF:(th + 1) * HALF], ACT.Exp,
                                   scale=cols[:, hc, TD:TD + 1]).then_inc(S["decay_done"], 1)
                for n in range(NT // 2):
                    act.wait_ge(S["r_done"], n + 1)
                    if n >= 2:
                        act.wait_ge(S["r_used"], n - 1)
                    act.activation(rg[:, n % 2, :], ps[:, 4 + n % 2, :], ACT.Sigmoid).then_inc(S["r_ready"], 1)
                sqrt()
                sqrt()
                for th in range(2):
                    for ic in range(IC):
                        n = th * IC + ic
                        act.wait_ge(S["ck_done"], n + 1)
                        act.activation(kT[:, ic, :], ps[:, n % 4, :], ACT.Relu).then_inc(S["ck_relu"], 1)
                    for t in range(4):
                        n = th * 4 + t
                        act.wait_ge(S["cv_done"], n + 1)
                        if n >= 2:
                            act.wait_ge(S["cv_used"], n - 1)
                        act.activation(rg[:, n % 2, 0:D], ps[:, 4 + n % 2, D:2 * D], ACT.Sigmoid).then_inc(S["cv_sig"], 1)

            sqrt(2)
            attention(0)
            moe(0)
            rwkv()
            sqrt(2)
            attention(1)
            moe(1)

        @block.vector
        def _(dve):
            steps = [0]

            def link(ins):
                steps[0] += 1
                ins.then_inc(S["dve_step"], 1)
                dve.wait_ge(S["dve_step"], steps[0])

            n_std = [0]
            n_turn = [0]

            def rstds(k=1):
                n_std[0] += 1
                dve.wait_ge(S["std_ready"], n_std[0])
                link(dve.reciprocal(rstd[:, 0:k, :], std[:, 0:k, :]))

            def moments(src):
                for t in range(NT):
                    last = dve.bn_stats(stats[:, t, :], src[:, t, :])
                link(last)
                for t in range(NT):
                    last = dve.bn_aggr(meanvar[:, t, :], stats[:, t, :])
                link(last)

            def normalise(dst, src, row=0, signal=False):
                for t in range(NT):
                    last = dve.tensor_scalar(dst[:, t, :], src[:, t, :], meanvar[:, t, 0:1], rstd[:, row, t:t + 1],
                                             ALU.subtract, ALU.mult)
                    if signal:
                        last.then_inc(S["y_ready"], 1)
                if not signal:
                    link(last)

            def scale_rows(dst, src, row, signal):
                for t in range(NT):
                    last = dve.tensor_scalar(dst[:, t, :], src[:, t, :], rstd[:, row, t:t + 1], None, ALU.mult)
                    if signal:
                        last.then_inc(S["y_ready"], 1)
                if not signal:
                    link(last)

            def two_norms(eps1, eps2):
                link(dve.tensor_scalar(var[:, 0, :], meanvar[:, :, 1], eps1, None, ALU.add))
                link(dve.reciprocal(std[:, 0, :], var[:, 0, :]))
                link(dve.tensor_tensor(var[:, 1, :], meanvar[:, :, 1], std[:, 0, :], ALU.mult))
                dve.tensor_scalar(var[:, 1, :], var[:, 1, :], eps2, None, ALU.add).then_inc(S["var_ready"], 1)
                rstds(2)

            def one_norm(eps):
                dve.tensor_scalar(var[:, 0, :], meanvar[:, :, 1], eps, None, ALU.add).then_inc(S["var_ready"], 1)
                rstds()

            def take_turned(gain, bias=None):
                u0 = NT * n_turn[0]
                n_turn[0] += 1
                for t in range(NT):
                    dve.wait_ge(S["turned"], u0 + t + 1)
                    src = ps[:, 4 + t % 2, 0:D].rearrange("p (c n) -> p c n", c=DC)
                    for c in range(DC):
                        dst = xT[:, c, 1 + t * P:1 + (t + 1) * P]
                        g = cols[:, c, gain:gain + 1]
                        if bias is None:
                            last = dve.tensor_scalar(dst, src[:, c, :], g, None, ALU.mult)
                        else:
                            last = dve.tensor_scalar(dst, src[:, c, :], g, cols[:, c, bias:bias + 1], ALU.mult, ALU.add)
                    last.then_inc(S["xT_ready"], 1)

            dve.memset(ones[:], 1.0)
            dve.wait_ge(S["consts_in"], 16 * 4)
            dve.tensor_copy(square16[:], square[:, 0:2, :]).then_inc(S["consts_ready"], 1)
            dve.wait_ge(S["cols_in"], 16 * 8)
            dve.wait_ge(S["x_in"], 16)

            def attention(f):
                moments(x)
                two_norms(EPS, EPS)
                normalise(h, x)
                scale_rows(y, h, 1, True)
                u0 = NT * n_turn[0]
                n_turn[0] += 1
                for t in range(NT):
                    dve.wait_ge(S["tokT_high"], NT * f + t + 1)
                    for c in range(DC):
                        place = slice(t * P, (t + 1) * P)
                        last = dve.scalar_tensor_tensor(
                            out=tokT[:, 1, c, place], in0=ps[:, 4 + t % 2, c * P:(c + 1) * P], scalar=cols[:, c, N1:N1 + 1],
                            in1=tokT[:, 0, c, place].bitcast(F32), op0=ALU.mult, op1=ALU.subtract)
                    last.then_inc(S["xT_ready"], 1)
                group(f, 0, FIRST)
                with dve.Fori(0, KVH - 1) as g:
                    group(f, g, ORDERS[True])
                group(f, KVH - 1, ORDERS[False])
                dve.wait_ge(S["out_added"], REP * NT * KVH * (f + 1))

            def group(f, g, order):
                grp = Group(f, g, order)
                gg = grp.gg
                for what, i, k in order["DVE"]:
                    if what == "straight":
                        n, b, s = grp.qk_n((i, k)), grp.qk[i, k] % 2, grp.slot(("project", i, k))
                        _, half, _ = qk_place(i, k)
                        dve.wait_ge(S["cross_ready"], n + 1)
                        dve.scalar_tensor_tensor(out=straight[:, b, :], in0=ps[:, 2 * s, :],
                                                 scalar=SCALE if i == "k" else 1.0,
                                                 in1=rope[:, 0, half * HALF:(half + 1) * HALF],
                                                 op0=ALU.mult, op1=ALU.mult).then_inc(S["straight_ready"], 1)
                    if what == "v_low":
                        s = grp.slot(("project", "v", i))
                        dve.wait_ge(S["v_high"], grp.v0 + i + 1)
                        part = values[:, :, 4 * i:4 * i + 4, :]
                        dve.tensor_tensor(part[:, 1], ps[:, 2 * s, :].rearrange("p (t n) -> p t n", t=4),
                                          part[:, 0].bitcast(F32), ALU.subtract).then_inc(S["v_low"], 1)
                    if what == "max":
                        s, w, m = 2 * grp.slot(("scores", i, k)), (i + 1) * P, (i % 2) * REP + k
                        dve.wait_ge(S["scores_ready"], softmax_n(gg, i, k) + 1)
                        dve.tensor_reduce(negmax[:, m:m + 1], ps[:, s:s + 2, :].rearrange("p b n -> p (b n)")[:, 0:w],
                                          AX.X, ALU.max, negate=True).then_inc(S["max_ready"], 1)
                    if what == "low":
                        m = turns_before(i) + k
                        dve.wait_ge(S["probsT_high"], TURNS * gg + m + 1)
                        dve.tensor_tensor(probsT[:, m % 3, 1, :], ps[:, 4 + m % 2, :], probsT[:, m % 3, 0, :].bitcast(F32),
                                          ALU.subtract).then_inc(S["probsT_low"], 1)
                    if what == "attn_low":
                        m = (i % 3) * REP
                        dve.wait_ge(S["attnT_high"], NT * gg + i + 1)
                        dve.tensor_tensor(attnT[:, i % 2, 1, :], ps[:, 6 + i % 2, :], attnT[:, i % 2, 0, :].bitcast(F32),
                                          ALU.subtract).then_inc(S["attnT_low"], 1)
                        dve.reciprocal(rowinv[:, m:m + REP], rowsum[:, m:m + REP]).then_inc(S["rowinv_ready"], 1)
                    if what == "added":
                        m = (i % 3) * REP
                        dve.wait_ge(S["rowinv_ready"], NT * gg + i + 1)
                        dve.wait_ge(S["out_ps"], 2 * (NT * gg + i) + k + 1)
                        for hd in (2 * k, 2 * k + 1):
                            if hd:
                                dve.wait_ge(S["out_added"], REP * (NT * gg + i) + hd)
                            dve.scalar_tensor_tensor(out=h[:, i, :], in0=ps[:, 6 + i % 2, (hd % 2) * D:(hd % 2 + 1) * D],
                                                     scalar=rowinv[:, m + hd:m + hd + 1], in1=h[:, i, :],
                                                     op0=ALU.mult, op1=ALU.add).then_inc(S["out_added"], 1)

            def route(f):
                bc = lambda ap: ap.rearrange("p (t o) -> p t o", o=1).broadcast_to([P, NT, E])
                keys = small[:, C_KEY:C_KEY + E].rearrange("p (o e) -> p o e", o=1).broadcast_to([P, NT, E])
                dve.wait_ge(S["logits_ps"], f + 1)
                link(dve.tensor_copy(logits[:], ps[:, 0, 0:NT * E].rearrange("p (t e) -> p t e", t=NT)))
                for k in range(TOPK):
                    src = logits if k == 0 else work
                    if k == 1:
                        link(dve.scalar_tensor_tensor(out=work[:], in0=pick[:, 0], scalar=-BIG, in1=logits[:],
                                                      op0=ALU.mult, op1=ALU.add))
                    link(dve.tensor_reduce(top[:, k, :], src[:], AX.X, ALU.max))
                    link(dve.tensor_tensor(pick[:, k], src[:], bc(top[:, k, :]), ALU.is_equal))
                    link(dve.tensor_tensor(pick[:, k], pick[:, k], keys, ALU.mult))
                    link(dve.tensor_reduce(key[:], pick[:, k], AX.X, ALU.max))
                    link(dve.tensor_tensor(pick[:, k], pick[:, k], bc(key[:]), ALU.is_equal))
                dve.tensor_tensor(both[:], pick[:, 0], pick[:, 1], ALU.add).then_inc(S["pick_ready"], 1)
                dve.tensor_tensor(key[:], top[:, 1, :], top[:, 0, :], ALU.subtract).then_inc(S["gap_ready"], 1)
                dve.wait_ge(S["gap_exp"], f + 1)
                link(dve.tensor_scalar(wts[:, 1, :], key[:], 1.0, None, ALU.add))
                link(dve.reciprocal(wts[:, 0, :], wts[:, 1, :]))
                link(dve.tensor_tensor(wts[:, 1, :], key[:], wts[:, 0, :], ALU.mult))
                dve.wait_ge(S["routing_ps"], f + 1)
                link(dve.tensor_copy(count[:], ps[:, 1, 128:128 + E]))
                sq = cube[:, 0:E, :]
                link(dve.tensor_tensor(sq, count[:].rearrange("p (e o) -> p e o", o=1).broadcast_to([P, E, E]),
                                       small[:, C_THR:C_THR + E * E].rearrange("p (e k) -> p e k", e=E), ALU.is_gt))
                link(dve.tensor_reduce(tiles[:], sq, AX.X, ALU.add))
                link(dve.tensor_tensor(sq, tiles[:].rearrange("p (o e) -> p o e", o=1).broadcast_to([P, E, E]),
                                       small[:, C_BEFORE:C_BEFORE + E * E].rearrange("p (e k) -> p e k", e=E), ALU.mult))
                link(dve.tensor_reduce(first[:], sq, AX.X, ALU.add))
                link(dve.tensor_scalar(count[:], first[:], float(P), None, ALU.mult))
                link(dve.tensor_tensor(work[:], ps[:, 1, 0:NT * E].rearrange("p (t e) -> p t e", t=NT),
                                       count[:].rearrange("p (o e) -> p o e", o=1).broadcast_to([P, NT, E]), ALU.add))
                for k in range(TOPK):
                    link(dve.tensor_tensor(pick[:, k], pick[:, k], work[:], ALU.mult))
                    link(dve.tensor_reduce(slotf[:, k, :], pick[:, k], AX.X, ALU.add))
                dve.tensor_copy(slot[:], slotf[:]).then_inc(S["routed"], 1)
                link(dve.tensor_tensor(tiles[:], tiles[:], first[:], ALU.add))
                link(dve.tensor_tensor(cube[:], small[:, C_SLOT:].rearrange("p (n e) -> p n e", n=NS),
                                       tiles[:].rearrange("p (o e) -> p o e", o=1).broadcast_to([P, NS, E]), ALU.is_ge))
                link(dve.tensor_reduce(ownerf[:], cube[:], AX.X, ALU.add))
                dve.tensor_scalar(owner[:], ownerf[:], float(E - 1), None, ALU.min).then_inc(S["owner_ready"], 1)

            def take_xs(f, tau, par):
                n = NS * f + tau
                dve.wait_ge(S["xs_turned"], n + 1)
                for c in range(DC):
                    last = dve.tensor_scalar(xsT[:, par, c, :], ps[:, 4 + par, c * P:(c + 1) * P],
                                             cols[:, c, N2:N2 + 1], None, ALU.mult)
                last.then_inc(S["xsT_ready"], 1)

            def take_hid(f, tau, par):
                dve.wait_ge(S["silu_done"], NS * f + tau + 1)
                dve.tensor_tensor(hid[:, par, :], gated[:, par, :], ps[:, 2 * par + 1, :], ALU.mult).then_inc(S["hid_ready"], 1)

            def take_ys(f, tau, par, k):
                dve.wait_ge(S["down_done"], NS * f + tau + 1)
                if not (isinstance(k, int) and PAR[par] * f + k == 0):
                    dve.wait_ge(ys_out[par], 16 * (PAR[par] * f + k))
                dve.tensor_copy(ys[:, par, :], ps[:, 7, 0:D]).then_inc(S["ys_ready"], 1)

            def moe(f):
                dve.memset(xT[:, :, 0:1], 0.0).then_inc(S["xT_clear"], 1)
                for t in range(NT):
                    last = dve.scalar_tensor_tensor(out=y[:, t, :], in0=h[:, t, :], scalar=1.0 / D, in1=h[:, t, :],
                                                    op0=ALU.mult, op1=ALU.mult, accum_out=var[:, 1, t:t + 1])
                link(last)
                dve.tensor_scalar(var[:, 0, :], var[:, 1, :], EPS, None, ALU.add).then_inc(S["var_ready"], 1)
                rstds()
                scale_rows(y, h, 0, True)
                take_turned(N2)
                route(f)
                take_xs(f, 0, 0)
                take_hid(f, 0, 0)
                take_xs(f, 1, 1)
                take_hid(f, 1, 1)
                take_xs(f, 2, 0)
                take_ys(f, 0, 0, 0)
                take_hid(f, 2, 0)
                take_xs(f, 3, 1)
                take_ys(f, 1, 1, 0)
                with dve.Fori(1, (NS - 3) // 2) as k:
                    take_hid(f, 2 * k + 1, 1)
                    take_xs(f, 2 * k + 2, 0)
                    take_ys(f, 2 * k, 0, k)
                    take_hid(f, 2 * k + 2, 0)
                    take_xs(f, 2 * k + 3, 1)
                    take_ys(f, 2 * k + 1, 1, k)
                k = (NS - 3) // 2
                take_hid(f, 2 * k + 1, 1)
                take_xs(f, 2 * k + 2, 0)
                take_ys(f, 2 * k, 0, k)
                take_hid(f, 2 * k + 2, 0)
                take_ys(f, 2 * k + 1, 1, k)
                take_ys(f, 2 * k + 2, 0, k + 1)
                dve.wait_ge(S["x_back"], 16 * (f + 1))
                for t in range(NT):
                    dve.wait_ge(gathered[t], 32 * (f + 1))
                    for k in range(TOPK):
                        link(dve.scalar_tensor_tensor(out=h[:, t, :], in0=back[:, k, t, :], scalar=wts[:, k, t:t + 1],
                                                      in1=h[:, t, :], op0=ALU.mult, op1=ALU.add))
                    last = dve.scalar_tensor_tensor(out=x[:, t, :], in0=h[:, t, :], scalar=0.5, in1=x[:, t, :],
                                                    op0=ALU.mult, op1=ALU.add)
                if f == 0:
                    link(last)
                else:
                    last.then_inc(S["x_final"], 1)

            def gain_rows(dst, k):
                for j, op in ((0, ALU.mult), (1, ALU.add)):
                    row = rows[:, k + j, :].rearrange("p (o d) -> p o d", o=1).broadcast_to([P, NT, D])
                    link(dve.tensor_tensor(dst, dst, row, op))

            def rwkv():
                dve.wait_ge(S["rwkv_in"], 16 * 11)
                moments(x)
                two_norms(EPS, EPS_RWKV)
                normalise(h, x)
                scale_rows(y, h, 1, False)
                gain_rows(y, 0)
                moments(y)
                one_norm(EPS_RWKV)
                normalise(y, y, signal=True)
                take_turned(TMG, TMB)
                link(dve.tensor_scalar(vmix[:], cols[:, :, TF], -1.0, 1.0, ALU.mult, ALU.add))
                for c in range(DC):
                    link(dve.tensor_scalar(mixT[:, c, :], xT[:, c, 0:T], vmix[:, c:c + 1], None, ALU.mult))
                    dve.scalar_tensor_tensor(out=mixT[:, c, :], in0=xT[:, c, 1:1 + T], scalar=cols[:, c, TF:TF + 1],
                                             in1=mixT[:, c, :], op0=ALU.mult, op1=ALU.add).then_inc(S["mix_ready"], 1)
                for n in range(4):
                    dve.wait_ge(S["v_done"], n + 1)
                    dve.wait_ge(S["decay_done"], n + 1)
                    dve.tensor_tensor_reduce(out=decay[:], in0=ps[:, n, :], in1=decay[:], scale=1.0, scalar=0.0,
                                             op0=ALU.mult, op1=ALU.add, accum_out=vsum[:, n:n + 1]).then_inc(S["decay_used"], 1)
                dve.wait_ge(S["decay_used"], 4)
                dve.wait_ge(S["mix_ready"], 2)
                link(dve.tensor_reduce(vmix[:], vsum[:].rearrange("p (c k) -> p c k", c=2), AX.X, ALU.add))
                for c in range(DC):
                    dve.tensor_scalar(vwide[:, c, :], ones[:], vmix[:, c:c + 1], None, ALU.mult).then_inc(S["vw_ready"], 1)
                dve.wait_ge(S["u_done"], 1)
                link(dve.tensor_tensor(u[:], ps[:, 0, 0:D], rows[:, 4, :], ALU.add))
                wide = u[:].rearrange("p (o d) -> p o d", o=1).broadcast_to([P, 2, D])
                for n in range(NT // 2):
                    dve.wait_ge(S["r_ready"], n + 1)
                    r2 = rg[:, n % 2, :].rearrange("p (k d) -> p k d", k=2)
                    link(dve.tensor_tensor(r2, r2, wide, ALU.mult))
                    last = dve.tensor_tensor(h[:, 2 * n:2 * n + 2, :], h[:, 2 * n:2 * n + 2, :], r2, ALU.add)
                    last.then_inc(S["r_used"], 1)
                dve.wait_ge(S["r_used"], NT // 2)
                moments(h)
                one_norm(EPS_RWKV)
                normalise(y, h)
                gain_rows(y, 2)
                moments(y)
                one_norm(EPS_RWKV)
                normalise(y, y, signal=True)
                take_turned(CMG, CMB)
                for th in range(2):
                    for ic in range(IC):
                        n = th * IC + ic
                        dve.wait_ge(S["ck_relu"], n + 1)
                        dve.tensor_tensor(kT[:, ic, :], kT[:, ic, :], kT[:, ic, :], ALU.mult).then_inc(S["ck_sq"], 1)
                    for t in range(4):
                        n = th * 4 + t
                        dve.wait_ge(S["cv_sig"], n + 1)
                        link(dve.tensor_tensor(rg[:, n % 2, D:2 * D], rg[:, n % 2, 0:D], ps[:, 4 + n % 2, 0:D], ALU.mult))
                        link(dve.tensor_tensor(h[:, n, :], h[:, n, :], rg[:, n % 2, D:2 * D], ALU.add))
                        dve.tensor_tensor(x[:, n, :], x[:, n, :], h[:, n, :], ALU.add).then_inc(S["cv_used"], 1)
                dve.wait_ge(S["cv_used"], NT)
                dve.sem_inc(S["x_final"], 1)

            attention(0)
            moe(0)
            rwkv()
            attention(1)
            moe(1)

        @block.tensor
        def _(pe):
            n_turn = [0]

            pe.wait_ge(S["consts_ready"], 1)

            def turn_tokens():
                u0 = NT * n_turn[0]
                n_turn[0] += 1
                for t in range(NT):
                    pe.wait_ge(S["y_ready"], u0 + t + 1)
                    if t >= 2:
                        pe.wait_ge(S["xT_ready"], u0 + t - 1)
                    for c in range(DC):
                        last = pe.transpose(ps[:, 4 + t % 2, c * P:(c + 1) * P], y[:, t, c * P:(c + 1) * P], ident)
                    last.then_inc(S["turned"], 1)

            def tokens(c, t):
                return xT[:, c, 1 + t * P:1 + (t + 1) * P]

            def attention(f):
                turn_tokens()
                pe.wait_ge(S["xT_ready"], NT * n_turn[0])
                group(f, 0, FIRST)
                with pe.Fori(0, KVH - 1) as g:
                    group(f, g, ORDERS[True])
                group(f, KVH - 1, ORDERS[False])

            def products(dst, lhsT, rhs, start, stop):
                pe.matmul(dst, lhsT[0], rhs[0], start=start, stop=False)
                pe.matmul(dst, lhsT[1], rhs[0], start=False, stop=False)
                return pe.matmul(dst, lhsT[0], rhs[1], start=False, stop=stop)

            def parts(tensor, *index):
                return [tensor[(slice(None), part) + index] for part in range(2)]

            def group(f, g, order):
                grp = Group(f, g, order)
                gg = grp.gg
                every = slice(None)
                for step in order["PE"]:
                    what, i, k = step
                    if what in ("scores", "project"):
                        s, user = grp.slot(step), grp.users[step][2]
                        if user is None:
                            if order is not FIRST:
                                pe.wait_ge(S["v_low"], 2 * (gg + 1))
                        elif user[0] == "scores":
                            pe.wait_ge(S["exp_done"], softmax_n(gg, user[1], user[2]) + 1)
                        elif user[1] == "v":
                            pe.wait_ge(S["v_low"], grp.v0 + user[2] + 1)
                        else:
                            pe.wait_ge(S["straight_ready"], grp.qk_n(user[1:]) + 1)
                    if what == "project" and i == "v":
                        if k == 0:
                            pe.wait_ge(S["w_split"], 2 * (gg + (2 if order is not FIRST else 1)))
                        for t in range(4 * k, 4 * k + 4):
                            dst = ps[:, 2 * s, (t % 4) * HD:(t % 4 + 1) * HD]
                            for c in range(DC):
                                last = products(dst, parts(tokT, c, slice(t * P, (t + 1) * P)),
                                                parts(w_qkv, c, slice(REP * HD + HD, None)), c == 0, c == DC - 1)
                        last.then_inc(S["projected_v"], 1)
                    elif what == "project":
                        pe.wait_ge(S["w_split"], 2 * (gg + (1 if i == "q1" or order is FIRST else 2)))
                        col, half, _ = qk_place(i, k)
                        for c in range(DC):
                            last = products(ps[:, 2 * s, :], parts(w_qkv, c, slice(col, col + HD)),
                                            parts(tokT, c, slice(half * HALF, (half + 1) * HALF)), c == 0, c == DC - 1)
                        last.then_inc(S["projected_qk"], 1)
                    if what == "scores":
                        if (i, k) == (0, 0):
                            pe.wait_ge(S["qk_ready"], 10 * gg + 5)
                        if i == 4:
                            pe.wait_ge(S["qk_ready"], 10 * gg + 6 + k + 1)
                        w = (i + 1) * P
                        q = parts(queriesT, k, slice(i * P, (i + 1) * P))
                        for b in range(i // 4 + 1):
                            n1 = min(512, w - 512 * b)
                            last = products(ps[:, 2 * s + b, 0:n1], q, parts(keysT, slice(512 * b, 512 * b + n1)),
                                            True, b < i // 4)
                        last = pe.matmul(ps[:, 2 * s + i // 4, (i % 4) * P:(i % 4 + 1) * P], square16[:, 0, :], square16[:, 1, :],
                                         start=False, stop=True)
                        last.then_inc(S["scores_ready"], 1)
                    if what == "turn":
                        m = turns_before(i) + k
                        if k == 0:
                            pe.wait_ge(S["exp_done"], softmax_n(gg, i, REP))
                        if m >= 2:
                            pe.wait_ge(S["probsT_low"], TURNS * gg + m - 1)
                        for hd in range(REP):
                            last = pe.transpose(ps[:, 4 + m % 2, hd * P:(hd + 1) * P],
                                                probs[:, i % 2, hd, k * P:(k + 1) * P], ident)
                        last.then_inc(S["turn_done"], 1)
                    if what == "values":
                        m = turns_before(i) + k
                        pe.wait_ge(S["probsT_low"], TURNS * gg + m + 1)
                        if k == 0:
                            if i >= 2:
                                pe.wait_ge(S["out_added"], REP * (NT * gg + i - 1))
                        last = products(ps[:, 6 + i % 2, :], parts(values, k, every), [probsT[:, m % 3, 0], probsT[:, m % 3, 1]],
                                        k == 0, k == i)
                        if k == i:
                            last.then_inc(S["pv_done"], 1)
                    if what == "out":
                        if k == 0:
                            if i == 0:
                                pe.wait_ge(S["wo_split"], 2 * (gg + 1))
                            pe.wait_ge(S["attnT_low"], NT * gg + i + 1)
                        else:
                            pe.wait_ge(S["out_added"], REP * (NT * gg + i) + 2)
                        for hd in (2 * k, 2 * k + 1):
                            last = products(ps[:, 6 + i % 2, (hd % 2) * D:(hd % 2 + 1) * D],
                                            [attnT[:, i % 2, part, hd * P:(hd + 1) * P] for part in range(2)],
                                            parts(w_o, hd, every), True, True)
                        last.then_inc(S["out_ps"], 1)

            def expert(tau):
                return pe.value_load(owner[0:1, bass.ds(tau, 1)], min_val=0, max_val=E - 1)

            def turn_xs(f, tau, par, k):
                pe.wait_ge(xs_in[par], 16 * (PAR[par] * f + k + 1))
                for c in range(DC):
                    last = pe.transpose(ps[:, 4 + par, c * P:(c + 1) * P], xs[:, par, c * P:(c + 1) * P], ident)
                last.then_inc(S["xs_turned"], 1)

            def up(f, tau, par):
                e = expert(tau)
                pe.wait_ge(S["xsT_ready"], NS * f + tau + 1)
                for w, b in ((w1, 2 * par), (w3, 2 * par + 1)):
                    for c in range(DC):
                        last = pe.matmul(ps[:, b, :], xsT[:, par, c, :], w[:, bass.ds(e, 1), c, :],
                                         start=(c == 0), stop=(c == DC - 1))
                last.then_inc(S["up_done"], 1)

            def turn_hid(f, tau, par):
                pe.wait_ge(S["hid_ready"], NS * f + tau + 1)
                for c in range(FC):
                    last = pe.transpose(ps[:, 6, c * P:(c + 1) * P], hid[:, par, c * P:(c + 1) * P], ident)
                last.then_inc(S["hid_turned"], 1)

            def down(f, tau, par):
                e = expert(tau)
                pe.wait_ge(S["hidT_ready"], NS * f + tau + 1)
                if not (isinstance(tau, int) and NS * f + tau == 0):
                    pe.wait_ge(S["ys_ready"], NS * f + tau)
                for c in range(FC):
                    last = pe.matmul(ps[:, 7, 0:D], hidT[:, par, c, :], w2[:, bass.ds(e, 1), c, :],
                                     start=(c == 0), stop=(c == FC - 1))
                last.then_inc(S["down_done"], 1)

            def moe(f):
                turn_tokens()
                pe.wait_ge(S["xT_ready"], NT * n_turn[0])
                for t in range(NT):
                    for c in range(DC):
                        last = pe.matmul(ps[:, 0, t * E:(t + 1) * E], tokens(c, t), gate[:, c, :],
                                         start=(c == 0), stop=(c == DC - 1))
                last.then_inc(S["logits_ps"], 1)
                pe.wait_ge(S["pick_ready"], f + 1)
                pe.matmul(ps[:, 1, 0:NT * E], upper, both[:].rearrange("p t e -> p (t e)"), start=True, stop=False)
                for s in range(1, NT):
                    pe.matmul(ps[:, 1, s * E:NT * E], ones[:], both[:, 0:NT - s, :].rearrange("p t e -> p (t e)"),
                              start=False, stop=(s == NT - 1))
                for t in range(NT):
                    last = pe.matmul(ps[:, 1, 128:128 + E], ones[:], both[:, t, :], start=(t == 0), stop=(t == NT - 1))
                last.then_inc(S["routing_ps"], 1)
                pe.wait_ge(S["owner_ready"], f + 1)
                pe.wait_ge(S["experts_in"], 16 * 3 * (RES + (E - RES) * (f + 1)))
                turn_xs(f, 0, 0, 0)
                up(f, 0, 0)
                turn_xs(f, 1, 1, 0)

                def step(tau, par, k, more=True):
                    turn_hid(f, tau - 1, 1 - par)
                    up(f, tau, par)
                    if more:
                        turn_xs(f, tau + 1, 1 - par, k)
                    down(f, tau - 1, 1 - par)

                with pe.Fori(0, (NS - 3) // 2) as k:
                    step(2 * k + 1, 1, k + 1)
                    step(2 * k + 2, 0, k + 1)
                k = (NS - 3) // 2
                step(NS - 2, 1, k + 1)
                step(NS - 1, 0, k + 1, more=False)
                turn_hid(f, NS - 1, 0)
                down(f, NS - 1, 0)

            def rwkv():
                turn_tokens()
                pe.wait_ge(S["xT_ready"], NT * n_turn[0])
                for n in range(4):
                    hc, th = divmod(n, 2)
                    for c in range(DC):
                        last = pe.matmul(ps[:, n, :], Wv[:, c, hc * P:(hc + 1) * P], xT[:, c, 1 + th * HALF:1 + (th + 1) * HALF],
                                         start=(c == 0), stop=(c == DC - 1))
                    last.then_inc(S["v_done"], 1)
                pe.wait_ge(S["mix_ready"], 2)
                for n in range(NT // 2):
                    if n >= 2:
                        pe.wait_ge(S["r_ready"], n - 1)
                    for k in range(2):
                        t = 2 * n + k
                        for c in range(DC):
                            last = pe.matmul(ps[:, 4 + n % 2, k * D:(k + 1) * D], mixT[:, c, t * P:(t + 1) * P], Wr[:, c, :],
                                             start=(c == 0), stop=(c == DC - 1))
                    last.then_inc(S["r_done"], 1)
                    if n == 1:
                        pe.wait_ge(S["vw_ready"], 2)
                        for c in range(DC):
                            last = pe.matmul(ps[:, 0, 0:D], vwide[:, c, :], Wo[:, c, :], start=(c == 0), stop=(c == DC - 1))
                        last.then_inc(S["u_done"], 1)
                turn_tokens()
                pe.wait_ge(S["xT_ready"], NT * n_turn[0])
                for th in range(2):
                    for ic in range(IC):
                        n = th * IC + ic
                        if n >= 4:
                            pe.wait_ge(S["ck_relu"], n - 3)
                        for c in range(DC):
                            last = pe.matmul(ps[:, n % 4, :], Wck[:, c, ic * P:(ic + 1) * P], xT[:, c, th * HALF:(th + 1) * HALF],
                                             start=(c == 0), stop=(c == DC - 1))
                        last.then_inc(S["ck_done"], 1)
                    pe.wait_ge(S["ck_sq"], IC * (th + 1))
                    for t in range(4):
                        n = th * 4 + t
                        if n >= 2:
                            pe.wait_ge(S["cv_used"], n - 1)
                        for c in range(DC):
                            pe.matmul(ps[:, 4 + n % 2, D:2 * D], tokens(c, n), Wcr[:, c, :], start=(c == 0), stop=(c == DC - 1))
                        for ic in range(IC):
                            last = pe.matmul(ps[:, 4 + n % 2, 0:D], kT[:, ic, t * P:(t + 1) * P], Wcv[:, ic, :],
                                             start=(ic == 0), stop=(ic == IC - 1))
                        last.then_inc(S["cv_done"], 1)

            attention(0)
            moe(0)
            rwkv()
            attention(1)
            moe(1)


_INS = ["L0_attn_x", "L0_attn_ln1_g", "L0_attn_ln1_b", "L0_attn_ln2_g", "L0_attn_ln2_b", "L0_attn_tm_g",
        "L0_attn_tm_b", "L0_attn_time_decay", "L0_attn_time_first", "L0_attn_Wv", "L0_attn_Wr", "L0_attn_Wo",
        "L0_attn_bo", "L0_attn_cm_g", "L0_attn_cm_b", "L0_attn_Wck", "L0_attn_Wcv", "L0_attn_Wcr",
        "L0_ffn_norm1_w", "L0_ffn_norm2_w", "L0_ffn_wq", "L0_ffn_wk", "L0_ffn_wv", "L0_ffn_wo",
        "L0_ffn_gate_w", "L0_ffn_w1", "L0_ffn_w3", "L0_ffn_w2"]


def kernel(**inputs):
    import concourse.bacc as _bacc
    from concourse.bass_utils import run_bass_kernel_spmd as _run

    nc = _bacc.Bacc("TRN2", target_bir_lowering=False, num_devices=1)
    arrays, args = {}, {}
    given = {name: inputs[name] for name in _INS}
    given.update(constants())
    for name, value in given.items():
        v = np.ascontiguousarray(value)
        arrays[f"in_{name}_dram"] = v
        args[name] = nc.dram_tensor(f"in_{name}_dram", v.shape, mybir.dt.from_np(v.dtype), kind="ExternalInput").ap()
    out = nc.dram_tensor("out_dram", (1, T, D), F32, kind="ExternalOutput").ap()
    scratch = (nc.dram_tensor("xs_dram", (NS * P, D), F32, kind="Internal").ap(),
               nc.dram_tensor("ys_dram", (NS * P, D), F32, kind="Internal").ap(),
               nc.dram_tensor("xsave_dram", (T, D), F32, kind="Internal").ap())
    macaron(nc, args, out, scratch)
    r = _run(nc, [arrays], core_ids=[0])
    return r.results[0]["out_dram"]
```

```python
from contextlib import ExitStack

import numpy as np

import concourse.bass as bass
from concourse import mybir

F32 = mybir.dt.float32
F32R = mybir.dt.float32r
BF16 = mybir.dt.bfloat16
I32 = mybir.dt.int32
U32 = mybir.dt.uint32
ALU = mybir.AluOpType
ACT = mybir.ActivationFunctionType
AX = mybir.AxisListType

P = 128
T, D = 1024, 256
NT, DC = T // P, D // P
HEADS, KVH, HD = 16, 4, 128
REP = HEADS // KVH
E, F = 8, 512
FC = F // P
TOPK = 2
NS = (TOPK * T + E * (P - 1)) // P
RI = 1024
IC = RI // P
HALF = 512
SCALE = float(1.0 / np.sqrt(HD))
EPS, EPS_RWKV = 1e-5, 1e-12
BIG = 1e30
THETA = 1000000.0

RES = 2
TURNS = NT * (NT + 1) // 2
SOFT = NT * REP


def turns_before(i):
    return i * (i + 1) // 2


def group_order(more):
    steps = {}

    def add(engine, step, us, place, *before):
        steps[step] = (engine, us, place + DUE.get(step[0], 0.0), [x for x in before if x in steps])

    blocks = [("q1", k, DUE["q1"] + DUE["q1_each"] * k) for k in range(REP)]
    if more:
        blocks += [("q0", k, DUE["q0"] + DUE["q0_each"] * k) for k in range(REP)] + [("k", 0, 6.9), ("k", 1, 7.1)]
    later = []
    add("Pool", ("wo_split", 0, 0), 4.4, 0)
    for i in range(NT + (EARLY if more else 0)):
        for hd in range(REP if i >= EARLY else 0):
            w = (i % NT + 1) * P
            add("PE", ("scores", i, hd), 0.06 + 3 * w / 2400, i - 0.8 + 0.2 * hd, ("scores", i, hd - 1), ("scores", i - 1, REP - 1),
                ("turn", i - 2, i - 2), ("exp", i - 2, hd))
            add("DVE", ("max", i, hd), 0.17 + w / 960, i - 0.8 + 0.2 * hd, ("scores", i, hd), ("max", i, hd - 1),
                ("max", i - 1, REP - 1), ("attn_low", i - 4, 0))
            add("ACT", ("exp", i, hd), 0.38 + w / 1200, i - 0.8 + 0.2 * hd, ("max", i, hd), ("exp", i, hd - 1),
                ("exp", i - 1, REP - 1))
        if i >= NT:
            continue
        for j in range(i + 1):
            at = i + j / (i + 1)
            m = turns_before(i) + j
            m_of = {turns_before(a) + b: (a, b) for a in range(NT) for b in range(a + 1)}
            bank, ring = m_of.get(m - 2, (-1, -1)), m_of.get(m - 3, (-1, -1))
            last = m_of.get(m - 1, (-1, -1))
            add("PE", ("turn", i, j), 0.43, at, ("exp", i, REP - 1), ("low", *bank), ("values", *ring), ("turn", *last))
            add("ACT", ("high", i, j), 0.52, at, ("turn", i, j), ("high", *last))
            add("DVE", ("low", i, j), 0.62, at, ("high", i, j), ("low", *last))
            add("PE", ("values", i, j), 0.64, at + 1.0 / (i + 1), ("low", i, j), ("values", *last), ("added", i - 2, 1))
        add("ACT", ("attn_high", i, 0), 0.52, i + 1.2, ("values", i, i), ("attn_high", i - 1, 0), ("out", i - 2, 1))
        add("DVE", ("attn_low", i, 0), 0.75, i + 1.2, ("attn_high", i, 0), ("attn_low", i - 1, 0))
        for k in range(2):
            add("PE", ("out", i, k), 0.64, i + 1.3 + 0.2 * k, ("attn_low", i, 0), ("added", i, k - 1), ("out", i - 1, 1),
                ("wo_split", 0, 0))
            add("DVE", ("added", i, k), 0.95 if more or not k else 1.4, i + 1.3 + 0.2 * k, ("out", i, k), ("added", i, k - 1), ("added", i - 1, 1))
    for n, (w, k, at) in enumerate(blocks):
        before = [(what, *blocks[n - 1][:2]) for what in ("project", "crossed", "straight", "rotated")] if n else [None] * 4
        two = [(what, *blocks[n - 2][:2]) for what in ("rotated",)] if n > 1 else [None]
        free = {"q1": None, "q0": ("scores", 3, REP - 1), "k": ("scores", NT - 1, REP - 1)}[w]
        add("PE", ("project", w, k), 1.28, at, before[0], free, ("w_split", 0, 0) if w != "q1" else None)
        add("ACT", ("crossed", w, k), 1.1, at, ("project", w, k), before[1], two[0])
        add("DVE", ("straight", w, k), 0.66, at, ("crossed", w, k), before[2])
        add("Pool", ("rotated", w, k), 4.6, at, ("crossed", w, k), ("straight", w, k), before[3])
        if (w, k) == ("q1", REP - 1) and more:
            add("Pool", ("w_split", 0, 0), 7.0, at + 0.1, ("project", w, k), ("rotated", w, k))
    if more:
        for k in range(2):
            add("PE", ("project", "v", k), 1.28, 8.3, ("project", "k", 1), ("scores", NT + EARLY - 1, REP - 1),
                ("project", "v", k - 1))
            add("ACT", ("v_high", k, 0), 0.52, 8, ("values", NT - 1, NT - 1), ("project", "v", k), ("v_high", k - 1, 0))
            add("DVE", ("v_low", k, 0), 0.66, 8, ("v_high", k, 0), ("v_low", k - 1, 0))
    for step in steps:
        if step[0] == "scores" and step[1] == 4:
            later.append((step, ("rotated", "q1", step[2])))
        if step[:2] == ("scores", NT):
            later += [(step, ("rotated", "q0", hd)) for hd in range(REP)] + [(step, ("rotated", "k", 0))]
    for step, before in later:
        steps[step][3].append(before)

    leaves = {"scores": ["exp"], "project": ["straight"]}
    free_at = dict.fromkeys(("PE", "ACT", "DVE", "Pool"), 0.0)
    done, orders, slots = {}, {e: [] for e in free_at}, []
    while len(done) < len(steps):
        best = None
        for step, (engine, us, at, before) in steps.items():
            if step in done or any(x not in done for x in before):
                continue
            start = max([free_at[engine]] + [done[x] + (0.12 if steps[x][0] != engine else 0.07 * (engine != "PE")) for x in before])
            if step[0] in ("scores", "project") and len(slots) >= 2:
                user = slots[-2]
                left = [("v_low", user[2], 0)] if user[1] == "v" else [(what, *user[1:]) for what in leaves[user[0]]]
                if any(x not in done for x in left):
                    continue
                start = max([start] + [done[x] + 0.12 for x in left])
            rank = (max(start, free_at[engine] + SLACK[engine]), at, start)
            if best is None or rank < best[0]:
                best = (rank, start, step)
        _, start, step = best
        engine, us, _, _ = steps[step]
        done[step] = free_at[engine] = start + us
        orders[engine].append(step)
        if step[0] in ("scores", "project"):
            slots.append(step)
    if more:
        assert slots[-2:] == [("project", "v", 0), ("project", "v", 1)]
    return orders, max(done.values())


EARLY = 2
DUE = {"q1": -0.182, "q1_each": 0.383, "q0": 3.086, "q0_each": 0.322, "scores": -1.558, "max": 2.133, "exp": -0.895,
       "turn": -0.582, "high": 0.85, "low": 0.822, "values": 1.425, "attn_high": -0.768, "attn_low": 0.788,
       "out": -0.274, "added": 2.599, "project": -0.001, "crossed": 2.06, "straight": -2.935, "rotated": 0.513}
SLACK = {"PE": 0.15, "ACT": 0.05, "DVE": 0.15, "Pool": 0}


def slot_users(order):
    found, n, last = {}, 0, [None, None]
    for step in order["PE"]:
        if step[0] in ("scores", "project"):
            found[step] = (n % 2, last[n % 2])
            last[n % 2] = step
            n += 1
    return found


_first = [("k", 0), ("q0", 0), ("q0", 1), ("q0", 2), ("q0", 3), ("k", 1)]


def staggered(*lags):
    return [(what, *_first[n - lag]) for n in range(len(_first) + max(lag for _, lag in lags))
            for what, lag in lags if 0 <= n - lag < len(_first)]


def _softmaxes(what):
    return [(what, i, hd) for i in range(EARLY) for hd in range(REP)]


def on_pool(step):
    return _first.index(step[1:]) % 3 == 0


FIRST = {
    "PE": [("project", *b) for b in _first] + _softmaxes("scores") + [("project", "v", 0), ("project", "v", 1)],
    "ACT": staggered(("crossed", 0), ("qk_high", 2)) + _softmaxes("exp") + [("v_high", 0, 0), ("v_high", 1, 0)],
    "DVE": [step for step in staggered(("straight", 0), ("qk_sum", 1), ("qk_low", 2)) if step[0] != "qk_low" or not on_pool(step)]
           + _softmaxes("max") + [("v_low", 0, 0), ("v_low", 1, 0)],
    "Pool": [step for step in staggered(("times_sines", 0), ("qk_low", 2)) if step[0] != "qk_low" or on_pool(step)],
}


C_KEY, C_THR, C_BEFORE, C_SLOT = 0, 8, 72, 136
C_TOKEN = C_SLOT + NS * E
C_ALL = C_TOKEN + NT + 1
ROW = D + 2


def constants():
    inv = (1.0 / THETA ** (np.arange(0, HD, 2, dtype=np.float32) / np.float32(HD))).astype(np.float32)
    ang = np.arange(T, dtype=np.float32)[None, :] * inv[:, None]
    cos, sin = np.cos(ang).astype(np.float32), np.sin(ang).astype(np.float32)
    rope = np.concatenate([np.concatenate([cos, cos]), np.concatenate([-sin, sin])], axis=1)
    ident = np.eye(P, dtype=np.float32)
    r = np.arange(P)
    mask = np.where(r[None, :] <= r[:, None], 0.0, -BIG).astype(np.float32)
    before = (r[:, None] < r[None, :]).astype(np.float32)
    small = np.zeros((P, C_ALL), np.float32)
    e = np.arange(E)
    small[:, C_KEY:C_KEY + E] = E - e
    small[:, C_THR:C_THR + E * E] = np.tile(P * e, E)
    small[:, C_BEFORE:C_BEFORE + E * E] = (e[None, :] < e[:, None]).ravel()
    small[:, C_SLOT:C_TOKEN] = np.repeat(np.arange(NS), E)
    small[:, C_TOKEN:] = r[:, None] + P * np.arange(NT + 1)
    left = np.tile((T - 1 - np.arange(T, dtype=np.float32))[None, :], (P, 1))
    return {
        "c_rope": np.ascontiguousarray(rope, np.float32),
        "c_square": np.ascontiguousarray(np.concatenate([ident, mask, before], axis=1)),
        "c_small": small,
        "c_left": np.ascontiguousarray(left, np.float32),
    }


def macaron(nc, a, out, scratch):
    xs_dram, sum_dram, xsave_dram = scratch

    with ExitStack() as ctx:
        def sb(name, shape, dt=F32, c=ctx):
            return c.enter_context(nc.sbuf_tensor(name, shape, dt))

        def sem(name):
            return ctx.enter_context(nc.semaphore(name))

        ps = ctx.enter_context(nc.psum_tensor("ps", [P, 8, 512], F32))

        h = sb("h", [P, NT, D])
        rope = sb("rope", [P, 2, T])
        with ExitStack() as phase:
            sb("x_place", [P, NT, D], c=phase)
            xs = sb("xs", [P, 2, ROW], c=phase)
            ys = sb("ys", [P, 2, D], c=phase)
            xsT = sb("xsT", [P, 2, 2, DC, P], F32R, c=phase)
            hid = sb("hid", [P, 2, F], c=phase)
            hidT = sb("hidT", [P, 2, 2, F], F32R, c=phase)
        with ExitStack() as phase:
            sb("x_place_too", [P, NT, D], c=phase)
            kT_low0 = sb("kT_low0", [P, IC // 2, HALF], F32R, c=phase)
            kT_high = sb("kT_high", [P, IC, HALF], F32R, c=phase)
        probs = sb("probs", [P, 2, REP, T])
        flat = probs[:].rearrange("p a b t -> p (a b t)")
        x = flat[:, 0:NT * D].rearrange("p (t d) -> p t d", t=NT)
        y = flat[:, NT * D:2 * NT * D].rearrange("p (t d) -> p t d", t=NT)
        rows_out = flat[:, NT * D:NT * D + TOPK * NT * ROW].rearrange("p (k t w) -> p k t w", k=TOPK, t=NT)
        gated = flat[:, 0:2 * F].rearrange("p (b n) -> p b n", b=2)
        square = sb("square", [P, 3, P])
        ident = square[:, 0, :]
        square16 = sb("square16", [P, 3, P], BF16)
        ones16 = sb("ones16", [P, P], BF16)
        ones = sb("ones", [P, P])
        small = sb("small", [P, C_ALL])
        cols = sb("cols", [P, 2, 8])
        gate = sb("gate", [P, DC, E])
        blank = sb("blank", [P, ROW])
        gatekeeper = sb("gatekeeper", [P, 1])
        slot_token = sb("slot_token", [P, 2], U32)
        slot_weight = sb("slot_weight", [P, 2])
        stats = sb("stats", [P, NT, 6])
        meanvar = sb("meanvar", [P, NT, 2])
        mean = sb("mean", [P, NT])
        var = sb("var", [P, 2, NT])
        std = sb("std", [P, 2, NT])
        rstd = sb("rstd", [P, 2, NT])
        negmax = sb("negmax", [P, 8])
        rowsum = sb("rowsum", [P, 4 * REP])
        rowinv = sb("rowinv", [P, 4 * REP])

        with ExitStack() as phase:
            sb("resident", [P, RES, 3 * DC * F], c=phase)
            tokT = sb("tokT", [P, 2, DC, T], F32R, c=phase)
            keysT = sb("keysT", [P, 2, T], F32R, c=phase)
            values = sb("values", [P, 2, NT, HD], F32R, c=phase)
            queriesT = sb("queriesT", [P, 2, REP, T], F32R, c=phase)
            straight = sb("straight", [P, 2, HALF], c=phase)
            crossed = sb("crossed", [P, 2, HALF], c=phase)
            probsT = sb("probsT", [P, 3, 2, REP * P], F32R, c=phase)
            attnT = sb("attnT", [P, 2, 2, REP * P], F32R, c=phase)
            w_in = sb("w_in", [P, DC, REP * HD + 2 * HD], c=phase)
            w_qkv = sb("w_qkv", [P, 2, DC, REP * HD + 2 * HD], F32R, c=phase)
            wo_in = sb("wo_in", [P, REP, D], c=phase)
            w_o = sb("w_o", [P, 2, REP, D], F32R, c=phase)

        with ExitStack() as phase:
            experts = sb("experts", [P, E, 3 * DC * F], c=phase)
            w1 = experts[:, :, 0:DC * F].rearrange("p e (c n) -> p e c n", c=DC)
            w3 = experts[:, :, DC * F:2 * DC * F].rearrange("p e (c n) -> p e c n", c=DC)
            w2 = experts[:, :, 2 * DC * F:].rearrange("p e (c n) -> p e c n", c=FC)
            logits = sb("logits", [P, NT, E], c=phase)
            work = sb("work", [P, NT, E], c=phase)
            pick = sb("pick", [P, 2, NT, E], c=phase)
            both = sb("both", [P, NT, E], BF16, c=phase)
            top = sb("top", [P, 2, NT], c=phase)
            key = sb("key", [P, NT], c=phase)
            wts = sb("wts", [P, 2, NT], c=phase)
            count = sb("count", [P, E], c=phase)
            cube = sb("cube", [P, NS, E], c=phase)
            tiles = sb("tiles", [P, E], c=phase)
            first = sb("first", [P, E], c=phase)
            slotf = sb("slotf", [P, 2, NT], c=phase)
            slot = sb("slot", [P, 2, NT], U32, c=phase)
            ownerf = sb("ownerf", [P, NS], c=phase)
            owner = sb("owner", [P, NS], I32, c=phase)
            with ExitStack() as tiles_phase:
                parts13 = sb("parts13", [P, 2, 2, 2 * DC * F], F32R, c=tiles_phase)
                parts2 = sb("parts2", [P, 2, 2, FC * D], F32R, c=tiles_phase)
            xT = sb("xT", [P, DC, 1 + T], c=phase)
            kT_low1 = sb("kT_low1", [P, IC // 2, HALF], F32R, c=phase)
            Wv = sb("Wv", [P, DC, D], c=phase)
            Wr = sb("Wr", [P, DC, D], c=phase)
            Wo = sb("Wo", [P, DC, D], c=phase)
            Wck = sb("Wck", [P, DC, RI], c=phase)
            Wcv = sb("Wcv", [P, IC, D], c=phase)
            Wcr = sb("Wcr", [P, DC, D], c=phase)
            rows = sb("rows", [P, 5, D], c=phase)
        with ExitStack() as phase:
            sb("resident_too", [P, RES, 3 * DC * F], c=phase)
            mixT = sb("mixT", [P, DC, T], c=phase)
            decay = sb("decay", [P, HALF], c=phase)
            vsum = sb("vsum", [P, 4], c=phase)
            vmix = sb("vmix", [P, 2], c=phase)
            vwide = sb("vwide", [P, DC, P], c=phase)
            u = sb("u", [P, D], c=phase)
            rg = sb("rg", [P, 2, HALF], c=phase)
            ck_parts = sb("ck_parts", [P, 2, DC, RI], F32R, c=phase)
            cv_parts = sb("cv_parts", [P, 2, IC, D], F32R, c=phase)
            cr_parts = sb("cr_parts", [P, 2, DC, D], F32R, c=phase)
            xT_parts = sb("xT_parts", [P, 2, DC, 1 + T], F32R, c=phase)
        relu = mixT[:].rearrange("p c (k n) -> p (c k) n", k=2)
        crossed4 = flat[:, 0:NT * D].rearrange("p (k n) -> p k n", k=4)
        straight4 = flat[:, NT * D:2 * NT * D].rearrange("p (k n) -> p k n", k=4)
        leftv = flat[:, NT * D:NT * D + T]

        N1, N2, TMG, TMB, CMG, CMB, TF, TD = range(8)

        S = {}
        for name in (
            "square_in consts_in experts_in x_in cols_in blank_set blank_out pad_out qkv_in wo_in rwkv_in left_in saved x_back stored "
            "h_ready owner_ready dve_step consts_ready var_ready std_ready y_ready turned xT_ready "
            "w_split wo_split projected_qk projected_v cross_ready straight_ready rotated qk_ready v_high v_low "
            "sines_in qk_sum qk_high "
            "tokT_high scores_ready max_ready exp_done rowinv_ready pool_step "
            "turn_done probsT_high probsT_low pv_done attnT_high attnT_low squared out_ps out_added xT_clear "
            "logits_ps routing_ps routed pick_ready scattered gap_ready gap_exp "
            "rstd_ready rows_copied base_ready base_out meta_ready gate_open added sum_in_first sum_in_last "
            "xs_turned xsT_high xsT_ready up_done silu_done hid_ready hid_turned hidT_high hidT_ready down_done ys_ready "
            "w13_high w13_low w2_high w2_low "
            "mix_ready v_done decay_done decay_used vw_ready u_done r_done r_ready r_used ck_done ck_relu ck_sq "
            "rows_in shift_ready gained scaled biased kT_high kT_ready ck_split ck_split_low xT_high xT_low "
            "cv_done cv_sig cv_used x_final"
        ).split():
            S[name] = sem(name)
        xs_in = [sem("xs_in_even"), sem("xs_in_odd")]
        PAR = [(NS + 1) // 2, NS // 2]

        x_dram = a["L0_attn_x"].rearrange("a (t p) d -> p (a t) d", p=P)
        out_dram = out.rearrange("a (t p) d -> p (a t) d", p=P)
        xsave = xsave_dram.rearrange("(t p) d -> p t d", p=P)
        xs_tiles = xs_dram.rearrange("(n p) d -> p n d", p=P)
        sums = sum_dram.rearrange("(t p) d -> p t d", p=P)
        wq_d = a["L0_ffn_wq"].rearrange("(c p) (g n) -> p c g n", p=P, g=KVH)
        wk_d = a["L0_ffn_wk"].rearrange("(c p) (g n) -> p c g n", p=P, g=KVH)
        wv_d = a["L0_ffn_wv"].rearrange("(c p) (g n) -> p c g n", p=P, g=KVH)
        wo_d = a["L0_ffn_wo"].rearrange("(g r p) d -> p g r d", p=P, g=KVH)

        def chunks(name):
            return a[name].rearrange("(c p) n -> p c n", p=P)

        def column(name):
            return a[name].rearrange("(c p) -> p c", p=P)

        def softmax_n(gg, i, hd):
            return gg * SOFT + i * REP + hd

        ORDERS = {more: group_order(more)[0] for more in (True, False)}

        TURN_OF = [0, 4]

        class Group:

            def __init__(self, f, g, order):
                self.gg = f * KVH + g
                self.users = slot_users(order)
                self.first = first = order is FIRST
                self.qk0 = 10 * KVH * f + (0 if first else 6 + 10 * g)
                self.qk = {}
                for step in order["PE"]:
                    if step[0] == "project" and step[1] != "v":
                        self.qk[step[1:]] = len(self.qk)
                self.v0 = 2 * (KVH * f + (0 if first else g + 1))

            def slot(self, step):
                return self.users[step][0]

            def terms(self, block):
                n = self.qk[block]
                if self.first:
                    return straight4[:, n % 4, :], crossed4[:, n % 4, :]
                return straight[:, n % 2, :], crossed[:, n % 2, :]

            def qk_n(self, block):
                return self.qk0 + self.qk[block]

        def qk_place(what, k):
            if what == "k":
                return REP * HD, k, keysT[:, :, k * HALF:(k + 1) * HALF]
            half = int(what[1])
            return k * HD, half, queriesT[:, :, k, half * HALF:(half + 1) * HALF]

        block = ctx.enter_context(nc.Block())

        @block.sync
        def _(sp):
            sp.dma_start(x, x_dram).then_inc(S["x_in"], 16)
            sp.dma_start(square[:], a["c_square"].rearrange("p (k n) -> p k n", k=3)).then_inc(S["square_in"], 16)

            def load_constants():
                for n, name in enumerate(("L0_ffn_norm1_w", "L0_ffn_norm2_w", "L0_attn_tm_g", "L0_attn_tm_b",
                                          "L0_attn_cm_g", "L0_attn_cm_b", "L0_attn_time_first", "L0_attn_time_decay")):
                    with nc.allow_non_contiguous_dma(reason="256 single features"):
                        sp.dma_start(cols[:, :, n], column(name)).then_inc(S["cols_in"], 16)
                sp.dma_start(rope[:], a["c_rope"].rearrange("p (k t) -> p k t", k=2)).then_inc(S["consts_in"], 16)
                sp.dma_start(small[:], a["c_small"]).then_inc(S["consts_in"], 16)
                sp.dma_start(gate[:], chunks("L0_ffn_gate_w")).then_inc(S["consts_in"], 16)

            def load_expert(e):
                sp.dma_start(w1[:, e], a["L0_ffn_w1"][e].rearrange("(c p) n -> p c n", p=P)).then_inc(S["experts_in"], 16)
                sp.dma_start(w3[:, e], a["L0_ffn_w3"][e].rearrange("(c p) n -> p c n", p=P)).then_inc(S["experts_in"], 16)
                sp.dma_start(w2[:, e], a["L0_ffn_w2"][e].rearrange("(c p) n -> p c n", p=P)).then_inc(S["experts_in"], 16)

            def blank_slots(f):
                sp.wait_ge(S["blank_set"], 1)
                sp.dma_start(xs_tiles, blank[:].rearrange("p (n w) -> p n w", n=1).broadcast_to([P, NS, ROW])
                             ).then_inc(S["blank_out"], 16)

            def attention_weights(f):
                def load(g, first=False):
                    gg = f * KVH + g
                    sp.dma_start(w_in[:, :, 0:REP * HD], wq_d[:, :, bass.ds(g, 1), :]).then_inc(S["qkv_in"], 16)
                    sp.dma_start(w_in[:, :, REP * HD:REP * HD + HD], wk_d[:, :, bass.ds(g, 1), :]).then_inc(S["qkv_in"], 16)
                    sp.dma_start(w_in[:, :, REP * HD + HD:], wv_d[:, :, bass.ds(g, 1), :]).then_inc(S["qkv_in"], 16)
                    if first:
                        load_constants()
                    sp.dma_start(wo_in[:], wo_d[:, bass.ds(g, 1), :, :]).then_inc(S["wo_in"], 16)
                if f == 0:
                    load(0, True)
                    for e in range(RES):
                        load_expert(e)
                    blank_slots(0)
                    sp.dma_start(sums[:, NT, :], blank[:, 0:D]).then_inc(S["pad_out"], 16)
                else:
                    sp.wait_ge(S["ck_split_low"], 3)
                    sp.wait_ge(S["r_done"], NT // 2)
                    sp.wait_ge(S["u_done"], 1)
                    load(0)
                    sp.wait_ge(S["x_final"], 1)
                    sp.dma_start(xsave, x).then_inc(S["saved"], 16)
                    blank_slots(1)
                with sp.Fori(1, KVH) as g:
                    sp.wait_ge(S["w_split"], 2 * (f * KVH + g))
                    sp.wait_ge(S["wo_split"], 2 * (f * KVH + g))
                    load(g)

            def load_xs(k, par):
                sp.dma_start(xs[:, par, :], xs_tiles[:, bass.ds(2 * k + par, 1), :]).then_inc(xs_in[par], 16)

            def moe(f):
                sp.wait_ge(S["out_ps"], 2 * NT * KVH * (f + 1))
                sp.wait_ge(S["squared"], NT * (f + 1))
                sp.dma_start(x, x_dram if f == 0 else xsave).then_inc(S["x_back"], 16)
                for e in range(RES, E):
                    load_expert(e)
                sp.wait_ge(S["base_ready"], f + 1)
                sp.dma_start(sums[:, 0:NT, :], h[:]).then_inc(S["base_out"], 16)
                sp.wait_ge(S["scattered"], 16 * 16 * (f + 1))
                for par in range(2):
                    load_xs(0, par)
                with sp.Fori(0, (NS - 3) // 2) as k:
                    for par in range(2):
                        sp.wait_ge(S["meta_ready"], NS * f + 2 * k + par + 1)
                        load_xs(k + 1, par)
                sp.wait_ge(S["meta_ready"], NS * f + NS - 2)
                load_xs((NS - 1) // 2, 0)
                sp.wait_ge(S["added"], 16 * NS * (f + 1))
                if f == 0:
                    sp.dma_start(x[:, 0:NT // 2, :], sums[:, 0:NT // 2, :]).then_inc(S["sum_in_first"], 16)
                    sp.dma_start(x[:, NT // 2:, :], sums[:, NT // 2:NT, :]).then_inc(S["sum_in_last"], 16)
                    for n, name in enumerate(("ln1_g", "ln1_b", "ln2_g", "ln2_b", "bo")):
                        sp.dma_start(rows[:, n, :], a["L0_attn_" + name].rearrange("(a d) -> a d", a=1)
                                     .broadcast_to([P, D])).then_inc(S["rows_in"], 16)
                    for tile, src in ((Wv, "L0_attn_Wv"), (Wr, "L0_attn_Wr"), (Wo, "L0_attn_Wo"),
                                      (Wck, "L0_attn_Wck"), (Wcv, "L0_attn_Wcv"), (Wcr, "L0_attn_Wcr")):
                        sp.dma_start(tile[:], chunks(src)).then_inc(S["rwkv_in"], 16)

            attention_weights(0)
            moe(0)
            sp.wait_ge(S["turned"], 3 * NT)
            sp.dma_start(leftv, a["c_left"]).then_inc(S["left_in"], 16)
            attention_weights(1)
            sp.wait_ge(S["saved"], 16)
            moe(1)
            sp.dma_start(out.rearrange("a t d -> (a t) d"), sum_dram[0:T, :]).then_inc(S["stored"], 16)
            sp.wait_ge(S["stored"], 16)

        @block.gpsimd
        def _(pool):
            pool.wait_ge(S["consts_ready"], 1)
            pool.wait_ge(S["consts_in"], 16 * 3)

            def split(g_n, dst, src, arrived, need, signal):
                pool.wait_ge(S[arrived], need * (g_n + 1))
                one = ones[:, 0:1].rearrange("p (a b) -> p a b", a=1).broadcast_to([P, src.shape[1], src.shape[2]])
                pool.tensor_tensor(dst[:, 0], src, one, ALU.mult).then_inc(S[signal], 1)
                pool.wait_ge(S[signal], 2 * g_n + 1)
                pool.tensor_tensor(dst[:, 1], src, dst[:, 0].bitcast(F32), ALU.subtract).then_inc(S[signal], 1)

            def group(f, g, order):
                grp = Group(f, g, order)
                for what, i, k in order["Pool"]:
                    if what == "wo_split":
                        continue
                    if what == "w_split":
                        pool.wait_ge(S["projected_qk"], grp.qk_n(("q1", REP - 1)) + 1)
                        split(grp.gg + 1, w_qkv, w_in[:], "qkv_in", 48, "w_split")
                        continue
                    _, half, dst = qk_place(i, k)
                    n, (direct, across) = grp.qk_n((i, k)), grp.terms((i, k))
                    if what == "qk_low":
                        pool.wait_ge(S["qk_high"], len(_first) * f + grp.qk[i, k] + 1)
                        if grp.qk[i, k] or f:
                            pool.wait_ge(S["qk_ready"], n)
                        pool.tensor_tensor(dst[:, 1], direct, dst[:, 0].bitcast(F32), ALU.subtract
                                           ).then_inc(S["qk_ready"], 1)
                        continue
                    pool.wait_ge(S["cross_ready"], n + 1)
                    if what == "times_sines":
                        pool.tensor_tensor(across, across, rope[:, 1, half * HALF:(half + 1) * HALF], ALU.mult
                                           ).then_inc(S["sines_in"], 1)
                        continue
                    r = n - len(_first) * (f + 1)
                    pool.tensor_tensor(across, across, rope[:, 1, half * HALF:(half + 1) * HALF], ALU.mult
                                       ).then_inc(S["rotated"], 1)
                    pool.wait_ge(S["rotated"], 3 * r + 1)
                    pool.wait_ge(S["straight_ready"], n + 1)
                    pool.tensor_tensor(dst[:, 0], direct, across, ALU.add).then_inc(S["rotated"], 1)
                    pool.wait_ge(S["rotated"], 3 * r + 2)
                    pool.tensor_tensor(direct, direct, across, ALU.add).then_inc(S["rotated"], 1)
                    pool.wait_ge(S["rotated"], 3 * r + 3)
                    pool.tensor_tensor(dst[:, 1], direct, dst[:, 0].bitcast(F32), ALU.subtract).then_inc(S["qk_ready"], 1)
                if order is ORDERS[True]:
                    pool.wait_ge(S["out_ps"], 2 * NT * (grp.gg + 1))
                    split(grp.gg + 1, w_o, wo_in[:], "wo_in", 16, "wo_split")

            def first_weights(f):
                pool.wait_ge(S["w_split"], 2 * KVH * f + 1)
                pool.tensor_tensor(w_qkv[:, 1], w_in[:], w_qkv[:, 0].bitcast(F32), ALU.subtract).then_inc(S["w_split"], 1)

            def attention(f):
                if f == 0:
                    first_weights(f)
                group(f, 0, FIRST)
                if f == 0:
                    split(f * KVH, w_o, wo_in[:], "wo_in", 16, "wo_split")
                with pool.Fori(0, KVH - 1) as g:
                    group(f, g, ORDERS[True])
                group(f, KVH - 1, ORDERS[False])

            def split_w2(f, tau, par):
                e = pool.value_load(owner[0:1, bass.ds(tau, 1)], min_val=0, max_val=E - 1)
                pool.wait_ge(S["w2_high"], NS * f + tau + 1)
                pool.tensor_tensor(parts2[:, par, 1], experts[:, bass.ds(e, 1), 2 * DC * F:], parts2[:, par, 0].bitcast(F32),
                                   ALU.subtract).then_inc(S["w2_low"], 1)

            def add_rows(f, tau, par):
                pool.wait_ge(S["ys_ready"], NS * f + tau + 1)
                if not isinstance(tau, int) or NS * f + tau > 0:
                    pool.wait_ge(S["added"], 16 * (NS * f + tau))
                    pool.wait_ge(S["gate_open"], NS * f + tau)
                pool.tensor_tensor(gatekeeper[:], ones[:, 0:1], ones[:, 0:1], ALU.mult).then_inc(S["gate_open"], 1)
                pool.indirect_dma_start(
                    out=sum_dram, out_offset=bass.IndirectOffsetOnAxis(ap=slot_token[:, par:par + 1], axis=0),
                    in_=ys[:, par, :], in_offset=None, compute_op=ALU.add).then_inc(S["added"], 16)

            def moe(f):
                pool.wait_ge(S["routed"], f + 1)
                pool.wait_ge(S["blank_out"], 16 * (f + 1))
                pool.wait_ge(S["rows_copied"], f + 1)
                for t in range(NT):
                    for k in range(TOPK):
                        pool.indirect_dma_start(
                            out=xs_dram, out_offset=bass.IndirectOffsetOnAxis(ap=slot[:, k, t:t + 1], axis=0),
                            in_=rows_out[:, k, t, :], in_offset=None).then_inc(S["scattered"], 16)
                pool.wait_ge(S["owner_ready"], f + 1)
                split_w2(f, 0, 0)
                pool.wait_ge(S["base_out"], 16 * (f + 1))
                if f == 0:
                    pool.wait_ge(S["pad_out"], 16)
                split_w2(f, 1, 1)
                add_rows(f, 0, 0)
                split_w2(f, 2, 0)
                add_rows(f, 1, 1)
                with pool.Fori(1, (NS - 1) // 2) as k:
                    split_w2(f, 2 * k + 1, 1)
                    add_rows(f, 2 * k, 0)
                    split_w2(f, 2 * k + 2, 0)
                    add_rows(f, 2 * k + 1, 1)
                add_rows(f, NS - 1, 0)

            def add_bias(k):
                for t in range(NT):
                    pool.wait_ge(S["scaled"], NT * (k // 2) + t + 1)
                    pool.tensor_tensor(y[:, t, :], y[:, t, :], rows[:, k, :], ALU.add).then_inc(S["biased"], 1)

            def rwkv():
                pool.wait_ge(S["rows_in"], 16 * 5)
                add_bias(1)
                for n, (parts, weights) in enumerate(((ck_parts, Wck), (cv_parts, Wcv), (cr_parts, Wcr))):
                    pool.wait_ge(S["ck_split"], n + 1)
                    pool.tensor_tensor(parts[:, 1], weights[:], parts[:, 0].bitcast(F32), ALU.subtract
                                       ).then_inc(S["ck_split_low"], 1)
                add_bias(3)
                pool.wait_ge(S["xT_high"], 1)
                pool.tensor_tensor(xT_parts[:, 1, :, 0:1], xT[:, :, 0:1], xT_parts[:, 0, :, 0:1].bitcast(F32), ALU.subtract
                                   ).then_inc(S["xT_low"], 1)
                for t in range(NT):
                    place = slice(1 + t * P, 1 + (t + 1) * P)
                    pool.wait_ge(S["xT_high"], t + 2)
                    pool.tensor_tensor(xT_parts[:, 1, :, place], xT[:, :, place], xT_parts[:, 0, :, place].bitcast(F32),
                                       ALU.subtract).then_inc(S["xT_low"], 1)
                first_weights(1)
                split(KVH, w_o, wo_in[:], "wo_in", 16, "wo_split")

            attention(0)
            moe(0)
            rwkv()
            attention(1)
            moe(1)

        @block.scalar
        def _(act):
            n_std = [0]

            def sqrt(k=1):
                n_std[0] += 1
                act.wait_ge(S["var_ready"], n_std[0])
                act.activation(std[:, 0:k, :], var[:, 0:k, :], ACT.Sqrt).then_inc(S["std_ready"], 1)

            def group(f, g, order):
                grp = Group(f, g, order)
                gg = grp.gg
                for what, i, k in order["ACT"]:
                    if what == "crossed":
                        n, (_, across), s = grp.qk_n((i, k)), grp.terms((i, k)), grp.slot(("project", i, k))
                        scale = SCALE if i == "k" else 1.0
                        act.wait_ge(S["projected_qk"], n + 1)
                        if order is FIRST and grp.qk[i, k] >= 4:
                            act.wait_ge(S["qk_sum"], len(_first) * f + grp.qk[i, k] - 3)
                        elif order is not FIRST:
                            act.wait_ge(S["qk_ready"], n - 1)
                        act.activation(across[0:64, :], ps[64:128, 2 * s, :], ACT.Copy, scale=scale)
                        act.activation(across[64:128, :], ps[0:64, 2 * s, :], ACT.Copy, scale=scale
                                       ).then_inc(S["cross_ready"], 1)
                    if what == "qk_high":
                        (direct, _), (_, _, dst) = grp.terms((i, k)), qk_place(i, k)
                        act.wait_ge(S["qk_sum"], len(_first) * f + grp.qk[i, k] + 1)
                        act.activation(dst[:, 0], direct, ACT.Copy).then_inc(S["qk_high"], 1)
                    if what == "v_high":
                        s = grp.slot(("project", "v", i))
                        act.wait_ge(S["projected_v"], grp.v0 + i + 1)
                        if order is not FIRST:
                            act.wait_ge(S["pv_done"], NT * (gg + 1))
                        act.activation(values[:, 0, 4 * i:4 * i + 4, :], ps[:, 2 * s, :].rearrange("p (t n) -> p t n", t=4),
                                       ACT.Copy).then_inc(S["v_high"], 1)
                    if what == "exp":
                        n, w, slot_n = softmax_n(gg, i, k), (i % NT + 1) * P, grp.slot(("scores", i, k))
                        m, r = (i % 2) * REP + k, (i % 4) * REP + k
                        act.wait_ge(S["max_ready"], n + 1)
                        act.activation(probs[:, i % 2, k, 0:w],
                                       ps[:, 2 * slot_n:2 * slot_n + 2, :].rearrange("p b n -> p (b n)")[:, 0:w], ACT.Exp,
                                       bias=negmax[:, m:m + 1], accum_out=rowsum[:, r:r + 1]).then_inc(S["exp_done"], 1)
                    if what == "high":
                        m = turns_before(i) + k
                        act.wait_ge(S["turn_done"], TURNS * gg + m + 1)
                        act.activation(probsT[:, m % 3, 0, :], ps[:, 4 + m % 2, :], ACT.Copy).then_inc(S["probsT_high"], 1)
                    if what == "attn_high":
                        act.wait_ge(S["pv_done"], NT * gg + i + 1)
                        act.activation(attnT[:, i % 2, 0, :], ps[:, 6 + i % 2, :], ACT.Copy).then_inc(S["attnT_high"], 1)

            def first_weights(f):
                act.wait_ge(S["qkv_in"], 48 * (KVH * f + 1))
                act.activation(w_qkv[:, 0], w_in[:], ACT.Copy).then_inc(S["w_split"], 1)

            def attention(f):
                if f == 0:
                    first_weights(f)
                for t in range(NT):
                    act.wait_ge(S["h_ready"], NT * f + t + 1)
                    act.activation(y[:, t, :], h[:, t, :], ACT.Copy, scale=rstd[:, 1, t:t + 1]).then_inc(S["y_ready"], 1)
                if f == 0:
                    act.wait_ge(S["cols_in"], 16 * 8)
                for t in range(NT):
                    act.wait_ge(S["turned"], NT * TURN_OF[f] + t + 1)
                    for c in range(DC):
                        last = act.activation(tokT[:, 0, c, t * P:(t + 1) * P], ps[:, 4 + t % 4, c * P:(c + 1) * P],
                                              ACT.Copy, scale=cols[:, c, N1:N1 + 1])
                    last.then_inc(S["tokT_high"], 1)
                if f:
                    act.wait_ge(S["saved"], 16)
                group(f, 0, FIRST)
                with act.Fori(0, KVH - 1) as g:
                    group(f, g, ORDERS[True])
                group(f, KVH - 1, ORDERS[False])

            def expert(tau):
                return act.value_load(owner[0:1, bass.ds(tau, 1)], min_val=0, max_val=E - 1)

            def split_up(f, tau, par):
                e = expert(tau)
                if not isinstance(tau, int) or tau >= 2:
                    act.wait_ge(S["up_done"], NS * f + tau - 1)
                for k in range(2):
                    block = slice(k * DC * F, (k + 1) * DC * F)
                    act.activation(parts13[:, par, 0, block], experts[:, bass.ds(e, 1), block], ACT.Copy
                                   ).then_inc(S["w13_high"], 1)

            def split_w2(f, tau, par):
                e = expert(tau)
                if not isinstance(tau, int) or tau >= 2:
                    act.wait_ge(S["down_done"], NS * f + tau - 1)
                act.activation(parts2[:, par, 0], experts[:, bass.ds(e, 1), 2 * DC * F:], ACT.Copy).then_inc(S["w2_high"], 1)

            def take_xs(f, tau, par):
                act.wait_ge(S["xs_turned"], NS * f + tau + 1)
                for c in range(DC):
                    last = act.activation(xsT[:, par, 0, c, :], ps[:, 4 + par, c * P:(c + 1) * P], ACT.Copy,
                                          scale=cols[:, c, N2:N2 + 1])
                last.then_inc(S["xsT_high"], 1)

            def silu(f, tau, par):
                act.wait_ge(S["up_done"], NS * f + tau + 1)
                act.activation(gated[:, par, :], ps[:, 2 * par, :], ACT.Silu).then_inc(S["silu_done"], 1)

            def take_hid(f, tau, par):
                act.wait_ge(S["hid_turned"], NS * f + tau + 1)
                act.activation(hidT[:, par, 0], ps[:, 6, :], ACT.Copy).then_inc(S["hidT_high"], 1)

            def moe(f):
                sqrt()
                act.wait_ge(S["rstd_ready"], f + 1)
                for t in range(NT):
                    last = act.activation(rows_out[:, 1, t, 0:D], h[:, t, :], ACT.Copy, scale=rstd[:, 0, t:t + 1])
                last.then_inc(S["rows_copied"], 1)
                act.wait_ge(S["gap_ready"], f + 1)
                act.activation(key[:], key[:], ACT.Exp).then_inc(S["gap_exp"], 1)
                act.wait_ge(S["owner_ready"], f + 1)
                act.wait_ge(S["experts_in"], 16 * 3 * (RES + (E - RES) * (f + 1)))
                for tau in range(2):
                    split_up(f, tau, tau)
                split_w2(f, 0, 0)
                take_xs(f, 0, 0)

                def step(tau, par, after=2):
                    silu(f, tau, par)
                    if after > 0:
                        take_xs(f, tau + 1, 1 - par)
                    if after > 1:
                        split_up(f, tau + 2, par)
                    take_hid(f, tau, par)
                    if after > 0:
                        split_w2(f, tau + 1, 1 - par)

                step(0, 0)
                step(1, 1)
                step(2, 0)
                with act.Fori(1, (NS - 3) // 2) as k:
                    step(2 * k + 1, 1)
                    step(2 * k + 2, 0)
                step(NS - 2, 1, 1)
                step(NS - 1, 0, 0)

            def second_norm(n):
                act.wait_ge(S["shift_ready"], n + 1)
                for t in range(NT):
                    act.activation(y[:, t, :], y[:, t, :], ACT.Identity, scale=rstd[:, 0, t:t + 1], bias=mean[:, t:t + 1]
                                   ).then_inc(S["y_ready"], 1)

            def rwkv():
                sqrt(2)
                sqrt()
                second_norm(0)
                act.wait_ge(S["rwkv_in"], 16 * 6)
                act.wait_ge(S["left_in"], 16)
                for n in range(4):
                    th, hc = divmod(n, 2)
                    if n:
                        act.wait_ge(S["decay_used"], n)
                    act.activation(decay[:], leftv[:, th * HALF:(th + 1) * HALF], ACT.Exp,
                                   scale=cols[:, hc, TD:TD + 1]).then_inc(S["decay_done"], 1)
                    if n < 3:
                        parts, weights = ((ck_parts, Wck), (cv_parts, Wcv), (cr_parts, Wcr))[n]
                        act.activation(parts[:, 0], weights[:], ACT.Copy).then_inc(S["ck_split"], 1)
                for n in range(NT // 2):
                    act.wait_ge(S["r_done"], n + 1)
                    if n >= 2:
                        act.wait_ge(S["r_used"], n - 1)
                    act.activation(rg[:, n % 2, :], ps[:, 4 + n % 2, :], ACT.Sigmoid).then_inc(S["r_ready"], 1)
                sqrt()
                for t in range(NT):
                    act.wait_ge(S["gained"], t + 1)
                    act.activation(y[:, t, :], y[:, t, :], ACT.Copy, scale=rstd[:, 0, t:t + 1]).then_inc(S["scaled"], 1)
                sqrt()
                second_norm(1)
                act.activation(xT_parts[:, 0, :, 0:1], xT[:, :, 0:1], ACT.Copy).then_inc(S["xT_high"], 1)
                for t in range(NT):
                    place = slice(1 + t * P, 1 + (t + 1) * P)
                    act.wait_ge(S["xT_ready"], 3 * NT + t + 1)
                    act.activation(xT_parts[:, 0, :, place], xT[:, :, place], ACT.Copy).then_inc(S["xT_high"], 1)
                for th in range(2):
                    if th:
                        first_weights(1)
                    for ic in range(IC + 1):
                        n = th * IC + ic
                        if ic < IC:
                            act.wait_ge(S["ck_done"], n + 1)
                            if n >= 4:
                                act.wait_ge(S["kT_ready"], n - 3)
                            act.activation(relu[:, n % 4, :], ps[:, n % 4, :], ACT.Relu).then_inc(S["ck_relu"], 1)
                        if ic:
                            n -= 1
                            act.wait_ge(S["ck_sq"], n + 1)
                            if th:
                                act.wait_ge(S["cv_done"], 4)
                            act.activation(kT_high[:, ic - 1, :], relu[:, n % 4, :], ACT.Copy).then_inc(S["kT_high"], 1)
                    for t in range(4):
                        n = th * 4 + t
                        act.wait_ge(S["cv_done"], n + 1)
                        if n >= 2:
                            act.wait_ge(S["cv_used"], n - 1)
                        act.activation(rg[:, n % 2, 0:D], ps[:, 4 + n % 4, D:2 * D], ACT.Sigmoid).then_inc(S["cv_sig"], 1)

            sqrt(2)
            attention(0)
            moe(0)
            rwkv()
            sqrt(2)
            attention(1)
            moe(1)

        @block.vector
        def _(dve):
            steps = [0]

            def link(ins):
                steps[0] += 1
                ins.then_inc(S["dve_step"], 1)
                dve.wait_ge(S["dve_step"], steps[0])

            n_std = [0]
            n_turn = [0]

            def rstds(k=1):
                n_std[0] += 1
                dve.wait_ge(S["std_ready"], n_std[0])
                link(dve.reciprocal(rstd[:, 0:k, :], std[:, 0:k, :]))

            def aggregate():
                for t in range(NT):
                    last = dve.bn_aggr(meanvar[:, t, :], stats[:, t, :])
                link(last)

            def normalise(dst, src):
                for t in range(NT):
                    last = dve.tensor_scalar(dst[:, t, :], src[:, t, :], meanvar[:, t, 0:1], rstd[:, 0, t:t + 1],
                                             ALU.subtract, ALU.mult)
                link(last)

            def two_norms(eps1, eps2):
                link(dve.tensor_scalar(var[:, 0, :], meanvar[:, :, 1], eps1, None, ALU.add))
                link(dve.reciprocal(std[:, 0, :], var[:, 0, :]))
                link(dve.tensor_tensor(var[:, 1, :], meanvar[:, :, 1], std[:, 0, :], ALU.mult))
                dve.tensor_scalar(var[:, 1, :], var[:, 1, :], eps2, None, ALU.add).then_inc(S["var_ready"], 1)
                rstds(2)

            def one_norm(eps):
                dve.tensor_scalar(var[:, 0, :], meanvar[:, :, 1], eps, None, ALU.add).then_inc(S["var_ready"], 1)
                rstds()

            def take_turned(gain, bias=None):
                u0 = NT * n_turn[0]
                n_turn[0] += 1
                for t in range(NT):
                    dve.wait_ge(S["turned"], u0 + t + 1)
                    src = ps[:, 4 + t % 4, 0:D].rearrange("p (c n) -> p c n", c=DC)
                    for c in range(DC):
                        dst = xT[:, c, 1 + t * P:1 + (t + 1) * P]
                        g = cols[:, c, gain:gain + 1]
                        if bias is None:
                            last = dve.tensor_scalar(dst, src[:, c, :], g, None, ALU.mult)
                        else:
                            last = dve.tensor_scalar(dst, src[:, c, :], g, cols[:, c, bias:bias + 1], ALU.mult, ALU.add)
                    last.then_inc(S["xT_ready"], 1)

            dve.memset(ones[:], 1.0)
            dve.memset(ones16[:], 1.0)
            link(dve.memset(blank[:], 0.0))
            dve.wait_ge(S["square_in"], 16)
            dve.tensor_copy(square16[:], square[:]).then_inc(S["consts_ready"], 1)
            dve.wait_ge(S["x_in"], 16)

            def attention(f):
                if f == 0:
                    for t in range(NT):
                        last = dve.bn_stats(stats[:, t, :], x[:, t, :])
                    link(last)
                aggregate()
                two_norms(EPS, EPS)
                for t in range(NT):
                    dve.tensor_scalar(h[:, t, :], x[:, t, :], meanvar[:, t, 0:1], rstd[:, 0, t:t + 1],
                                      ALU.subtract, ALU.mult).then_inc(S["h_ready"], 1)
                if f == 0:
                    dve.wait_ge(S["cols_in"], 16 * 8)
                    dve.wait_ge(S["consts_in"], 16 * 3)
                    dve.tensor_copy(blank[:, D:D + 1], small[:, C_TOKEN + NT:C_TOKEN + NT + 1]).then_inc(S["blank_set"], 1)
                u0 = NT * n_turn[0]
                n_turn[0] += 1
                for t in range(NT):
                    dve.wait_ge(S["tokT_high"], NT * f + t + 1)
                    for c in range(DC):
                        place = slice(t * P, (t + 1) * P)
                        last = dve.scalar_tensor_tensor(
                            out=tokT[:, 1, c, place], in0=ps[:, 4 + t % 4, c * P:(c + 1) * P], scalar=cols[:, c, N1:N1 + 1],
                            in1=tokT[:, 0, c, place].bitcast(F32), op0=ALU.mult, op1=ALU.subtract)
                    last.then_inc(S["xT_ready"], 1)
                group(f, 0, FIRST)
                with dve.Fori(0, KVH - 1) as g:
                    group(f, g, ORDERS[True])
                group(f, KVH - 1, ORDERS[False])
                dve.wait_ge(S["out_added"], REP * NT * KVH * (f + 1))

            def group(f, g, order):
                grp = Group(f, g, order)
                gg = grp.gg
                for what, i, k in order["DVE"]:
                    if what == "straight":
                        n, (direct, _), s = grp.qk_n((i, k)), grp.terms((i, k)), grp.slot(("project", i, k))
                        _, half, _ = qk_place(i, k)
                        dve.wait_ge(S["cross_ready"], n + 1)
                        if order is FIRST and grp.qk[i, k] >= 4:
                            dve.wait_ge(S["qk_ready"], n - 3)
                        dve.scalar_tensor_tensor(out=direct, in0=ps[:, 2 * s, :],
                                                 scalar=SCALE if i == "k" else 1.0,
                                                 in1=rope[:, 0, half * HALF:(half + 1) * HALF],
                                                 op0=ALU.mult, op1=ALU.mult).then_inc(S["straight_ready"], 1)
                    if what == "qk_sum":
                        n, (direct, across) = grp.qk_n((i, k)), grp.terms((i, k))
                        dve.wait_ge(S["sines_in"], len(_first) * f + grp.qk[i, k] + 1)
                        dve.wait_ge(S["straight_ready"], n + 1)
                        dve.tensor_tensor(direct, direct, across, ALU.add).then_inc(S["qk_sum"], 1)
                    if what == "qk_low":
                        n, (direct, _), (_, _, dst) = grp.qk_n((i, k)), grp.terms((i, k)), qk_place(i, k)
                        dve.wait_ge(S["qk_high"], len(_first) * f + grp.qk[i, k] + 1)
                        dve.wait_ge(S["qk_ready"], n)
                        dve.tensor_tensor(dst[:, 1], direct, dst[:, 0].bitcast(F32), ALU.subtract
                                          ).then_inc(S["qk_ready"], 1)
                    if what == "v_low":
                        s = grp.slot(("project", "v", i))
                        dve.wait_ge(S["v_high"], grp.v0 + i + 1)
                        part = values[:, :, 4 * i:4 * i + 4, :]
                        dve.tensor_tensor(part[:, 1], ps[:, 2 * s, :].rearrange("p (t n) -> p t n", t=4),
                                          part[:, 0].bitcast(F32), ALU.subtract).then_inc(S["v_low"], 1)
                    if what == "max":
                        s, w, m = 2 * grp.slot(("scores", i, k)), (i % NT + 1) * P, (i % 2) * REP + k
                        dve.wait_ge(S["scores_ready"], softmax_n(gg, i, k) + 1)
                        dve.tensor_reduce(negmax[:, m:m + 1], ps[:, s:s + 2, :].rearrange("p b n -> p (b n)")[:, 0:w],
                                          AX.X, ALU.max, negate=True).then_inc(S["max_ready"], 1)
                    if what == "low":
                        m = turns_before(i) + k
                        dve.wait_ge(S["probsT_high"], TURNS * gg + m + 1)
                        dve.tensor_tensor(probsT[:, m % 3, 1, :], ps[:, 4 + m % 2, :], probsT[:, m % 3, 0, :].bitcast(F32),
                                          ALU.subtract).then_inc(S["probsT_low"], 1)
                    if what == "attn_low":
                        m = (i % 4) * REP
                        dve.wait_ge(S["attnT_high"], NT * gg + i + 1)
                        dve.tensor_tensor(attnT[:, i % 2, 1, :], ps[:, 6 + i % 2, :], attnT[:, i % 2, 0, :].bitcast(F32),
                                          ALU.subtract).then_inc(S["attnT_low"], 1)
                        dve.reciprocal(rowinv[:, m:m + REP], rowsum[:, m:m + REP]).then_inc(S["rowinv_ready"], 1)
                    if what == "added":
                        m = (i % 4) * REP
                        dve.wait_ge(S["rowinv_ready"], NT * gg + i + 1)
                        dve.wait_ge(S["out_ps"], 2 * (NT * gg + i) + k + 1)
                        for hd in (2 * k, 2 * k + 1):
                            if hd:
                                dve.wait_ge(S["out_added"], REP * (NT * gg + i) + hd)
                            dve.scalar_tensor_tensor(out=h[:, i, :], in0=ps[:, 6 + i % 2, (hd % 2) * D:(hd % 2 + 1) * D],
                                                     scalar=rowinv[:, m + hd:m + hd + 1], in1=h[:, i, :],
                                                     op0=ALU.mult, op1=ALU.add).then_inc(S["out_added"], 1)
                        if k == 1 and order is ORDERS[False]:
                            dve.wait_ge(S["out_added"], REP * (NT * gg + i + 1))
                            dve.scalar_tensor_tensor(out=w_in[:, 0, 0:D], in0=h[:, i, :], scalar=1.0 / D, in1=h[:, i, :],
                                                     op0=ALU.mult, op1=ALU.mult, accum_out=var[:, 1, i:i + 1]
                                                     ).then_inc(S["squared"], 1)

            def route(f):
                bc = lambda ap: ap.rearrange("p (t o) -> p t o", o=1).broadcast_to([P, NT, E])
                keys = small[:, C_KEY:C_KEY + E].rearrange("p (o e) -> p o e", o=1).broadcast_to([P, NT, E])
                dve.wait_ge(S["logits_ps"], f + 1)
                link(dve.tensor_copy(logits[:], ps[:, 0, 0:NT * E].rearrange("p (t e) -> p t e", t=NT)))
                for k in range(TOPK):
                    src = logits if k == 0 else work
                    if k == 1:
                        link(dve.scalar_tensor_tensor(out=work[:], in0=pick[:, 0], scalar=-BIG, in1=logits[:],
                                                      op0=ALU.mult, op1=ALU.add))
                    link(dve.tensor_reduce(top[:, k, :], src[:], AX.X, ALU.max))
                    link(dve.tensor_tensor(pick[:, k], src[:], bc(top[:, k, :]), ALU.is_equal))
                    link(dve.tensor_tensor(pick[:, k], pick[:, k], keys, ALU.mult))
                    link(dve.tensor_reduce(key[:], pick[:, k], AX.X, ALU.max))
                    link(dve.tensor_tensor(pick[:, k], pick[:, k], bc(key[:]), ALU.is_equal))
                dve.tensor_tensor(both[:], pick[:, 0], pick[:, 1], ALU.add).then_inc(S["pick_ready"], 1)
                dve.tensor_tensor(key[:], top[:, 1, :], top[:, 0, :], ALU.subtract).then_inc(S["gap_ready"], 1)
                dve.wait_ge(S["gap_exp"], f + 1)
                link(dve.tensor_scalar(wts[:, 1, :], key[:], 1.0, 2.0, ALU.add, ALU.mult))
                link(dve.reciprocal(wts[:, 0, :], wts[:, 1, :]))
                dve.tensor_copy(rows_out[:, 0, :, D + 1], wts[:, 0, :])
                dve.tensor_tensor(rows_out[:, 1, :, D + 1], key[:], wts[:, 0, :], ALU.mult)
                dve.wait_ge(S["routing_ps"], f + 1)
                link(dve.tensor_copy(count[:], ps[:, 1, 128:128 + E]))
                sq = cube[:, 0:E, :]
                link(dve.tensor_tensor(sq, count[:].rearrange("p (e o) -> p e o", o=1).broadcast_to([P, E, E]),
                                       small[:, C_THR:C_THR + E * E].rearrange("p (e k) -> p e k", e=E), ALU.is_gt))
                link(dve.tensor_reduce(tiles[:], sq, AX.X, ALU.add))
                link(dve.tensor_tensor(sq, tiles[:].rearrange("p (o e) -> p o e", o=1).broadcast_to([P, E, E]),
                                       small[:, C_BEFORE:C_BEFORE + E * E].rearrange("p (e k) -> p e k", e=E), ALU.mult))
                link(dve.tensor_reduce(first[:], sq, AX.X, ALU.add))
                link(dve.tensor_scalar(count[:], first[:], float(P), None, ALU.mult))
                link(dve.tensor_tensor(work[:], ps[:, 1, 0:NT * E].rearrange("p (t e) -> p t e", t=NT),
                                       count[:].rearrange("p (o e) -> p o e", o=1).broadcast_to([P, NT, E]), ALU.add))
                for k in range(TOPK):
                    link(dve.tensor_tensor(pick[:, k], pick[:, k], work[:], ALU.mult))
                    link(dve.tensor_reduce(slotf[:, k, :], pick[:, k], AX.X, ALU.add))
                link(dve.tensor_copy(slot[:], slotf[:]))
                dve.sem_inc(S["routed"], 1)
                link(dve.tensor_tensor(tiles[:], tiles[:], first[:], ALU.add))
                link(dve.tensor_tensor(cube[:], small[:, C_SLOT:C_TOKEN].rearrange("p (n e) -> p n e", n=NS),
                                       tiles[:].rearrange("p (o e) -> p o e", o=1).broadcast_to([P, NS, E]), ALU.is_ge))
                link(dve.tensor_reduce(ownerf[:], cube[:], AX.X, ALU.add))
                dve.tensor_scalar(owner[:], ownerf[:], float(E - 1), None, ALU.min).then_inc(S["owner_ready"], 1)

            def expert(tau):
                return dve.value_load(owner[0:1, bass.ds(tau, 1)], min_val=0, max_val=E - 1)

            def split_up(f, tau, par, e):
                for k in range(2):
                    block = slice(k * DC * F, (k + 1) * DC * F)
                    dve.wait_ge(S["w13_high"], 2 * (NS * f + tau) + k + 1)
                    dve.tensor_tensor(parts13[:, par, 1, block], experts[:, bass.ds(e, 1), block],
                                      parts13[:, par, 0, block].bitcast(F32), ALU.subtract).then_inc(S["w13_low"], 1)

            def take_xs(f, tau, par):
                dve.wait_ge(S["xsT_high"], NS * f + tau + 1)
                for c in range(DC):
                    last = dve.scalar_tensor_tensor(
                        out=xsT[:, par, 1, c, :], in0=ps[:, 4 + par, c * P:(c + 1) * P], scalar=cols[:, c, N2:N2 + 1],
                        in1=xsT[:, par, 0, c, :].bitcast(F32), op0=ALU.mult, op1=ALU.subtract)
                last.then_inc(S["xsT_ready"], 1)

            def gate_hid(f, tau, par):
                dve.wait_ge(S["silu_done"], NS * f + tau + 1)
                dve.tensor_tensor(hid[:, par, :], gated[:, par, :], ps[:, 2 * par + 1, :], ALU.mult).then_inc(S["hid_ready"], 1)

            def take_hid(f, tau, par):
                dve.wait_ge(S["hidT_high"], NS * f + tau + 1)
                dve.tensor_tensor(hidT[:, par, 1], ps[:, 6, :], hidT[:, par, 0].bitcast(F32), ALU.subtract
                                  ).then_inc(S["hidT_ready"], 1)

            def take_ys(f, tau, par):
                dve.wait_ge(S["down_done"], NS * f + tau + 1)
                dve.tensor_scalar(ys[:, par, :], ps[:, 7, 0:D], slot_weight[:, par:par + 1], None, ALU.mult
                                  ).then_inc(S["ys_ready"], 1)

            def take_meta(f, tau, par):
                if not isinstance(tau, int) or tau >= 2:
                    dve.wait_ge(S["added"], 16 * (NS * f + tau - 1))
                dve.tensor_copy(slot_weight[:, par:par + 1], xs[:, par, D + 1:D + 2])
                dve.tensor_copy(slot_token[:, par:par + 1], xs[:, par, D:D + 1]).then_inc(S["meta_ready"], 1)

            def moe(f):
                dve.wait_ge(S["squared"], NT * (f + 1))
                dve.tensor_scalar(var[:, 0, :], var[:, 1, :], EPS, None, ALU.add).then_inc(S["var_ready"], 1)
                rstds()
                dve.sem_inc(S["rstd_ready"], 1)
                for t in range(NT):
                    dve.tensor_scalar(rows_out[:, 0, t, 0:D], h[:, t, :], rstd[:, 0, t:t + 1], None, ALU.mult
                                      ).then_inc(S["y_ready"], 1)
                for k in range(TOPK):
                    dve.tensor_copy(rows_out[:, k, :, D], small[:, C_TOKEN:C_TOKEN + NT])
                take_turned(N2)
                route(f)
                dve.wait_ge(S["x_back"], 16 * (f + 1))
                dve.wait_ge(S["rows_copied"], f + 1)
                for t in range(NT):
                    last = dve.scalar_tensor_tensor(out=h[:, t, :], in0=h[:, t, :], scalar=0.5, in1=x[:, t, :],
                                                    op0=ALU.mult, op1=ALU.add)
                last.then_inc(S["base_ready"], 1)
                dve.wait_ge(S["owner_ready"], f + 1)
                for tau in range(2):
                    split_up(f, tau, tau, expert(tau))
                take_xs(f, 0, 0)

                def step(tau, par, after=2):
                    if after > 1:
                        e = expert(tau + 2)
                    gate_hid(f, tau, par)
                    if after > 0:
                        take_xs(f, tau + 1, 1 - par)
                    if not isinstance(tau, int) or tau > 0:
                        take_ys(f, tau - 1, 1 - par)
                    take_meta(f, tau, par)
                    if after > 1:
                        split_up(f, tau + 2, par, e)
                    take_hid(f, tau, par)

                step(0, 0)
                step(1, 1)
                step(2, 0)
                with dve.Fori(1, (NS - 3) // 2) as k:
                    step(2 * k + 1, 1)
                    step(2 * k + 2, 0)
                step(NS - 2, 1, 1)
                step(NS - 1, 0, 0)
                take_ys(f, NS - 1, 0)
                if f == 0:
                    dve.memset(xT[:, :, 0:1], 0.0)
                if f == 0:
                    for t in range(NT):
                        dve.wait_ge(S["sum_in_first" if t < NT // 2 else "sum_in_last"], 16)
                        last = dve.bn_stats(stats[:, t, :], x[:, t, :])
                    link(last)

            def shift():
                dve.scalar_tensor_tensor(out=mean[:], in0=meanvar[:, :, 0], scalar=-1.0, in1=rstd[:, 0, :],
                                         op0=ALU.mult, op1=ALU.mult).then_inc(S["shift_ready"], 1)

            def biased_moments(n, work):
                for t in range(NT + 2):
                    if t < NT:
                        work(t)
                    if t >= 2:
                        dve.wait_ge(S["biased"], NT * n + t - 1)
                        last = dve.bn_stats(stats[:, t - 2, :], y[:, t - 2, :])
                link(last)
                aggregate()
                one_norm(EPS_RWKV)
                shift()

            def rwkv():
                aggregate()
                two_norms(EPS, EPS_RWKV)
                normalise(h, x)
                dve.wait_ge(S["rows_in"], 16 * 5)

                def first_gain(t):
                    dve.scalar_tensor_tensor(out=y[:, t, :], in0=h[:, t, :], scalar=rstd[:, 1, t:t + 1], in1=rows[:, 0, :],
                                             op0=ALU.mult, op1=ALU.mult).then_inc(S["scaled"], 1)

                biased_moments(0, first_gain)
                take_turned(TMG, TMB)
                link(dve.tensor_scalar(vmix[:], cols[:, :, TF], -1.0, 1.0, ALU.mult, ALU.add))
                for c in range(DC):
                    link(dve.tensor_scalar(mixT[:, c, :], xT[:, c, 0:T], vmix[:, c:c + 1], None, ALU.mult))
                    dve.scalar_tensor_tensor(out=mixT[:, c, :], in0=xT[:, c, 1:1 + T], scalar=cols[:, c, TF:TF + 1],
                                             in1=mixT[:, c, :], op0=ALU.mult, op1=ALU.add).then_inc(S["mix_ready"], 1)
                for n in range(4):
                    th, hc = divmod(n, 2)
                    dve.wait_ge(S["v_done"], n + 1)
                    dve.wait_ge(S["decay_done"], n + 1)
                    dve.tensor_tensor_reduce(out=decay[:], in0=ps[:, n, :], in1=decay[:], scale=1.0, scalar=0.0,
                                             op0=ALU.mult, op1=ALU.add, accum_out=vsum[:, 2 * hc + th:2 * hc + th + 1]
                                             ).then_inc(S["decay_used"], 1)
                dve.wait_ge(S["decay_used"], 4)
                dve.wait_ge(S["mix_ready"], 2)
                link(dve.tensor_reduce(vmix[:], vsum[:].rearrange("p (c k) -> p c k", c=2), AX.X, ALU.add))
                for c in range(DC):
                    dve.tensor_scalar(vwide[:, c, :], ones[:], vmix[:, c:c + 1], None, ALU.mult).then_inc(S["vw_ready"], 1)
                dve.wait_ge(S["u_done"], 1)
                link(dve.tensor_tensor(u[:], ps[:, 0, 0:D], rows[:, 4, :], ALU.add))
                wide = u[:].rearrange("p (o d) -> p o d", o=1).broadcast_to([P, 2, D])
                for n in range(NT // 2):
                    dve.wait_ge(S["r_ready"], n + 1)
                    r2 = rg[:, n % 2, :].rearrange("p (k d) -> p k d", k=2)
                    link(dve.tensor_tensor(r2, r2, wide, ALU.mult))
                    dve.tensor_tensor(h[:, 2 * n:2 * n + 2, :], h[:, 2 * n:2 * n + 2, :], r2, ALU.add).then_inc(S["r_used"], 1)
                    dve.wait_ge(S["r_used"], n + 1)
                    for t in (2 * n, 2 * n + 1):
                        last = dve.bn_stats(stats[:, t, :], h[:, t, :])
                link(last)
                aggregate()
                one_norm(EPS_RWKV)

                def second_gain(t):
                    dve.scalar_tensor_tensor(out=y[:, t, :], in0=h[:, t, :], scalar=meanvar[:, t, 0:1], in1=rows[:, 2, :],
                                             op0=ALU.subtract, op1=ALU.mult).then_inc(S["gained"], 1)

                biased_moments(1, second_gain)
                take_turned(CMG, CMB)
                for th in range(2):
                    for ic in range(IC + 1):
                        n = th * IC + ic
                        if ic < IC:
                            dve.wait_ge(S["ck_relu"], n + 1)
                            dve.tensor_tensor(relu[:, n % 4, :], relu[:, n % 4, :], relu[:, n % 4, :], ALU.mult
                                              ).then_inc(S["ck_sq"], 1)
                        if ic:
                            n -= 1
                            low = (kT_low0, kT_low1)[(ic - 1) // 4][:, (ic - 1) % 4, :]
                            dve.wait_ge(S["kT_high"], n + 1)
                            dve.tensor_tensor(low, relu[:, n % 4, :], kT_high[:, ic - 1, :].bitcast(F32), ALU.subtract
                                              ).then_inc(S["kT_ready"], 1)
                    for t in range(4):
                        n = th * 4 + t
                        dve.wait_ge(S["cv_sig"], n + 1)
                        link(dve.tensor_tensor(rg[:, n % 2, D:2 * D], rg[:, n % 2, 0:D], ps[:, 4 + n % 4, 0:D], ALU.mult))
                        link(dve.tensor_tensor(h[:, n, :], h[:, n, :], rg[:, n % 2, D:2 * D], ALU.add))
                        dve.tensor_tensor(x[:, n, :], x[:, n, :], h[:, n, :], ALU.add).then_inc(S["cv_used"], 1)
                        dve.wait_ge(S["cv_used"], n + 1)
                        last = dve.bn_stats(stats[:, n, :], x[:, n, :])
                link(last)
                dve.sem_inc(S["x_final"], 1)

            attention(0)
            moe(0)
            rwkv()
            attention(1)
            moe(1)

        @block.tensor
        def _(pe):
            n_turn = [0]

            pe.wait_ge(S["consts_ready"], 1)

            def turn_token(t, src):
                u0 = NT * n_turn[0]
                pe.wait_ge(S["y_ready"], u0 + t + 1)
                if t >= 4:
                    pe.wait_ge(S["xT_ready"], u0 + t - 3)
                for c in range(DC):
                    last = pe.transpose(ps[:, 4 + t % 4, c * P:(c + 1) * P], src[:, t, c * P:(c + 1) * P], ident)
                last.then_inc(S["turned"], 1)

            def turn_tokens():
                for t in range(NT):
                    turn_token(t, y)
                n_turn[0] += 1

            def tokens(c, t):
                return xT[:, c, 1 + t * P:1 + (t + 1) * P]

            def attention(f):
                turn_tokens()
                pe.wait_ge(S["xT_ready"], NT * n_turn[0])
                group(f, 0, FIRST)
                with pe.Fori(0, KVH - 1) as g:
                    group(f, g, ORDERS[True])
                group(f, KVH - 1, ORDERS[False])

            def products(dst, lhsT, rhs, start, stop):
                pe.matmul(dst, lhsT[0], rhs[0], start=start, stop=False)
                pe.matmul(dst, lhsT[1], rhs[0], start=False, stop=False)
                return pe.matmul(dst, lhsT[0], rhs[1], start=False, stop=stop)

            def parts(tensor, *index):
                index += (slice(None),) * (len(tensor.shape) - 2 - len(index))
                return [tensor[(slice(None), part) + index] for part in range(2)]

            def group(f, g, order):
                grp = Group(f, g, order)
                gg = grp.gg
                every = slice(None)
                for step in order["PE"]:
                    what, i, k = step
                    if what in ("scores", "project"):
                        s, user = grp.users[step]
                        if user is None:
                            if order is not FIRST:
                                pe.wait_ge(S["v_low"], 2 * gg + s + 1)
                        elif user[0] == "scores":
                            pe.wait_ge(S["exp_done"], softmax_n(gg, user[1], user[2]) + 1)
                        elif user[1] == "v":
                            pe.wait_ge(S["v_low"], grp.v0 + user[2] + 1)
                        else:
                            pe.wait_ge(S["straight_ready"], grp.qk_n(user[1:]) + 1)
                    if what == "project" and i == "v":
                        if k == 0:
                            pe.wait_ge(S["w_split"], 2 * (gg + (2 if order is not FIRST else 1)))
                        for t in range(4 * k, 4 * k + 4):
                            dst = ps[:, 2 * s, (t % 4) * HD:(t % 4 + 1) * HD]
                            for c in range(DC):
                                last = products(dst, parts(tokT, c, slice(t * P, (t + 1) * P)),
                                                parts(w_qkv, c, slice(REP * HD + HD, None)), c == 0, c == DC - 1)
                        last.then_inc(S["projected_v"], 1)
                    elif what == "project":
                        pe.wait_ge(S["w_split"], 2 * (gg + (1 if i == "q1" or order is FIRST else 2)))
                        col, half, _ = qk_place(i, k)
                        for c in range(DC):
                            last = products(ps[:, 2 * s, :], parts(w_qkv, c, slice(col, col + HD)),
                                            parts(tokT, c, slice(half * HALF, (half + 1) * HALF)), c == 0, c == DC - 1)
                        last.then_inc(S["projected_qk"], 1)
                    if what == "scores":
                        if i % NT == 0 and k == 0:
                            pe.wait_ge(S["qk_ready"], 10 * (gg + i // NT) + 5)
                        if i == 4:
                            pe.wait_ge(S["qk_ready"], 10 * gg + 6 + k + 1)
                        i %= NT
                        w = (i + 1) * P
                        q = parts(queriesT, k, slice(i * P, (i + 1) * P))
                        for b in range(i // 4 + 1):
                            n1 = min(512, w - 512 * b)
                            last = products(ps[:, 2 * s + b, 0:n1], q, parts(keysT, slice(512 * b, 512 * b + n1)),
                                            True, b < i // 4)
                        last = pe.matmul(ps[:, 2 * s + i // 4, (i % 4) * P:(i % 4 + 1) * P], square16[:, 0, :], square16[:, 1, :],
                                         start=False, stop=True)
                        last.then_inc(S["scores_ready"], 1)
                    if what == "turn":
                        m = turns_before(i) + k
                        if k == 0:
                            pe.wait_ge(S["exp_done"], softmax_n(gg, i, REP))
                        if m >= 2:
                            pe.wait_ge(S["probsT_low"], TURNS * gg + m - 1)
                        for hd in range(REP):
                            last = pe.transpose(ps[:, 4 + m % 2, hd * P:(hd + 1) * P],
                                                probs[:, i % 2, hd, k * P:(k + 1) * P], ident)
                        last.then_inc(S["turn_done"], 1)
                    if what == "values":
                        m = turns_before(i) + k
                        if m == 0:
                            pe.wait_ge(S["v_low"], 2 * (gg + 1))
                        pe.wait_ge(S["probsT_low"], TURNS * gg + m + 1)
                        if k == 0:
                            if i >= 2:
                                pe.wait_ge(S["out_added"], REP * (NT * gg + i - 1))
                        last = products(ps[:, 6 + i % 2, :], parts(values, k, every), [probsT[:, m % 3, 0], probsT[:, m % 3, 1]],
                                        k == 0, k == i)
                        if k == i:
                            last.then_inc(S["pv_done"], 1)
                    if what == "out":
                        if k == 0:
                            if i == 0:
                                pe.wait_ge(S["wo_split"], 2 * (gg + 1))
                            pe.wait_ge(S["attnT_low"], NT * gg + i + 1)
                        else:
                            pe.wait_ge(S["out_added"], REP * (NT * gg + i) + 2)
                        for hd in (2 * k, 2 * k + 1):
                            last = products(ps[:, 6 + i % 2, (hd % 2) * D:(hd % 2 + 1) * D],
                                            [attnT[:, i % 2, part, hd * P:(hd + 1) * P] for part in range(2)],
                                            parts(w_o, hd, every), True, True)
                        last.then_inc(S["out_ps"], 1)

            def turn_xs(f, tau, par, k):
                pe.wait_ge(xs_in[par], 16 * (PAR[par] * f + k + 1))
                for c in range(DC):
                    last = pe.transpose(ps[:, 4 + par, c * P:(c + 1) * P], xs[:, par, c * P:(c + 1) * P], ident)
                last.then_inc(S["xs_turned"], 1)

            def up(f, tau, par):
                pe.wait_ge(S["xsT_ready"], NS * f + tau + 1)
                for k in range(2):
                    pe.wait_ge(S["w13_low"], 2 * (NS * f + tau) + k + 1)
                    for c in range(DC):
                        block = slice((k * DC + c) * F, (k * DC + c + 1) * F)
                        last = products(ps[:, 2 * par + k, :], [xsT[:, par, part, c, :] for part in range(2)],
                                        [parts13[:, par, part, block] for part in range(2)], c == 0, c == DC - 1)
                last.then_inc(S["up_done"], 1)

            def turn_hid(f, tau, par):
                pe.wait_ge(S["hid_ready"], NS * f + tau + 1)
                for c in range(FC):
                    last = pe.transpose(ps[:, 6, c * P:(c + 1) * P], hid[:, par, c * P:(c + 1) * P], ident)
                last.then_inc(S["hid_turned"], 1)

            def down(f, tau, par):
                pe.wait_ge(S["hidT_ready"], NS * f + tau + 1)
                pe.wait_ge(S["w2_low"], NS * f + tau + 1)
                if not (isinstance(tau, int) and NS * f + tau == 0):
                    pe.wait_ge(S["ys_ready"], NS * f + tau)
                for c in range(FC):
                    last = products(ps[:, 7, 0:D], [hidT[:, par, part, c * P:(c + 1) * P] for part in range(2)],
                                    [parts2[:, par, part, c * D:(c + 1) * D] for part in range(2)], c == 0, c == FC - 1)
                last.then_inc(S["down_done"], 1)

            def moe(f):
                def gate_logits(t):
                    pe.wait_ge(S["xT_ready"], NT * n_turn[0] + t + 1)
                    for c in range(DC):
                        last = pe.matmul(ps[:, 0, t * E:(t + 1) * E], tokens(c, t), gate[:, c, :],
                                         start=(c == 0), stop=(c == DC - 1))
                    if t == NT - 1:
                        last.then_inc(S["logits_ps"], 1)

                for t in range(NT):
                    turn_token(t, rows_out[:, 0])
                    if t:
                        gate_logits(t - 1)
                gate_logits(NT - 1)
                n_turn[0] += 1
                pe.wait_ge(S["pick_ready"], f + 1)
                pe.matmul(ps[:, 1, 0:NT * E], square16[:, 2, :], both[:].rearrange("p t e -> p (t e)"), start=True, stop=False)
                for s in range(1, NT):
                    pe.matmul(ps[:, 1, s * E:NT * E], ones16[:], both[:, 0:NT - s, :].rearrange("p t e -> p (t e)"),
                              start=False, stop=(s == NT - 1))
                for t in range(NT):
                    last = pe.matmul(ps[:, 1, 128:128 + E], ones16[:], both[:, t, :], start=(t == 0), stop=(t == NT - 1))
                last.then_inc(S["routing_ps"], 1)
                pe.wait_ge(S["owner_ready"], f + 1)
                pe.wait_ge(S["experts_in"], 16 * 3 * (RES + (E - RES) * (f + 1)))
                turn_xs(f, 0, 0, 0)
                up(f, 0, 0)
                turn_xs(f, 1, 1, 0)

                def step(tau, par, k, more=True):
                    turn_hid(f, tau - 1, 1 - par)
                    up(f, tau, par)
                    if more:
                        turn_xs(f, tau + 1, 1 - par, k)
                    down(f, tau - 1, 1 - par)

                with pe.Fori(0, (NS - 3) // 2) as k:
                    step(2 * k + 1, 1, k + 1)
                    step(2 * k + 2, 0, k + 1)
                k = (NS - 3) // 2
                step(NS - 2, 1, k + 1)
                step(NS - 1, 0, k + 1, more=False)
                turn_hid(f, NS - 1, 0)
                down(f, NS - 1, 0)

            def rwkv():
                turn_tokens()
                pe.wait_ge(S["rwkv_in"], 16 * 6)
                for n in range(4):
                    th, hc = divmod(n, 2)
                    if hc == 0:
                        pe.wait_ge(S["xT_ready"], NT * n_turn[0] - 4 * (1 - th))
                    for c in range(DC):
                        last = pe.matmul(ps[:, n, :], Wv[:, c, hc * P:(hc + 1) * P], xT[:, c, 1 + th * HALF:1 + (th + 1) * HALF],
                                         start=(c == 0), stop=(c == DC - 1))
                    last.then_inc(S["v_done"], 1)
                pe.wait_ge(S["mix_ready"], 2)
                for n in range(NT // 2):
                    if n >= 2:
                        pe.wait_ge(S["r_ready"], n - 1)
                    for k in range(2):
                        t = 2 * n + k
                        for c in range(DC):
                            last = pe.matmul(ps[:, 4 + n % 2, k * D:(k + 1) * D], mixT[:, c, t * P:(t + 1) * P], Wr[:, c, :],
                                             start=(c == 0), stop=(c == DC - 1))
                    last.then_inc(S["r_done"], 1)
                    if n == 1:
                        pe.wait_ge(S["vw_ready"], 2)
                        for c in range(DC):
                            last = pe.matmul(ps[:, 0, 0:D], vwide[:, c, :], Wo[:, c, :], start=(c == 0), stop=(c == DC - 1))
                        last.then_inc(S["u_done"], 1)
                turn_tokens()

                def receptance(n):
                    for c in range(DC):
                        products(ps[:, 4 + n % 4, D:2 * D], parts(xT_parts, c, slice(1 + n * P, 1 + (n + 1) * P)),
                                 parts(cr_parts, c), c == 0, c == DC - 1)

                pe.wait_ge(S["ck_split_low"], 3)
                for th in range(2):
                    pe.wait_ge(S["xT_low"], 1 + 4 * (th + 1))
                    for ic in range(IC):
                        n = th * IC + ic
                        if n >= 4:
                            pe.wait_ge(S["ck_relu"], n - 3)
                        for c in range(DC):
                            last = products(ps[:, n % 4, :], parts(ck_parts, c, slice(ic * P, (ic + 1) * P)),
                                            parts(xT_parts, c, slice(th * HALF, (th + 1) * HALF)), c == 0, c == DC - 1)
                        last.then_inc(S["ck_done"], 1)
                    for t in range(4):
                        if th:
                            pe.wait_ge(S["cv_used"], t + 1)
                        receptance(th * 4 + t)
                    pe.wait_ge(S["kT_ready"], IC * (th + 1))
                    for t in range(4):
                        n = th * 4 + t
                        for ic in range(IC):
                            place = slice(t * P, (t + 1) * P)
                            last = products(ps[:, 4 + n % 4, 0:D], [kT_high[:, ic, place], (kT_low0, kT_low1)[ic // 4][:, ic % 4, place]],
                                            parts(cv_parts, ic), ic == 0, ic == IC - 1)
                        last.then_inc(S["cv_done"], 1)

            attention(0)
            moe(0)
            rwkv()
            attention(1)
            moe(1)


_INS = ["L0_attn_x", "L0_attn_ln1_g", "L0_attn_ln1_b", "L0_attn_ln2_g", "L0_attn_ln2_b", "L0_attn_tm_g",
        "L0_attn_tm_b", "L0_attn_time_decay", "L0_attn_time_first", "L0_attn_Wv", "L0_attn_Wr", "L0_attn_Wo",
        "L0_attn_bo", "L0_attn_cm_g", "L0_attn_cm_b", "L0_attn_Wck", "L0_attn_Wcv", "L0_attn_Wcr",
        "L0_ffn_norm1_w", "L0_ffn_norm2_w", "L0_ffn_wq", "L0_ffn_wk", "L0_ffn_wv", "L0_ffn_wo",
        "L0_ffn_gate_w", "L0_ffn_w1", "L0_ffn_w3", "L0_ffn_w2"]


def kernel(**inputs):
    import concourse.bacc as _bacc
    from concourse.bass_utils import run_bass_kernel_spmd as _run

    nc = _bacc.Bacc("TRN2", target_bir_lowering=False, num_devices=1)
    arrays, args = {}, {}
    given = {name: inputs[name] for name in _INS}
    given.update(constants())
    for name, value in given.items():
        v = np.ascontiguousarray(value)
        arrays[f"in_{name}_dram"] = v
        args[name] = nc.dram_tensor(f"in_{name}_dram", v.shape, mybir.dt.from_np(v.dtype), kind="ExternalInput").ap()
    out = nc.dram_tensor("out_dram", (1, T, D), F32, kind="ExternalOutput").ap()
    scratch = (nc.dram_tensor("xs_dram", (NS * P, ROW), F32, kind="Internal").ap(),
               nc.dram_tensor("sum_dram", (T + P, D), F32, kind="Internal").ap(),
               nc.dram_tensor("xsave_dram", (T, D), F32, kind="Internal").ap())
    macaron(nc, args, out, scratch)
    r = _run(nc, [arrays], core_ids=[0])
    return r.results[0]["out_dram"]
```
